# Optimizing a Trainium2 kernel written in Bass

```python
import numpy as np
import jax
import jax.numpy as jnp

def _softmax(x, axis=-1):
    return jax.nn.softmax(x, axis=axis)

def _gelu(x):
    return jax.nn.gelu(x, approximate=True)

def _silu(x):
    return jax.nn.silu(x)

def _sigmoid(x):
    return jax.nn.sigmoid(x)

def _layernorm(x, axis=-1, eps=1e-05):
    m = jnp.mean(x, axis=axis, keepdims=True)
    v = jnp.var(x, axis=axis, keepdims=True)
    return (x - m) / jnp.sqrt(v + eps)

def _scatter_add(tgt, idx, src, axis=0):
    return tgt.at[idx].add(src)

def _segment_sum(src, seg, n):
    return jax.ops.segment_sum(src, seg, n)
kernel_name = 'mk_adj_ffn_d2_adj_r2_599d93'

def setup_inputs(seed: int=0):
    np.random.seed(seed)
    _w = jnp.asarray

    def _rec_inputs():
        import jax
        import jax.numpy as jnp
        _gk = jax.random.key(seed)
        x = -0.000929 + 1 * jax.random.normal(jax.random.fold_in(_gk, 1), (64, 128, 128), jnp.float32)
        _a = jax.random.bernoulli(jax.random.fold_in(_gk, 2), 0.125, (128, 128))
        _a = jnp.logical_or(_a, jnp.eye(128, dtype=bool))
        adj = _a.astype(jnp.int32)
        return (x, adj)
    x, adj = _rec_inputs()

    def _L0_gnn_setup():
        import jax, jax.numpy as jnp
        import numpy as np
        ALPHA = 0.2
        EPS = 1e-06
        key = jax.random.key(seed)
        ks = jax.random.split(key, 8)
        B, N, D, H = (2, 1024, 128, 8)
        dh = D // H
        x = jax.random.normal(ks[0], (B, N, D), dtype=jnp.float32)
        adj = jax.random.randint(ks[1], (N, N), 0, 2, dtype=jnp.int32)
        adj = jnp.maximum(adj, jnp.eye(N, dtype=jnp.int32))
        p = jax.random.uniform(ks[2], (B, N, N), dtype=jnp.float32)
        prior = p / jnp.sum(p, axis=-1, keepdims=True)
        W = jax.random.normal(ks[3], (H, D, dh), dtype=jnp.float32) * (1.0 / np.sqrt(D))
        a_src = jax.random.normal(ks[4], (H, dh), dtype=jnp.float32) * (1.0 / np.sqrt(dh))
        a_dst = jax.random.normal(ks[5], (H, dh), dtype=jnp.float32) * (1.0 / np.sqrt(dh))
        beta_tilde = jnp.ones((), dtype=jnp.float32)
        W_out = jax.random.normal(ks[6], (D, D), dtype=jnp.float32) * (1.0 / np.sqrt(D))
        return {'x': x, 'adj': adj, 'prior': prior, 'W': W, 'a_src': a_src, 'a_dst': a_dst, 'beta_tilde': beta_tilde, 'W_out': W_out}
    _L0_gnn_all = _L0_gnn_setup()
    _L0_gnn_in = {k: v for k, v in _L0_gnn_all.items() if k in ('W', 'a_src', 'a_dst', 'beta_tilde', 'W_out')}
    del _L0_gnn_all

    def _L0_ffn_setup():
        import jax, jax.numpy as jnp
        import numpy as np
        H, P, G, NS, K = (8, 64, 64, 64, 3)
        D_INNER = H * P
        CONV_DIM = D_INNER + 2 * NS
        D_IN_PROJ = 2 * D_INNER + 2 * NS + 2 * H

        def _hydra(u, in_w, conv_w, conv_b, dt_bias, A_log, Dp, fcD_w, norm_w, out_w):
            Bt, L, _ = u.shape
            zxbcdt = u @ in_w.T
            z = zxbcdt[..., :D_INNER]
            xBC = zxbcdt[..., D_INNER:D_INNER + CONV_DIM]
            dt = zxbcdt[..., -2 * H:]
            dt = jnp.concatenate([dt[..., :H], jnp.flip(dt[..., H:], axis=1)], axis=0)
            dt = jax.nn.softplus(dt + dt_bias)
            xp = jnp.pad(xBC, ((0, 0), (K - 1, 0), (0, 0)))
            xBC = sum((xp[:, k:k + L, :] * conv_w[:, k] for k in range(K))) + conv_b
            xBC = jax.nn.silu(xBC)
            x = xBC[..., :D_INNER]
            Bm = xBC[..., D_INNER:D_INNER + NS]
            Cm = xBC[..., D_INNER + NS:]
            x_og = x
            x2 = jnp.concatenate([x, jnp.flip(x, 1)], 0).reshape(2 * Bt, L, H, P)
            B2 = jnp.concatenate([Bm, jnp.flip(Bm, 1)], 0)
            C2 = jnp.concatenate([Cm, jnp.flip(Cm, 1)], 0)
            dA = jnp.exp(dt * -jnp.exp(A_log))
            dBx = jnp.einsum('blh,bln,blhp->blhpn', dt, B2, x2)

            def step(h, inp):
                dA_t, dBx_t, C_t = inp
                h = h * dA_t[:, :, None, None] + dBx_t
                return (h, jnp.einsum('bhpn,bn->bhp', h, C_t))
            h0 = jnp.zeros((2 * Bt, H, P, NS), u.dtype)
            _, ys = jax.lax.scan(step, h0, (dA.transpose(1, 0, 2), dBx.transpose(1, 0, 2, 3, 4), C2.transpose(1, 0, 2)))
            y = ys.transpose(1, 0, 2, 3).reshape(2 * Bt, L, D_INNER)
            y_fw, y_bw = (y[:Bt], jnp.flip(y[Bt:], 1))
            y = jnp.pad(y_fw[:, :-1], ((0, 0), (1, 0), (0, 0))) + jnp.pad(y_bw[:, 1:], ((0, 0), (0, 1), (0, 0)))
            y = y + x_og * jnp.repeat(x_og @ fcD_w.T + Dp, P, axis=-1)
            yg = y * jax.nn.silu(z)
            yg = yg * jax.lax.rsqrt(jnp.mean(jnp.square(yg), -1, keepdims=True) + 1e-05) * norm_w
            return yg @ out_w.T
        key = jax.random.key(seed)
        ks = jax.random.split(key, 10)
        dim, Bsz, N = (128, 4, 4096)
        s = 0.02
        return {'x': jax.random.normal(ks[0], (Bsz, N, dim), jnp.float32), 'W_fx': jax.random.normal(ks[1], (D_INNER, dim), jnp.float32) * s, 'b_fx': jnp.zeros((D_INNER,), jnp.float32), 'W_x': jax.random.normal(ks[2], (D_INNER, dim), jnp.float32) * s, 'b_x': jnp.zeros((D_INNER,), jnp.float32), 'W_slice': jax.random.normal(ks[3], (G, P), jnp.float32) * s, 'b_slice': jnp.zeros((G,), jnp.float32), 'temperature': jnp.full((1, H, 1, 1), 0.5, jnp.float32), 'hy_in_w': jax.random.normal(ks[4], (D_IN_PROJ, D_INNER), jnp.float32) * s, 'hy_conv_w': jax.random.normal(ks[5], (CONV_DIM, K), jnp.float32) * s, 'hy_conv_b': jnp.zeros((CONV_DIM,), jnp.float32), 'hy_dt_bias': jnp.log(jnp.expm1(jnp.full((H,), 0.01, jnp.float32))), 'hy_A_log': jnp.log(jnp.linspace(1.0, 16.0, H)).astype(jnp.float32), 'hy_D': jnp.ones((H,), jnp.float32), 'hy_fcD_w': jax.random.normal(ks[6], (H, D_INNER), jnp.float32) * s, 'hy_norm_w': jnp.ones((D_INNER,), jnp.float32), 'hy_out_w': jax.random.normal(ks[7], (D_INNER, D_INNER), jnp.float32) * s, 'out_w': jax.random.normal(ks[8], (dim, D_INNER), jnp.float32) * s, 'out_b': jnp.zeros((dim,), jnp.float32)}
    _L0_ffn_all = _L0_ffn_setup()
    _L0_ffn_in = {k: v for k, v in _L0_ffn_all.items() if k in ('W_fx', 'b_fx', 'W_x', 'b_x', 'W_slice', 'b_slice', 'temperature', 'hy_in_w', 'hy_conv_w', 'hy_conv_b', 'hy_dt_bias', 'hy_A_log', 'hy_D', 'hy_fcD_w', 'hy_norm_w', 'hy_out_w', 'out_w', 'out_b')}
    del _L0_ffn_all

    def _L1_gnn_setup():
        import jax, jax.numpy as jnp
        import numpy as np
        NEG_BIG = -9000000000000000.0
        key = jax.random.key(seed)
        k1, k2, k3, k4 = jax.random.split(key, 4)
        bs, N, Fin, Fout = (8, 1024, 128, 128)
        x = jax.random.normal(k1, (bs, N, Fin), dtype=jnp.float32)
        adj = jax.random.randint(k2, (N, N), 0, 2, dtype=jnp.int32)
        W = jax.random.normal(k3, (Fin, Fout), dtype=jnp.float32) * (1.414 / np.sqrt(Fin))
        a = jax.random.normal(k4, (2 * Fout, 1), dtype=jnp.float32) * 0.1
        return {'x': x, 'adj': adj, 'W': W, 'a': a}
    _L1_gnn_all = _L1_gnn_setup()
    _L1_gnn_in = {k: v for k, v in _L1_gnn_all.items() if k in ('W', 'a')}
    del _L1_gnn_all

    def _L1_ffn_setup():
        import jax, jax.numpy as jnp
        import numpy as np
        N_EXPERTS = 8
        TOP_K = 2
        key = jax.random.key(seed)
        ks = jax.random.split(key, 5)
        B, T, C, E, H = (8, 1024, 128, 8, 341)
        scale = 1.0 / np.sqrt(C)
        return {'x': jax.random.normal(ks[0], (B, T, C), dtype=jnp.float32), 'router_w': jax.random.normal(ks[1], (E, C), dtype=jnp.float32) * scale, 'w1': jax.random.normal(ks[2], (E, H, C), dtype=jnp.float32) * scale, 'w2': jax.random.normal(ks[3], (E, C, H), dtype=jnp.float32) * (1.0 / np.sqrt(H)), 'w3': jax.random.normal(ks[4], (E, H, C), dtype=jnp.float32) * scale}
    _L1_ffn_all = _L1_ffn_setup()
    _L1_ffn_in = {k: v for k, v in _L1_ffn_all.items() if k in ('router_w', 'w1', 'w2', 'w3')}
    del _L1_ffn_all
    return {'x': x, 'adj': adj, 'L0_gnn_W': _L0_gnn_in['W'], 'L0_gnn_a_src': _L0_gnn_in['a_src'], 'L0_gnn_a_dst': _L0_gnn_in['a_dst'], 'L0_gnn_beta_tilde': _L0_gnn_in['beta_tilde'], 'L0_gnn_W_out': _L0_gnn_in['W_out'], 'L0_ffn_W_fx': _L0_ffn_in['W_fx'], 'L0_ffn_b_fx': _L0_ffn_in['b_fx'], 'L0_ffn_W_x': _L0_ffn_in['W_x'], 'L0_ffn_b_x': _L0_ffn_in['b_x'], 'L0_ffn_W_slice': _L0_ffn_in['W_slice'], 'L0_ffn_b_slice': _L0_ffn_in['b_slice'], 'L0_ffn_temperature': _L0_ffn_in['temperature'], 'L0_ffn_hy_in_w': _L0_ffn_in['hy_in_w'], 'L0_ffn_hy_conv_w': _L0_ffn_in['hy_conv_w'], 'L0_ffn_hy_conv_b': _L0_ffn_in['hy_conv_b'], 'L0_ffn_hy_dt_bias': _L0_ffn_in['hy_dt_bias'], 'L0_ffn_hy_A_log': _L0_ffn_in['hy_A_log'], 'L0_ffn_hy_D': _L0_ffn_in['hy_D'], 'L0_ffn_hy_fcD_w': _L0_ffn_in['hy_fcD_w'], 'L0_ffn_hy_norm_w': _L0_ffn_in['hy_norm_w'], 'L0_ffn_hy_out_w': _L0_ffn_in['hy_out_w'], 'L0_ffn_out_w': _L0_ffn_in['out_w'], 'L0_ffn_out_b': _L0_ffn_in['out_b'], 'L1_gnn_W': _L1_gnn_in['W'], 'L1_gnn_a': _L1_gnn_in['a'], 'L1_ffn_router_w': _L1_ffn_in['router_w'], 'L1_ffn_w1': _L1_ffn_in['w1'], 'L1_ffn_w2': _L1_ffn_in['w2'], 'L1_ffn_w3': _L1_ffn_in['w3']}

def reference(x, adj, L0_gnn_W, L0_gnn_a_src, L0_gnn_a_dst, L0_gnn_beta_tilde, L0_gnn_W_out, L0_ffn_W_fx, L0_ffn_b_fx, L0_ffn_W_x, L0_ffn_b_x, L0_ffn_W_slice, L0_ffn_b_slice, L0_ffn_temperature, L0_ffn_hy_in_w, L0_ffn_hy_conv_w, L0_ffn_hy_conv_b, L0_ffn_hy_dt_bias, L0_ffn_hy_A_log, L0_ffn_hy_D, L0_ffn_hy_fcD_w, L0_ffn_hy_norm_w, L0_ffn_hy_out_w, L0_ffn_out_w, L0_ffn_out_b, L1_gnn_W, L1_gnn_a, L1_ffn_router_w, L1_ffn_w1, L1_ffn_w2, L1_ffn_w3):
    import jax
    import jax.numpy as jnp

    def _L0_gnn_ref(x, adj, prior, W, a_src, a_dst, beta_tilde, W_out):
        import jax, jax.numpy as jnp
        import numpy as np
        ALPHA = 0.2
        EPS = 1e-06
        B, N, D = x.shape
        x_proj = jnp.einsum('bnd,hdf->bhnf', x, W)
        e_src = jnp.einsum('bhnf,hf->bhn', x_proj, a_src)
        e_dst = jnp.einsum('bhnf,hf->bhn', x_proj, a_dst)
        e = jax.nn.leaky_relu(e_src[..., :, None] + e_dst[..., None, :], ALPHA)
        beta = jax.nn.softplus(beta_tilde)
        e = e + (beta * jnp.log(prior + EPS))[:, None, :, :]
        neg_inf = jnp.finfo(e.dtype).min
        e = jnp.where(adj[None, None, :, :] > 0, e, neg_inf)
        attn = jax.nn.softmax(e, axis=-1)
        h = jnp.einsum('bhij,bhjf->bhif', attn, x_proj)
        h = h.transpose(0, 2, 1, 3).reshape(B, N, D)
        return h @ W_out.T

    def _L0_ffn_ref(x, W_fx, b_fx, W_x, b_x, W_slice, b_slice, temperature, hy_in_w, hy_conv_w, hy_conv_b, hy_dt_bias, hy_A_log, hy_D, hy_fcD_w, hy_norm_w, hy_out_w, out_w, out_b):
        import jax, jax.numpy as jnp
        import numpy as np
        H, P, G, NS, K = (8, 64, 64, 64, 3)
        D_INNER = H * P
        CONV_DIM = D_INNER + 2 * NS
        D_IN_PROJ = 2 * D_INNER + 2 * NS + 2 * H

        def _hydra(u, in_w, conv_w, conv_b, dt_bias, A_log, Dp, fcD_w, norm_w, out_w):
            Bt, L, _ = u.shape
            zxbcdt = u @ in_w.T
            z = zxbcdt[..., :D_INNER]
            xBC = zxbcdt[..., D_INNER:D_INNER + CONV_DIM]
            dt = zxbcdt[..., -2 * H:]
            dt = jnp.concatenate([dt[..., :H], jnp.flip(dt[..., H:], axis=1)], axis=0)
            dt = jax.nn.softplus(dt + dt_bias)
            xp = jnp.pad(xBC, ((0, 0), (K - 1, 0), (0, 0)))
            xBC = sum((xp[:, k:k + L, :] * conv_w[:, k] for k in range(K))) + conv_b
            xBC = jax.nn.silu(xBC)
            x = xBC[..., :D_INNER]
            Bm = xBC[..., D_INNER:D_INNER + NS]
            Cm = xBC[..., D_INNER + NS:]
            x_og = x
            x2 = jnp.concatenate([x, jnp.flip(x, 1)], 0).reshape(2 * Bt, L, H, P)
            B2 = jnp.concatenate([Bm, jnp.flip(Bm, 1)], 0)
            C2 = jnp.concatenate([Cm, jnp.flip(Cm, 1)], 0)
            dA = jnp.exp(dt * -jnp.exp(A_log))
            dBx = jnp.einsum('blh,bln,blhp->blhpn', dt, B2, x2)

            def step(h, inp):
                dA_t, dBx_t, C_t = inp
                h = h * dA_t[:, :, None, None] + dBx_t
                return (h, jnp.einsum('bhpn,bn->bhp', h, C_t))
            h0 = jnp.zeros((2 * Bt, H, P, NS), u.dtype)
            _, ys = jax.lax.scan(step, h0, (dA.transpose(1, 0, 2), dBx.transpose(1, 0, 2, 3, 4), C2.transpose(1, 0, 2)))
            y = ys.transpose(1, 0, 2, 3).reshape(2 * Bt, L, D_INNER)
            y_fw, y_bw = (y[:Bt], jnp.flip(y[Bt:], 1))
            y = jnp.pad(y_fw[:, :-1], ((0, 0), (1, 0), (0, 0))) + jnp.pad(y_bw[:, 1:], ((0, 0), (0, 1), (0, 0)))
            y = y + x_og * jnp.repeat(x_og @ fcD_w.T + Dp, P, axis=-1)
            yg = y * jax.nn.silu(z)
            yg = yg * jax.lax.rsqrt(jnp.mean(jnp.square(yg), -1, keepdims=True) + 1e-05) * norm_w
            return yg @ out_w.T
        B, N, _ = x.shape
        fx = (x @ W_fx.T + b_fx).reshape(B, N, H, P).transpose(0, 2, 1, 3)
        xm = (x @ W_x.T + b_x).reshape(B, N, H, P).transpose(0, 2, 1, 3)
        temp = jnp.maximum(temperature, 1e-06)
        sw = jax.nn.softmax((xm @ W_slice.T + b_slice) / temp, axis=-1)
        snorm = sw.sum(2)
        st = jnp.einsum('bhnc,bhng->bhgc', fx, sw) / (snorm + 1e-05)[..., None]
        st = st.transpose(0, 2, 1, 3).reshape(B, G, D_INNER)
        ot = _hydra(st, hy_in_w, hy_conv_w, hy_conv_b, hy_dt_bias, hy_A_log, hy_D, hy_fcD_w, hy_norm_w, hy_out_w)
        ot = ot.reshape(B, G, H, P).transpose(0, 2, 1, 3)
        out = jnp.einsum('bhgc,bhng->bhnc', ot, sw).transpose(0, 2, 1, 3).reshape(B, N, D_INNER)
        return out @ out_w.T + out_b

    def _L1_gnn_ref(x, adj, W, a):
        import jax, jax.numpy as jnp
        import numpy as np
        NEG_BIG = -9000000000000000.0
        alpha = 0.2
        h = jnp.matmul(x, W)
        Fout = h.shape[-1]
        a1, a2 = (a[:Fout, 0], a[Fout:, 0])
        s1 = jnp.einsum('bnf,f->bn', h, a1)
        s2 = jnp.einsum('bnf,f->bn', h, a2)
        e = jax.nn.leaky_relu(s1[:, :, None] + s2[:, None, :], negative_slope=alpha)
        attention = jnp.where(adj[None, :, :] > 0, e, NEG_BIG)
        attention = jax.nn.softmax(attention, axis=-1)
        h_prime = jnp.matmul(attention, h)
        return jax.nn.elu(h_prime)

    def _L1_ffn_ref(x, router_w, w1, w2, w3):
        import jax, jax.numpy as jnp
        import numpy as np
        N_EXPERTS = 8
        TOP_K = 2
        B, T, C = x.shape
        flat = x.reshape(-1, C)
        logits = flat @ router_w.T
        probs = jax.nn.softmax(logits, axis=-1)
        topk_probs, topk_idx = jax.lax.top_k(probs, TOP_K)
        topk_probs = topk_probs / (jnp.sum(topk_probs, axis=-1, keepdims=True) + 1e-09)
        onehot = jax.nn.one_hot(topk_idx, N_EXPERTS, dtype=flat.dtype)
        gates = jnp.einsum('nk,nke->ne', topk_probs, onehot)
        h1 = jnp.einsum('nc,ehc->neh', flat, w1)
        h3 = jnp.einsum('nc,ehc->neh', flat, w3)
        h = jax.nn.silu(h1) * h3
        y = jnp.einsum('neh,ech->nec', h, w2)
        out = jnp.einsum('ne,nec->nc', gates, y)
        return out.reshape(B, T, C)
    x = x + _L0_gnn_ref(_layernorm(x, axis=-1), adj, adj[None], L0_gnn_W, L0_gnn_a_src, L0_gnn_a_dst, L0_gnn_beta_tilde, L0_gnn_W_out)
    x = x + _L0_ffn_ref(_layernorm(x, axis=-1), L0_ffn_W_fx, L0_ffn_b_fx, L0_ffn_W_x, L0_ffn_b_x, L0_ffn_W_slice, L0_ffn_b_slice, L0_ffn_temperature, L0_ffn_hy_in_w, L0_ffn_hy_conv_w, L0_ffn_hy_conv_b, L0_ffn_hy_dt_bias, L0_ffn_hy_A_log, L0_ffn_hy_D, L0_ffn_hy_fcD_w, L0_ffn_hy_norm_w, L0_ffn_hy_out_w, L0_ffn_out_w, L0_ffn_out_b)
    x = x + _L1_gnn_ref(_layernorm(x, axis=-1), adj, L1_gnn_W, L1_gnn_a)
    x = x + _L1_ffn_ref(_layernorm(x, axis=-1), L1_ffn_router_w, L1_ffn_w1, L1_ffn_w2, L1_ffn_w3)
    return x

_drawn_inputs = setup_inputs


def setup_inputs(seed=0):
    import zlib

    import numpy as np

    out = dict(_drawn_inputs(seed))
    spreads = {'L0_ffn_b_fx': (0.0, 0.1),
     'L0_ffn_b_x': (0.0, 0.8),
     'L0_ffn_b_slice': (0.0, 0.8),
     'L0_ffn_temperature': (0.5, 0.6),
     'L0_ffn_hy_conv_b': (0.0, 0.1),
     'L0_ffn_hy_dt_bias': (-4.600166320800781, 0.6),
     'L0_ffn_hy_D': (1.0, 0.2),
     'L0_ffn_hy_norm_w': (1.0, 0.2),
     'L0_ffn_out_b': (0.0, 0.1)}
    factors = {'L0_ffn_W_x': 8.0,
     'L0_ffn_W_slice': 8.0,
     'L0_ffn_hy_conv_w': 8.0,
     'L0_ffn_hy_A_log': 8.0,
     'L0_ffn_hy_fcD_w': 6.973}
    for name, (base, spread) in spreads.items():
        noise = np.random.default_rng([zlib.crc32(name.encode()), seed]).standard_normal(out[name].shape)
        drawn = base * np.exp(spread * noise) if base else spread * noise
        out[name] = jnp.asarray(drawn.astype(out[name].dtype))
    for name, factor in factors.items():
        out[name] = (out[name] * factor).astype(out[name].dtype)
    return out
```

```python
from contextlib import ExitStack

import concourse.bass as bass
from concourse import mybir

F32 = mybir.dt.float32
BF16 = mybir.dt.bfloat16
I32 = mybir.dt.int32
ALU = mybir.AluOpType
ACT = mybir.ActivationFunctionType
AX = mybir.AxisListType
ds = bass.ds

P = 128
H0, DH = 8, 16
HF, PF = 8, 64
G = 64
NS = 64
DI = HF * PF
CD = DI + 2 * NS
KC = DI // P
E8, HID = 8, 341
HCH = [128, 128, 85]
GB = 8


def wait(eng, sem, n):
    if isinstance(n, int) and n <= 0:
        return
    eng.wait_ge(sem, n)


def pipelined(eng, total, unroll, stages):
    last = max(lag for lag, _ in stages)
    head = min(total, unroll * -(-(last + 2) // unroll))
    for t in range(head):
        for lag, emit in stages:
            if 0 <= t - lag:
                emit(t - lag, (t - lag) % unroll)
    if total > head:
        with eng.Fori(head // unroll, total // unroll) as q:
            for r in range(unroll):
                for lag, emit in stages:
                    emit(q * unroll + (r - lag), (r - lag) % unroll)
    for t in range(total, total + last):
        for lag, emit in stages:
            if t - lag < total:
                emit(t - lag, (t - lag) % unroll)


def build(nc, io, out, stop=99, start=0):
    B = io["x"].shape[0]
    io = {k: v.bitcast(BF16) if v.dtype == mybir.dt.uint16 else v for k, v in io.items()}
    NQ = B // 4
    with ExitStack() as root:
        held = []

        def sem(name):
            held.append(nc.alloc_semaphore(name=name))
            return held[-1]

        def end_layer():
            nc.clear_and_free_semaphores(held)
            nc.all_engine_barrier()
            held.clear()

        def tile(ctx, name, shape, dt=F32):
            return ctx.enter_context(nc.sbuf_tensor("t_" + name, shape, dt))

        X = tile(root, "X", [P, B * P])
        X3 = X[:, :].rearrange("p (b d) -> p b d", d=P)
        ST = tile(root, "ST", [P, B * 6])
        MU = tile(root, "MU", [P, B])
        RS = tile(root, "RS", [P, B])
        LT6 = tile(root, "LT6", [P, 3 * B])
        IDF = tile(root, "IDF", [P, P])
        IDB = tile(root, "IDB", [P, P], BF16)
        PS = root.enter_context(nc.psum_tensor("PS", [P, 8, 512], F32))

        def bank(k, n=512, parts=P, col=0):
            return PS[0:parts, k, col:col + n]

        def xs(b):
            return X[:, ds(b * P, P)]

        s_const = sem("s_const")
        s_x = [sem(f"s_x{c}") for c in range(B // 8)]
        C = dict(nc=nc, io=io, sem=sem, tile=tile, X=X, X3=X3, ST=ST, MU=MU, RS=RS, LT6=LT6, IDF=IDF, IDB=IDB,
                 PS=PS, bank=bank, xs=xs, B=B, NQ=NQ)

        load_x(C, s_const, s_x)
        end_layer()
        if stop > 0 and start < 1:
            gnn0(C)
            end_layer()
        if stop > 1 and start < 2:
            ffn0(C)
            end_layer()
        if stop > 2 and start < 3:
            gnn1(C)
            end_layer()
        if stop > 3:
            moe(C, out)
        else:
            store_x(C, out)


def load_x(C, s_const, s_x):
    nc, io, X, B, sem = C["nc"], C["io"], C["X"], C["B"], C["sem"]
    CH = 8
    with nc.Block() as block:
        @block.sync
        def _(sp):
            sp.dma_start(C["IDF"][:, :], io["c_id"]).then_inc(s_const, 16)
            sp.dma_start(C["IDB"][:, :], io["c_idb"]).then_inc(s_const, 16)
            for c in range(B // CH):
                sp.dma_start(X[:, c * CH * P:(c + 1) * CH * P],
                             io["x"][c * CH:(c + 1) * CH].rearrange("b p d -> p b d")).then_inc(s_x[c], 16)
            sp.wait_ge(s_const, 32)

        @block.vector
        def _(dve):
            for c in range(B // CH):
                dve.wait_ge(s_x[c], 16)
                with dve.Fori(c * CH, (c + 1) * CH) as b:
                    dve.bn_stats(C["ST"][:, ds(b * 6, 6)], C["xs"](b))


def store_x(C, out):
    nc, X, B = C["nc"], C["X"], C["B"]
    s_out = C["sem"]("s_out")
    with nc.Block() as block:
        @block.sync
        def _(sp):
            for h in range(4):
                w = B // 4
                sp.dma_start(out[h * w:(h + 1) * w].rearrange("b p d -> p b d"),
                             C["X3"][:, h * w:(h + 1) * w]).then_inc(s_out, 16)
            sp.wait_ge(s_out, 64)


def ln_vector(C, dve, s_var, s_std):
    st = C["ST"][:, :].rearrange("p (b s) -> p b s", s=6)
    B = C["B"]
    dif, var, std = (C["LT6"][:, k * B:(k + 1) * B] for k in range(3))
    MU, RS = C["MU"][:, :], C["RS"][:, :]
    dve.drain()
    dve.tensor_tensor(MU, st[:, :, 1], st[:, :, 4], ALU.add)
    dve.tensor_tensor(dif, st[:, :, 1], st[:, :, 4], ALU.subtract)
    dve.tensor_tensor(var, st[:, :, 2], st[:, :, 5], ALU.add)
    dve.drain()
    dve.tensor_scalar(MU, MU, 0.5, None, ALU.mult)
    dve.tensor_tensor(dif, dif, dif, ALU.mult)
    dve.tensor_scalar(var, var, 1.0 / P, 1e-5, ALU.mult, ALU.add)
    dve.drain()
    dve.scalar_tensor_tensor(var, dif, 0.25, var, ALU.mult, ALU.add).then_inc(s_var, 1)
    dve.wait_ge(s_std, 1)
    dve.reciprocal(RS, std)
    dve.drain()


def ln_scalar(C, act, s_var, s_std):
    B = C["B"]
    act.wait_ge(s_var, 1)
    act.activation(C["LT6"][:, 2 * B:3 * B], C["LT6"][:, B:2 * B], ACT.Sqrt).then_inc(s_std, 1)


def normalise(C, dve, dst, b):
    return dve.tensor_scalar(dst, C["xs"](b), C["MU"][:, ds(b, 1)], C["RS"][:, ds(b, 1)], ALU.subtract, ALU.mult)


def project(C, tag, ctx, wcols, load, VS):
    nc, B, sem, tile, PS = C["nc"], C["B"], C["sem"], C["tile"], C["PS"]
    W = tile(ctx, tag + "W", [P, wcols])
    xn = tile(ctx, tag + "xn", [P, 2, P])
    xnT = tile(ctx, tag + "xnT", [P, 2, P])
    s_w, s_wz, s_var, s_std = (sem(tag + n) for n in ("w", "wz", "var", "std"))
    s_xn, s_tr, s_xnT, s_pr, s_vs = (sem(tag + n) for n in ("xn", "tr", "xnT", "pr", "vs"))
    with nc.Block() as block:
        load(block, W, s_w, s_wz)

        @block.vector
        def _(dve):
            load.vector(dve)
            ln_vector(C, dve, s_var, s_std)

            def norm(b, r):
                wait(dve, s_tr, b - 1)
                normalise(C, dve, xn[:, r % 2, :], b).then_inc(s_xn, 1)
            pipelined(dve, B, 2, [(0, norm)])

        @block.scalar
        def _(act):
            ln_scalar(C, act, s_var, s_std)

            def evac_t(b, r):
                wait(act, s_tr, b + 1)
                wait(act, s_pr, b - 1)
                act.copy(xnT[:, r % 2, :], PS[:, r % 2, 0:P]).then_inc(s_xnT, 1)

            def evac_p(b, r):
                wait(act, s_pr, b + 1)
                act.copy(VS[:, ds(b * wcols, wcols)], PS[:, 2 + r % 2, 0:wcols]).then_inc(s_vs, 1)
            pipelined(act, B, 2, [(0, evac_t), (1, evac_p)])

        @block.tensor
        def _(pe):
            def trans(b, r):
                wait(pe, s_xn, b + 1)
                wait(pe, s_xnT, b - 1)
                pe.transpose(PS[:, r % 2, 0:P], xn[:, r % 2, :], C["IDF"][:, :]).then_inc(s_tr, 1)

            def prod(b, r):
                wait(pe, s_xnT, b + 1)
                wait(pe, s_vs, b - 1)
                pe.matmul(PS[:, 2 + r % 2, 0:wcols], xnT[:, r % 2, :], W[:, :],
                          start=True, stop=True).then_inc(s_pr, 1)
            pe.wait_ge(s_w, load.count)
            wait(pe, s_wz, load.zcount)
            pipelined(pe, B, 2, [(0, trans), (1, prod)])


def factors(C, tag, ctx, S, Dd, NH, cf, bf, KT):
    nc, B, NQ, sem, tile, PS = C["nc"], C["B"], C["NQ"], C["sem"], C["tile"], C["PS"]
    n = B * NH
    nch = -(-n // P)
    w = min(n, P)
    dc = tile(ctx, tag + "dc", [P, n])
    dmax = tile(ctx, tag + "dmax", [P, nch])
    diag = tile(ctx, tag + "diag", [P, nch * w])
    z = tile(ctx, tag + "z", [P, n])
    Kf = tile(ctx, tag + "Kf", [P, n])
    Kp = tile(ctx, tag + "Kp", [P, NQ * 128], BF16)
    ones = tile(ctx, tag + "ones", [P, P])
    KpV = Kp[:, :].rearrange("p (q t r) -> p q t r", t=4, r=32)
    s_c, s_t, s_m, s_bc, s_e, s_k, s_kp, s_kt = (sem(tag + x) for x in
                                               ("fc", "ft", "fm", "fbc", "fe", "fk", "fkp", "fkt"))
    psb = PS[:, 4:8, :].rearrange("p k n -> p (k n)").bitcast(BF16)
    with nc.Block() as block:
        @block.vector
        def _(dve):
            dve.memset(ones[:, :], 1.0)
            dve.memset(Kp[:, :], 0.0)
            dve.tensor_copy(dc[:, :].rearrange("p (b h) -> p b h", h=NH), Dd).then_inc(s_c, 1)
            dve.wait_ge(s_t, 1)
            for c in range(nch):
                dve.tensor_reduce(dmax[0:w, c:c + 1], PS[0:w, 0, c * P:(c + 1) * P], AX.X, ALU.max)
            dve.drain()
            for c in range(nch):
                dve.tensor_scalar(diag[0:w, c * w:(c + 1) * w], C["IDF"][0:w, 0:w], dmax[0:w, c:c + 1], None, ALU.mult)
            dve.drain().then_inc(s_m, 1)
            dve.wait_ge(s_bc, 1)
            zv = z[:, :].rearrange("p (b h) -> p b h", h=NH)
            Dv = PS[:, 1, 0:n].rearrange("p (b h) -> p b h", h=NH)
            dve.tensor_tensor(dc[:, :], dc[:, :], PS[:, 1, 0:n], ALU.subtract)
            dve.tensor_tensor(zv, S, Dv, ALU.add)
            dve.drain()
            dve.tensor_scalar(z[:, :], z[:, :], -0.8, 0.0, ALU.mult, ALU.min)
            dve.drain().then_inc(s_e, 1)
            dve.wait_ge(s_k, 1)
            kk = Kf[:, :].rearrange("p (q r) -> p q r", q=NQ)
            wq = n // NQ
            dve.tensor_copy(KpV[:, :, 0, 0:wq], kk)
            dve.drain()
            dve.tensor_tensor(kk, kk, KpV[:, :, 0, 0:wq], ALU.subtract)
            dve.drain()
            dve.tensor_copy(KpV[:, :, 1, 0:wq], kk)
            dve.drain()
            dve.tensor_tensor(kk, kk, KpV[:, :, 1, 0:wq], ALU.subtract)
            dve.drain()
            dve.tensor_copy(KpV[:, :, 2, 0:wq], kk)
            dve.drain().then_inc(s_kp, 1)
            dve.wait_ge(s_kt, 1)
            dve.tensor_copy(KT[:, :], psb[:, 0:NQ * P])

        @block.scalar
        def _(act):
            act.wait_ge(s_e, 1)
            act.activation(cf, dc[:, :], ACT.Exp, scale=0.8)
            act.activation(bf, dc[:, :], ACT.Exp, scale=0.2)
            act.activation(Kf[:, :], z[:, :], ACT.Exp).then_inc(s_k, 1)

        @block.tensor
        def _(pe):
            pe.wait_ge(s_c, 1)
            for c in range(nch):
                last = pe.transpose(PS[0:w, 0, c * P:(c + 1) * P], dc[:, c * w:(c + 1) * w], C["IDF"][:, :])
            last.then_inc(s_t, 1)
            pe.wait_ge(s_m, 1)
            for c in range(nch):
                last = pe.matmul(PS[:, 1, c * w:(c + 1) * w], ones[0:w, :], diag[0:w, c * w:(c + 1) * w],
                                 start=True, stop=True)
            last.then_inc(s_bc, 1)
            pe.wait_ge(s_kp, 1)
            for q in range(NQ):
                last = pe.transpose(psb[:, q * P:(q + 1) * P], Kp[:, q * P:(q + 1) * P], C["IDB"][:, :])
            last.then_inc(s_kt, 1)


def gnn0(C):
    nc, io, B, NQ, sem, tile, PS = C["nc"], C["io"], C["B"], C["NQ"], C["sem"], C["tile"], C["PS"]
    IDF = C["IDF"]
    WC = P + 2 * H0
    with ExitStack() as ctx:
        VS = tile(ctx, "a_VS", [P, B * WC])
        V3 = VS[:, :].rearrange("p (b w) -> p b w", w=WC)
        cf = tile(ctx, "a_cf", [P, B * H0])
        bf = tile(ctx, "a_bf", [P, B * H0])
        KT = tile(ctx, "a_KT", [P, NQ * P], BF16)
        sel = tile(ctx, "a_sel", [P, 32 * P], BF16)
        MT = tile(ctx, "a_MT", [P, P])
        WoT = tile(ctx, "a_WoT", [P, P])
        adj = tile(ctx, "a_adj", [P, P], I32)
        mf = tile(ctx, "a_mf", [P, P])
        lb = tile(ctx, "a_lb", [P, P])
        msk = tile(ctx, "a_msk", [P, P])
        beta = tile(ctx, "a_beta", [P, 4])
        av = tile(ctx, "a_av", [P, 2 * P])
        tmp = tile(ctx, "a_tmp", [P, P])
        s_wd, s_w2, s_m1, s_m2, s_m3, s_mt, s_mc = (sem("a_" + x) for x in
                                                  ("wd", "w2", "m1", "m2", "m3", "mt", "mc"))

        class Load:
            count, zcount = 16, 1

            def __call__(self, block, W, s_w, s_wz):
                self.W, self.s_w, self.s_wz = W, s_w, s_wz

                @block.sync
                def _(sp):
                    sp.dma_start(W[:, 0:P], io["gW"]).then_inc(s_w, 16)
                    sp.dma_start(av[:, 0:P], io["g_as"].partition_broadcast(P)).then_inc(s_wd, 16)
                    sp.dma_start(av[:, P:2 * P], io["g_ad"].partition_broadcast(P)).then_inc(s_wd, 16)
                    sp.dma_start(adj[:, :], io["adj"]).then_inc(s_w2, 16)
                    sp.dma_start(beta[:, 0:1], io["beta"].partition_broadcast(P)).then_inc(s_w2, 16)
                    sp.dma_start(WoT[:, :], io["gWoT"]).then_inc(s_w2, 16)
                    sp.dma_start(sel[:, :], io["c_sel"]).then_inc(s_w2, 16)
                    sp.wait_ge(s_w2, 64)

            def vector(self, dve):
                dve.wait_ge(self.s_w, 16)
                dve.wait_ge(s_wd, 32)
                for k in range(2):
                    dve.tensor_tensor(tmp[:, :], self.W[:, 0:P], av[:, k * P:(k + 1) * P], ALU.mult)
                    dve.drain()
                    dve.tensor_reduce(self.W[:, P + k * H0:P + (k + 1) * H0],
                                      tmp[:, :].rearrange("p (h f) -> p h f", f=DH), AX.X, ALU.add)
                    dve.drain()
                dve.sem_inc(self.s_wz, 1)

        project(C, "a_", ctx, WC, Load(), VS)

        with nc.Block() as block:
            @block.vector
            def _(dve):
                dve.tensor_copy(mf[:, :], adj[:, :])
                dve.drain()
                dve.tensor_scalar(msk[:, :], mf[:, :], 0.0, None, ALU.is_gt)
                dve.tensor_scalar(mf[:, :], mf[:, :], 0.0, 1e-6, ALU.max, ALU.add)
                dve.scalar_tensor_tensor(beta[:, 1:2], beta[:, 0:1], -1.0, beta[:, 0:1], ALU.mult, ALU.max)
                dve.drain().then_inc(s_m1, 1)
                dve.wait_ge(s_m2, 1)
                dve.scalar_tensor_tensor(beta[:, 3:4], beta[:, 0:1], 0.0, beta[:, 2:3], ALU.max, ALU.add)
                dve.drain()
                dve.tensor_scalar(lb[:, :], lb[:, :], beta[:, 3:4], None, ALU.mult)
                dve.drain()
                dve.tensor_reduce(beta[:, 1:2], lb[:, :], AX.X, ALU.max, negate=True)
                dve.drain().then_inc(s_m1, 1)
                dve.wait_ge(s_m2, 2)
                dve.tensor_tensor(lb[:, :], lb[:, :], msk[:, :], ALU.mult).then_inc(s_m3, 1)
                dve.wait_ge(s_mt, 1)
                dve.tensor_copy(MT[:, :], PS[:, 0, 0:P])

            @block.scalar
            def _(act):
                act.wait_ge(s_m1, 1)
                act.activation(beta[:, 2:3], beta[:, 1:2], ACT.Exp, scale=-1.0)
                act.drain()
                act.activation(beta[:, 2:3], beta[:, 2:3], ACT.Ln, bias=1.0)
                act.activation(lb[:, :], mf[:, :], ACT.Ln).then_inc(s_m2, 1)
                act.wait_ge(s_m1, 2)
                act.activation(lb[:, :], lb[:, :], ACT.Exp, bias=beta[:, 1:2]).then_inc(s_m2, 1)

            @block.tensor
            def _(pe):
                pe.wait_ge(s_m3, 1)
                pe.transpose(PS[:, 0, 0:P], lb[:, :], IDF[:, :]).then_inc(s_mt, 1)

        with ExitStack() as c2:
            factors(C, "a_", c2, V3[:, :, P:P + H0], V3[:, :, P + H0:P + 2 * H0], H0, cf[:, :], bf[:, :], KT)

        with ExitStack() as c2:
            VX = tile(c2, "a_VX", [P, 2, H0 * (DH + 1)])
            PT = tile(c2, "a_PT", [P, 2, H0 * P])
            rec = tile(c2, "a_rec", [P, 2, H0])
            hn = tile(c2, "a_hn", [P, 2, P])
            hnT = tile(c2, "a_hnT", [P, 2, P])
            s_vx, s_K, s_pt, s_av, s_hn, s_ht, s_hc, s_y, s_res = (
                sem("a2_" + x) for x in ("vx", "K", "pt", "av", "hn", "ht", "hc", "y", "res"))
            W17 = DH + 1
            with nc.Block() as block:
                @block.gpsimd
                def _(pool):
                    def values(b, r):
                        wait(pool, s_av, b - 1)
                        vx = VX[:, r % 2, :].rearrange("p (h w) -> p h w", w=W17)
                        bb = bf[:, ds(b * H0, H0)]
                        pool.tensor_tensor(vx[:, :, 0:DH],
                                           VS[:, ds(b * WC, P)].rearrange("p (h f) -> p h f", f=DH),
                                           bb.unsqueeze(2).broadcast_to([P, H0, DH]), ALU.mult)
                        pool.tensor_copy(vx[:, :, DH], bb)
                        pool.drain().then_inc(s_vx, 1)
                    pipelined(pool, B, 2, [(0, values)])

                @block.tensor
                def _(pe):
                    def spread(b, r):
                        wait(pe, s_pt, b - 1)
                        col = (b - r) * (P // 4)
                        for h in range(H0):
                            o = PS[:, 2 * (r % 2) + h // 4, (h % 4) * P:(h % 4 + 1) * P]
                            k = (r * H0 + h) * P
                            last = pe.matmul(o, sel[0:96, k:k + P], KT[0:96, ds(col, P)], start=True, stop=True)
                        last.then_inc(s_K, 1)

                    def attend(b, r):
                        wait(pe, s_pt, b + 1)
                        wait(pe, s_vx, b + 1)
                        wait(pe, s_hn, b - 1)
                        for h in range(H0):
                            last = pe.matmul(PS[:, 4 + r % 2, h * W17:(h + 1) * W17],
                                             PT[:, r % 2, h * P:(h + 1) * P], VX[:, r % 2, h * W17:(h + 1) * W17],
                                             start=True, stop=True)
                        last.then_inc(s_av, 1)

                    def trans(b, r):
                        wait(pe, s_hn, b + 1)
                        wait(pe, s_hc, b)
                        pe.transpose(PS[:, 6, 0:P], hn[:, r % 2, :], IDF[:, :]).then_inc(s_ht, 1)

                    def mix(b, r):
                        wait(pe, s_hc, b + 1)
                        wait(pe, s_res, b)
                        pe.matmul(PS[:, 7, 0:P], hnT[:, r % 2, :], WoT[:, :], start=True, stop=True).then_inc(s_y, 1)
                    pipelined(pe, B, 4, [(0, spread), (1, attend), (2, trans), (3, mix)])

                @block.vector
                def _(dve):
                    def weights(b, r):
                        wait(dve, s_K, b + 1)
                        wait(dve, s_av, b - 1)
                        for h in range(H0):
                            last = dve.scalar_tensor_tensor(
                                PT[:, r % 2, h * P:(h + 1) * P],
                                PS[:, 2 * (r % 2) + h // 4, (h % 4) * P:(h % 4 + 1) * P],
                                cf[:, ds(b * H0 + h, 1)], MT[:, :], ALU.max, ALU.mult)
                        last.then_inc(s_pt, 1)

                    def norm(b, r):
                        wait(dve, s_av, b + 1)
                        wait(dve, s_ht, b - 1)
                        o = PS[:, 4 + r % 2, 0:H0 * W17].rearrange("p (h w) -> p h w", w=W17)
                        dve.reciprocal(rec[:, r % 2, :], o[:, :, DH])
                        dve.drain()
                        dve.tensor_tensor(hn[:, r % 2, :].rearrange("p (h f) -> p h f", f=DH), o[:, :, 0:DH],
                                          rec[:, r % 2, :].unsqueeze(2).broadcast_to([P, H0, DH]),
                                          ALU.mult).then_inc(s_hn, 1)

                    def residual(b, r):
                        wait(dve, s_y, b + 1)
                        dve.tensor_tensor(C["xs"](b), PS[:, 7, 0:P], C["xs"](b), ALU.add).then_inc(s_res, 1)
                        dve.drain()
                        dve.bn_stats(C["ST"][:, ds(b * 6, 6)], C["xs"](b))
                    pipelined(dve, B, 4, [(0, weights), (1, norm), (3, residual)])

                @block.scalar
                def _(act):
                    def copy_t(b, r):
                        wait(act, s_ht, b + 1)
                        wait(act, s_y, b - 1)
                        act.copy(hnT[:, r % 2, :], PS[:, 6, 0:P]).then_inc(s_hc, 1)
                    pipelined(act, B, 4, [(2, copy_t)])


def ffn0(C):
    nc, io, B, sem, tile, PS = C["nc"], C["io"], C["B"], C["sem"], C["tile"], C["PS"]
    IDF, IDB = C["IDF"], C["IDB"]
    NG = B // GB
    NW2 = 21
    NT = GB // 2
    N = GB * G
    with ExitStack() as ctx:
        def T(name, shape, dt=F32):
            return tile(ctx, "b_" + name, shape, dt)
        WXS = T("WXS", [P, DI])
        WfxT = T("WfxT", [P, DI])
        WinT = T("WinT", [P, KC * 1168])
        WhoT = T("WhoT", [P, KC * DI])
        WoT2 = T("WoT2", [P, KC * P])
        fcT = T("fcT", [P, KC * 8])
        BFX = T("BFX", [64, KC * P])
        BFM = T("BFM", [64, KC * P], BF16)
        Rm = T("Rm", [32, 8])
        LBP = T("LBP", [96, DI], BF16)
        OBP = T("OBP", [96, P], BF16)
        ONB = T("ONB", [96, P], BF16)
        SELH = T("SELH", [8, DI], BF16)
        ON1 = T("ON1", [P, 1])
        LTM = T("LTM", [P, G])
        UTM = T("UTM", [P, G])
        UF = T("UF", [P, P])
        UB = T("UB", [P, P])
        cw = T("cw", [P, 6 * 3])
        cb = T("cb", [P, 6])
        nA = T("nA", [P, 16])
        dtb = T("dtb", [P, 16])
        Dp = T("Dp", [P, 8])
        nw = T("nw", [P, KC])
        rt = T("rt", [P, 8])
        Win = WinT[:, :].rearrange("p (k n) -> p k n", k=KC)
        Who = WhoT[:, :].rearrange("p (k n) -> p k n", k=KC)
        s_w, s_w2 = sem("b_w"), sem("b_w2")
        s_p0, s_p1, s_p2, s_var, s_std = (sem("b_" + x) for x in ("p0", "p1", "p2", "var", "std"))

        with ExitStack() as c2, nc.Block() as block:
            WxR = tile(c2, "b_WxR", [64, 8 * P])
            WsT = tile(c2, "b_WsT", [64, G])
            bxc = tile(c2, "b_bxc", [64, 8])
            row = tile(c2, "b_row", [1, DI])
            rob = tile(c2, "b_rob", [1, DI], BF16)
            bsl = tile(c2, "b_bsl", [1, G])
            obr = tile(c2, "b_obr", [1, P])

            @block.sync
            def _(sp):
                n = [0]

                def ld(dst, src, s=s_w2):
                    sp.dma_start(dst, src).then_inc(s, 16)
                    n[0] += 1
                for dst, key in ((WxR, "bWxR"), (WsT, "bWsT"), (bxc, "bbx")):
                    ld(dst[:, :], io[key], s_w)
                ld(rt[:, :], io["btemp"].partition_broadcast(P), s_w)
                ld(bsl[:, :], io["bbs"], s_w)
                ld(obr[:, :], io["bob"], s_w)
                for dst, key in ((WinT, "bWin"), (WhoT, "bWho"), (WfxT, "bWfx"), (WoT2, "bWo2"), (fcT, "bfc"),
                                 (BFM, "c_bfm"), (Rm, "c_rm"), (SELH, "c_selh"), (LTM, "c_lt"), (UTM, "c_ut"),
                                 (UF, "c_uf"), (UB, "c_ub"), (nw, "bnw")):
                    ld(dst[:, :], io[key])
                ld(BFX[:, :], io["bbfx"].partition_broadcast(64))
                for c in range(2):
                    ld(dtb[:, 8 * c:8 * c + 8], io["bdtb"].partition_broadcast(P))
                    ld(nA[:, 8 * c:8 * c + 8], io["bAl"].partition_broadcast(P))
                ld(Dp[:, :], io["bD"].partition_broadcast(P))
                ld(cw[:, :], io["bcw"])
                ld(cb[:, :], io["bcb"])
                assert n[0] - 6 == NW2
                sp.wait_ge(s_w2, 16 * (n[0] - 6))

            @block.tensor
            def _(pe):
                pe.wait_ge(s_w, 96)
                for h in range(HF):
                    pe.matmul(PS[:, 0, h * G:(h + 1) * G], WxR[:, h * P:(h + 1) * P], WsT[:, :], start=True, stop=True)
                for h in range(HF):
                    last = pe.matmul(PS[0:1, 1, h * G:(h + 1) * G], bxc[:, h:h + 1], WsT[:, :], start=True, stop=True)
                last.then_inc(s_p0, 1)

            @block.vector
            def _(dve):
                dve.memset(LBP[:, :], 0.0)
                dve.memset(OBP[:, :], 0.0)
                dve.memset(ONB[:, :], 1.0)
                dve.memset(ON1[:, :], 1.0)
                dve.wait_ge(s_w, 96)
                dve.tensor_scalar(rt[:, :], rt[:, :], 1e-6, None, ALU.max)
                dve.drain()
                dve.reciprocal(rt[:, :], rt[:, :])
                dve.wait_ge(s_p0, 1)
                dve.drain()

                def by_head(ap, parts):
                    return ap.unsqueeze(2).broadcast_to([parts, HF, G])
                dve.tensor_tensor(WXS[:, :].rearrange("p (h g) -> p h g", g=G),
                                  PS[:, 0, :].rearrange("p (h g) -> p h g", g=G), by_head(rt[:, :], P), ALU.mult)
                r3 = row[:, :].rearrange("p (h g) -> p h g", g=G)
                dve.tensor_tensor(r3, PS[0:1, 1, :].rearrange("p (h g) -> p h g", g=G),
                                  bsl[:, :].unsqueeze(1).broadcast_to([1, HF, G]), ALU.add)
                dve.drain()
                dve.tensor_tensor(r3, r3, by_head(rt[0:1, :], 1), ALU.mult)
                dve.drain()
                for src, w, dst in ((row, DI, LBP), (obr, P, OBP)):
                    for k in range(3):
                        dve.tensor_copy(rob[:, 0:w], src[:, 0:w])
                        dve.drain()
                        dve.tensor_copy(dst[32 * k:32 * k + 1, 0:w], rob[:, 0:w])
                        dve.tensor_tensor(src[:, 0:w], src[:, 0:w], rob[:, 0:w], ALU.subtract)
                        dve.drain()
                dve.wait_ge(s_w2, 16 * NW2)
                dve.tensor_tensor(BFX[:, :], BFX[:, :], BFM[:, :], ALU.mult)
                dve.tensor_scalar(Win[:, :, 0:DI], Win[:, :, 0:DI], 0.5, None, ALU.mult)
                for k in range(KC):
                    dve.tensor_scalar(Who[:, k, :], Who[:, k, :], nw[:, k:k + 1], None, ALU.mult)
                dve.tensor_scalar(cw[:, :], cw[:, :], 0.5, None, ALU.mult)
                dve.tensor_scalar(cb[:, :], cb[:, :], 0.5, None, ALU.mult)
                dve.wait_ge(s_p1, 1)
                dve.tensor_scalar(nA[:, :], nA[:, :], -1.0, None, ALU.mult)
                ln_vector(C, dve, s_var, s_std)

            @block.scalar
            def _(act):
                act.wait_ge(s_w2, 16 * NW2)
                act.activation(nA[:, :], nA[:, :], ACT.Exp).then_inc(s_p1, 1)
                ln_scalar(C, act, s_var, s_std)

        xn = T("xn", [P, 4, P + 1])
        xnT = T("xnT", [P, 2, P])
        nm = T("nm", [P, 2, HF], BF16)
        mT = T("mT", [8, 2, P], BF16)
        E = T("E", [P, 2, DI])
        Z = T("Z", [P, HF])
        rZ = T("rZ", [P, HF])
        sw = T("sw", [P, 2, DI])
        swT = T("swT", [P, GB, DI])
        rs = T("rs", [P, 4])
        sn = T("sn", [P, 4])
        RT = T("RT", [P, GB * KC])
        Tn = T("Tn", [P, 2, DI])
        TT = T("TT", [P, GB, DI])
        R = T("R", [64, N])
        stT = T("stT", [P, KC, N])
        zs = T("zs", [P, KC, N])
        cx = T("cx", [P, KC, N])
        cB = T("cB", [64, 2, N])
        tn = T("tn", [P, 2, N])
        dv = T("dv", [P, 3, NT * 16])
        dtA = T("dtA", [P, NT * 16])
        xd = T("xd", [P, NT * 8])
        Rf = T("Rf", [P, 2, N])
        Dec = T("Dec", [P, N])
        CBl = T("CBl", [P, NT, G])
        CBu = T("CBu", [P, NT, G])
        Wl = T("Wl", [P, N])
        Wu = T("Wu", [P, N])
        XX = T("XX", [P, 3, N])
        R8 = T("R8", [P, GB])
        UU = T("UU", [P, 2, DI])
        ygT = TT[:, 0:4, :]
        sq = TT[:, 4:8, :]
        otT = stT

        (s_xn, s_tr, s_xnT, s_lg, s_nm, s_mt, s_mT, s_lm, s_E, s_sw, s_T, s_swt, s_swT, s_Tn, s_Tt, s_TT, s_rt, s_R,
         s_st, s_stT, s_z, s_th, s_zs, s_u, s_c0, s_c1, s_c2, s_cx, s_dt, s_v, s_sp, s_dv, s_Rf, s_seg, s_Dec, s_cb,
         s_CB, s_W, s_Wp, s_xt, s_xd, s_xdv, s_XX, s_Y, s_yg, s_sq, s_ss, s_ms, s_sd, s_R8, s_ot, s_otT, s_U, s_UU,
         s_UV, s_o, s_X, s_null) = (sem("b2_" + x) for x in
                      ("xn tr xnT lg nm mt mT lm E sw T swt swT Tn Tt TT rt R st stT z th zs u c0 c1 c2 cx dt v sp dv "
                       "Rf seg Dec cb CB W Wp xt xd xdv XX Y yg sq ss ms sd R8 ot otT U UU UV o X null").split())

        def groups(eng, body):
            body(0)
            if NG > 1:
                with eng.Fori(1, NG) as g:
                    body(g)

        def steps(g, stages):
            last = max(lag for lag, _ in stages)
            for t in range(GB + last):
                for lag, emit in stages:
                    if 0 <= t - lag < GB:
                        emit(g * GB + (t - lag), t - lag)

        TTb = [4, 5]
        with nc.Block() as block:
            @block.tensor
            def _(pe):
                def body(g):
                    def trans(b, j):
                        wait(pe, s_xn, b + 1)
                        wait(pe, s_xnT, b)
                        if j == 0:
                            wait(pe, s_UU, g * GB)
                            wait(pe, s_UV, g * GB)
                            wait(pe, s_X, g * GB)
                        pe.transpose(PS[:, 0, 0:P], xn[:, j % 4, 0:P], IDF[:, :]).then_inc(s_tr, 1)

                    def logits(b, j):
                        wait(pe, s_xnT, b + 1)
                        wait(pe, s_E, b - 1)
                        o = PS[:, 1 + j % 2, :]
                        pe.matmul(o, xnT[:, j % 2, :], WXS[:, :], start=True, stop=False)
                        pe.matmul(o, ONB[:, :], LBP[:, :], start=False, stop=True).then_inc(s_lg, 1)

                    def mtrans(b, j):
                        wait(pe, s_nm, b + 1)
                        wait(pe, s_mT, b)
                        pe.transpose(PS[0:8, 3, 0:P // 2].bitcast(BF16), nm[:, j % 2, :], IDB[:, :]).then_inc(s_mt, 1)

                    def msub(b, j):
                        wait(pe, s_mT, b + 1)
                        pe.matmul(PS[:, 1 + j % 2, :], mT[:, j % 2, :], SELH[:, :], start=False, stop=True,
                                  skip_group_check=True).then_inc(s_lm, 1)

                    def slices(b, j):
                        wait(pe, s_sw, b + 1)
                        wait(pe, s_Tn, b)
                        for c in range(KC):
                            o = PS[:, 4 + c // 2, (c % 2) * 256:(c % 2) * 256 + P + 1]
                            last = pe.matmul(o, sw[:, j % 2, c * P:(c + 1) * P], xn[:, j % 4, :], start=True, stop=True)
                        last.then_inc(s_T, 1)
                        wait(pe, s_swT, b)
                        for c in range(KC):
                            last = pe.transpose(PS[:, 6, c * P:(c + 1) * P], sw[:, j % 2, c * P:(c + 1) * P], IDF[:, :])
                        last.then_inc(s_swt, 1)

                    def ttrans(b, j):
                        wait(pe, s_Tn, b + 1)
                        wait(pe, s_TT, b)
                        for c in range(KC):
                            last = pe.transpose(PS[:, 7, c * P:(c + 1) * P], Tn[:, j % 2, c * P:(c + 1) * P], IDF[:, :])
                        last.then_inc(s_Tt, 1)

                    steps(g, [(5, ttrans), (4, slices), (3, msub), (2, mtrans), (1, logits), (0, trans)])

                    pe.transpose(PS[0:32, 4, 0:64], RT[0:64, :], IDF[0:64, 0:64])
                    pe.transpose(PS[0:32, 5, 0:64], RT[64:128, :], IDF[64:128, 64:128]).then_inc(s_rt, 1)
                    wait(pe, s_TT, g * GB + GB)
                    for c in range(KC):
                        for h2 in range(2):
                            h = 2 * c + h2
                            pe.matmul(PS[64 * h2:64 * h2 + 64, c, :], WfxT[:, h * 64:h * 64 + 64],
                                      TT[:, :, h * G:(h + 1) * G], start=True, stop=False)
                        if c == 0:
                            wait(pe, s_R, g + 1)
                        pe.matmul(PS[:, c, :], BFX[:, c * P:(c + 1) * P], R[:, :], start=False, stop=True).then_inc(s_st, 1)
                    wait(pe, s_stT, g * 4 + 4)
                    for m in range(KC):
                        for k in range(KC):
                            last = pe.matmul(PS[:, 4 + m, :], Win[:, k, m * P:(m + 1) * P], stT[:, k, :],
                                             start=(k == 0), stop=(k == KC - 1))
                        last.then_inc(s_z, 1)
                    for m in range(KC):
                        for k in range(KC):
                            last = pe.matmul(PS[:, m, :], Win[:, k, DI + m * P:DI + (m + 1) * P], stT[:, k, :],
                                             start=(k == 0), stop=(k == KC - 1))
                        last.then_inc(s_u, 1)
                    wait(pe, s_zs, g * 4 + 4)
                    for m in range(2):
                        for k in range(KC):
                            last = pe.matmul(PS[0:64, 4 + m, :], Win[:, k, 2 * DI + m * 64:2 * DI + (m + 1) * 64],
                                             stT[:, k, :], start=(k == 0), stop=(k == KC - 1))
                        last.then_inc(s_u, 1)
                    for t in range(NT):
                        for k in range(KC):
                            last = pe.matmul(PS[:, 6, t * 16:(t + 1) * 16], stT[:, k, t * P:(t + 1) * P],
                                             Win[:, k, 1152:1168], start=(k == 0), stop=(k == KC - 1))
                    last.then_inc(s_dt, 1)
                    wait(pe, s_cx, g * 6 + 4)
                    for t in range(NT):
                        for k in range(KC):
                            last = pe.matmul(PS[:, 7, t * 8:(t + 1) * 8], cx[:, k, t * P:(t + 1) * P],
                                             fcT[:, k * 8:(k + 1) * 8], start=(k == 0), stop=(k == KC - 1))
                    last.then_inc(s_xd, 1)
                    wait(pe, s_cx, g * 6 + 6)
                    wait(pe, s_v, g + 1)
                    pe.sem_inc(s_null, 1)
                    for j in range(GB):
                        last = pe.matmul(PS[64 * (j % 2):64 * (j % 2) + 64, 6, (j // 2) * G:(j // 2 + 1) * G],
                                         cB[:, 0, j * G:(j + 1) * G], cB[:, 1, j * G:(j + 1) * G], start=True, stop=True)
                    last.then_inc(s_cb, 1)

                    for t in range(NT):
                        n = g * NT + t
                        wait(pe, s_Rf, n + 1)
                        wait(pe, s_Dec, n)
                        pe.matmul(PS[:, 4, :], UF[:, :], Rf[:, 0, :], start=True, stop=False)
                        pe.matmul(PS[:, 4, :], UB[:, :], Rf[:, 1, :], start=False, stop=True).then_inc(s_seg, 1)
                        wait(pe, s_XX, n)
                        for c in range(KC):
                            last = pe.transpose(PS[:, 5, c * P:(c + 1) * P], cx[:, c, t * P:(t + 1) * P], IDF[:, :])
                        last.then_inc(s_xt, 1)
                        wait(pe, s_XX, n + 1)
                        wait(pe, s_W, n + 1)
                        wait(pe, s_Wp, n + 1)
                        for par in range(2):
                            q = slice(64 * par, 64 * par + 64)
                            for c in range(KC):
                                k0 = 2 * par + c // 2
                                col = (c % 2) * 256 + t * G
                                pe.matmul(PS[:, k0, col:col + G], XX[q, 2, c * P:(c + 1) * P],
                                          IDF[q, 64 * par:64 * par + 64], start=True, stop=False)
                                for h2 in range(2):
                                    h = 2 * c + h2
                                    o = PS[64 * h2:64 * h2 + 64, k0, col:col + G]
                                    pe.matmul(o, XX[q, 0, h * 64:(h + 1) * 64], Wl[q, h * G:(h + 1) * G],
                                              start=False, stop=False)
                                    last = pe.matmul(o, XX[q, 1, h * 64:(h + 1) * 64], Wu[q, h * G:(h + 1) * G],
                                                     start=False, stop=True)
                        last.then_inc(s_Y, 1)
                    wait(pe, s_sq, g + 1)
                    for w in range(-1, GB):
                        lo, hi = max(w, 0), min(w + 2, GB)
                        q = slice(64 * (lo - w), 64 * (hi - w))
                        for k in range(KC):
                            last = pe.matmul(PS[q, 4, w + 1:w + 2], sq[:, k, lo * G:hi * G], ON1[:, :],
                                             start=(k == 0), stop=(k == KC - 1))
                    last.then_inc(s_ss, 1)
                    wait(pe, s_yg, g * 2 + 2)
                    for i in range(KC):
                        m = (i + 1) % KC
                        if m == 0:
                            wait(pe, s_ms, g + 1)
                        for k in range(KC):
                            last = pe.matmul(PS[:, 4 + m, :], Who[:, k, m * P:(m + 1) * P], ygT[:, k, :],
                                             start=(k == 0), stop=(k == KC - 1))
                        last.then_inc(s_ot, 1)
                    wait(pe, s_otT, g * 4 + 4)
                    for j in range(GB + 1):
                        if j < GB:
                            b = g * GB + j
                            wait(pe, s_UU, b - 1)
                            wait(pe, s_UV, b - 1)
                            pe.sem_inc(s_null, 1)
                            for c in range(KC):
                                for h2 in range(2):
                                    q = slice(64 * h2, 64 * h2 + 64)
                                    last = pe.matmul(PS[q, 2 * (j % 2) + h2, c * P:(c + 1) * P],
                                                     otT[q, c, j * G:(j + 1) * G], WoT2[q, c * P:(c + 1) * P],
                                                     start=True, stop=True)
                            last.then_inc(s_U, 1)
                        if j >= 1:
                            b = g * GB + j - 1
                            wait(pe, s_UU, b + 1)
                            wait(pe, s_UV, b + 1)
                            wait(pe, s_X, b - 1)
                            o = PS[:, 4 + (j - 1) % 2, 0:P]
                            pe.matmul(o, ONB[:, :], OBP[:, :], start=True, stop=False)
                            for c in range(KC):
                                last = pe.matmul(o, swT[:, j - 1, c * P:(c + 1) * P], UU[:, (j - 1) % 2, c * P:(c + 1) * P],
                                                 start=False, stop=(c == KC - 1))
                            last.then_inc(s_o, 1)
                groups(pe, body)

            @block.vector
            def _(dve):
                dve.memset(xn[:, :, P:P + 1], 1.0)
                dve.memset(CBl[:, :, :], 0.0)
                dve.memset(CBu[:, :, :], 0.0)
                dve.drain()

                def body(g):
                    def norm(b, j):
                        wait(dve, s_T, b - 3)
                        normalise(C, dve, xn[:, j % 4, 0:P], b).then_inc(s_xn, 1)

                    def maxima(b, j):
                        wait(dve, s_lg, b + 1)
                        wait(dve, s_mt, b - 1)
                        dve.tensor_reduce(nm[:, j % 2, :], PS[:, 1 + j % 2, :].rearrange("p (h g) -> p h g", g=G),
                                          AX.X, ALU.max, negate=True).then_inc(s_nm, 1)

                    def weights(b, j):
                        wait(dve, s_E, b + 1)
                        e3 = E[:, j % 2, :].rearrange("p (h g) -> p h g", g=G)
                        dve.tensor_reduce(Z[:, :], e3, AX.X, ALU.add)
                        dve.drain()
                        dve.reciprocal(rZ[:, :], Z[:, :])
                        dve.drain()
                        wait(dve, s_swt, b - 1)
                        dve.tensor_tensor(sw[:, j % 2, :].rearrange("p (h g) -> p h g", g=G), e3,
                                          rZ[:, :].unsqueeze(2).broadcast_to([P, HF, G]), ALU.mult).then_inc(s_sw, 1)

                    def means(b, j):
                        wait(dve, s_T, b + 1)
                        t4 = PS[:, 4:6, :].rearrange("p k (c n) -> p (k c) n", c=2)
                        dve.tensor_copy(sn[:, :], t4[:, :, P])
                        dve.drain()
                        dve.tensor_scalar(rs[:, :], sn[:, :], 1e-5, None, ALU.add)
                        dve.drain()
                        dve.reciprocal(rs[:, :], rs[:, :])
                        dve.drain()
                        if j == 0:
                            wait(dve, s_rt, g)
                        dve.tensor_tensor(RT[:, j * KC:(j + 1) * KC], sn[:, :], rs[:, :], ALU.mult)
                        wait(dve, s_Tt, b - 1)
                        dve.tensor_tensor(Tn[:, j % 2, :].rearrange("p (c n) -> p c n", n=P), t4[:, :, 0:P],
                                          rs[:, :].unsqueeze(2).broadcast_to([P, KC, P]), ALU.mult)
                        dve.drain().then_inc(s_Tn, 1)
                    steps(g, [(0, norm), (4, means), (3, weights), (1, maxima)])

                    wait(dve, s_rt, g + 1)
                    for h2 in range(2):
                        last = dve.tensor_tensor(R[32 * h2:32 * h2 + 32, :].rearrange("p (b g) -> p b g", g=G),
                                                 PS[0:32, 4 + h2, 0:G].unsqueeze(1).broadcast_to([32, GB, G]),
                                                 Rm[:, :].unsqueeze(2).broadcast_to([32, GB, G]), ALU.mult)
                    last.then_inc(s_R, 1)
                    for c in range(KC):
                        wait(dve, s_st, g * 4 + c + 1)
                        dve.tensor_copy(stT[:, c, :], PS[:, c, :]).then_inc(s_stT, 1)
                    for m in range(KC):
                        wait(dve, s_th, g * 10 + m + 1)
                        dve.scalar_tensor_tensor(zs[:, m, :], tn[:, m % 2, :], 1.0, PS[:, 4 + m, :], ALU.add, ALU.mult)\
                           .then_inc(s_zs, 1)
                    for m in range(6):
                        wait(dve, s_c0, g * 6 + m + 1)
                        p, k = (P, m) if m < KC else (64, m)
                        u = PS[0:p, k, :].rearrange("p (b l) -> p b l", l=G)
                        dst = (cx[:, m, :] if m < KC else cB[:, m - KC, :]).rearrange("p (b l) -> p b l", l=G)
                        dve.scalar_tensor_tensor(dst[:, :, 1:], u[:, :, 0:G - 1], cw[0:p, 3 * m + 1:3 * m + 2],
                                                 dst[:, :, 1:], ALU.mult, ALU.add)
                        dve.drain()
                        dve.scalar_tensor_tensor(dst[:, :, 2:], u[:, :, 0:G - 2], cw[0:p, 3 * m:3 * m + 1],
                                                 dst[:, :, 2:], ALU.mult, ALU.add)
                        dve.drain().then_inc(s_c1, 1)
                        if m >= 1:
                            silu(g, m - 1)
                    silu(g, 5)
                    wait(dve, s_dt, g + 1)
                    v, e, l = dv[:, 0, :], dv[:, 1, :], dv[:, 2, :]
                    v3 = v.rearrange("p (t h) -> p t h", h=16)
                    dve.tensor_tensor(v3, PS[:, 6, 0:NT * 16].rearrange("p (t h) -> p t h", h=16),
                                      dtb[:, :].unsqueeze(1).broadcast_to([P, NT, 16]), ALU.add)
                    dve.drain().then_inc(s_v, 1)
                    dve.scalar_tensor_tensor(e, v, -1.0, v, ALU.mult, ALU.max)
                    dve.drain().then_inc(s_dv, 1)
                    wait(dve, s_sp, g + 1)
                    dve.scalar_tensor_tensor(v, v, 0.0, l, ALU.max, ALU.add)
                    dve.drain()
                    dve.tensor_tensor(dtA[:, :].rearrange("p (t h) -> p t h", h=16), v3,
                                      nA[:, :].unsqueeze(1).broadcast_to([P, NT, 16]), ALU.mult)
                    dve.drain().then_inc(s_dv, 1)
                    wait(dve, s_xd, g + 1)
                    dve.tensor_tensor(xd[:, :].rearrange("p (t h) -> p t h", h=8),
                                      PS[:, 7, 0:NT * 8].rearrange("p (t h) -> p t h", h=8),
                                      Dp[:, :].unsqueeze(1).broadcast_to([P, NT, 8]), ALU.add).then_inc(s_xdv, 1)
                    wait(dve, s_cb, g + 1)
                    cbp = PS[:, 6, 0:NT * G].rearrange("p (t l) -> p t l", l=G)
                    dve.tensor_tensor(CBl[:, :, 1:], cbp[:, :, 0:G - 1],
                                      LTM[:, 1:].unsqueeze(1).broadcast_to([P, NT, G - 1]), ALU.mult)
                    dve.tensor_tensor(CBu[:, :, 0:G - 1], cbp[:, :, 1:],
                                      UTM[:, 0:G - 1].unsqueeze(1).broadcast_to([P, NT, G - 1]), ALU.mult)
                    dve.drain().then_inc(s_CB, 1)
                    for t in range(NT):
                        n = g * NT + t
                        wait(dve, s_xt, n + 1)
                        wait(dve, s_Y, n)
                        x3 = PS[:, 5, :].rearrange("p (h c) -> p h c", c=64)
                        for i, s in enumerate((v[:, t * 16:t * 16 + 8], v[:, t * 16 + 8:t * 16 + 16],
                                               xd[:, t * 8:t * 8 + 8])):
                            last = dve.tensor_tensor(XX[:, i, :].rearrange("p (h c) -> p h c", c=64), x3,
                                                     s.unsqueeze(2).broadcast_to([P, 8, 64]), ALU.mult)
                        last.then_inc(s_XX, 1)
                        wait(dve, s_Dec, n + 1)
                        dve.tensor_tensor(Wl[:, :].rearrange("p (h l) -> p h l", l=G),
                                          Dec[:, :].rearrange("p (h l) -> p h l", l=G),
                                          CBl[:, t, :].unsqueeze(1).broadcast_to([P, 8, G]), ALU.mult).then_inc(s_W, 1)
                    wait(dve, s_Y, g * NT + NT)
                    for par in range(2):
                        def view(a):
                            return a.rearrange("p c (t r l) -> p c t r l", r=2, l=G)[:, :, :, par, :]
                        yv = PS[:, 2 * par:2 * par + 2, :].rearrange("p k (c t l) -> p (k c) t l", c=2, l=G)
                        last = dve.tensor_tensor(view(ygT), yv, view(zs), ALU.mult)
                        last.then_inc(s_yg, 1)
                    wait(dve, s_ss, g + 1)
                    for h2 in range(2):
                        q = slice(64 * h2, 64 * h2 + 64)
                        dve.tensor_scalar(R8[q, :], PS[q, 4, 1 - h2:1 - h2 + GB], 1.0 / DI, 1e-5, ALU.mult, ALU.add)
                    dve.drain().then_inc(s_ms, 1)
                    wait(dve, s_sd, g + 1)
                    dve.reciprocal(R8[:, :], R8[:, :])
                    dve.drain().then_inc(s_R8, 1)
                    for j in range(GB + 1):
                        if j < GB:
                            b = g * GB + j
                            wait(dve, s_U, b + 1)
                            wait(dve, s_o, b - 1)
                            dve.tensor_scalar(UU[64:128, j % 2, :], PS[64:128, 2 * (j % 2) + 1, :], R8[64:128, j:j + 1],
                                              None, ALU.mult).then_inc(s_UV, 1)
                        if j >= 1:
                            b = g * GB + j - 1
                            wait(dve, s_o, b + 1)
                            dve.tensor_tensor(C["xs"](b), PS[:, 4 + (j - 1) % 2, 0:P], C["xs"](b), ALU.add).then_inc(s_X, 1)
                            dve.drain()
                            dve.bn_stats(C["ST"][:, ds(b * 6, 6)], C["xs"](b))

                def silu(g, m):
                    p = P if m < KC else 64
                    dst = cx[:, m, :] if m < KC else cB[:, m - KC, :]
                    wait(dve, s_th, g * 10 + 4 + m + 1)
                    dve.scalar_tensor_tensor(dst, tn[0:p, m % 2, :], 1.0, dst, ALU.add, ALU.mult).then_inc(s_cx, 1)
                groups(dve, body)

            @block.gpsimd
            def _(pool):
                def body(g):
                    wait(pool, s_dv, g * 2 + 2)
                    wait(pool, s_CB, g + 1)
                    for t in range(NT):
                        n = g * NT + t
                        wait(pool, s_seg, n)
                        for d, M in enumerate((LTM, UTM)):
                            last = pool.tensor_tensor(
                                Rf[:, d, :].rearrange("p (h l) -> p h l", l=G),
                                dtA[:, t * 16 + 8 * d:t * 16 + 8 * d + 8].unsqueeze(2).broadcast_to([P, 8, G]),
                                M[:, :].unsqueeze(1).broadcast_to([P, 8, G]), ALU.mult)
                        pool.drain().then_inc(s_Rf, 1)
                        wait(pool, s_Dec, n + 1)
                        wait(pool, s_Y, n)
                        pool.tensor_tensor(Wu[:, :].rearrange("p (h l) -> p h l", l=G),
                                           Dec[:, :].rearrange("p (h l) -> p h l", l=G),
                                           CBu[:, t, :].unsqueeze(1).broadcast_to([P, 8, G]), ALU.mult).then_inc(s_Wp, 1)
                groups(pool, body)

            @block.scalar
            def _(act):
                def body(g):
                    def copy_t(b, j):
                        wait(act, s_tr, b + 1)
                        wait(act, s_lg, b - 1)
                        act.copy(xnT[:, j % 2, :], PS[:, 0, 0:P]).then_inc(s_xnT, 1)

                    def copy_m(b, j):
                        wait(act, s_mt, b + 1)
                        wait(act, s_lm, b - 1)
                        act.copy(mT[:, j % 2, :], PS[0:8, 3, 0:P // 2].bitcast(BF16)).then_inc(s_mT, 1)

                    def expo(b, j):
                        wait(act, s_lm, b + 1)
                        wait(act, s_sw, b - 1)
                        act.activation(E[:, j % 2, :], PS[:, 1 + j % 2, :], ACT.Exp).then_inc(s_E, 1)

                    def copy_sw(b, j):
                        wait(act, s_swt, b + 1)
                        wait(act, s_o, b - GB + 1)
                        act.copy(swT[:, j, :], PS[:, 6, :]).then_inc(s_swT, 1)

                    def copy_tt(b, j):
                        wait(act, s_Tt, b + 1)
                        if j == 0:
                            wait(act, s_ot, g * 4)
                            wait(act, s_ss, g)
                        act.copy(TT[:, j, :], PS[:, 7, :]).then_inc(s_TT, 1)
                    steps(g, [(5, copy_tt), (4, copy_sw), (3, expo), (2, copy_m), (0, copy_t)])
                    for m in range(KC):
                        wait(act, s_z, g * 4 + m + 1)
                        wait(act, s_zs, g * 4 + m - 1)
                        if m < 2:
                            wait(act, s_cx, g * 6 + m - 1)
                        act.activation(tn[:, m % 2, :], PS[:, 4 + m, :], ACT.Tanh).then_inc(s_th, 1)
                    for m in range(7):
                        if m < 6:
                            p = P if m < KC else 64
                            dst = cx[:, m, :] if m < KC else cB[:, m - KC, :]
                            wait(act, s_u, g * 6 + m + 1)
                            act.activation(dst, PS[0:p, m, :], ACT.Identity, bias=cb[0:p, m:m + 1],
                                           scale=cw[0:p, 3 * m + 2:3 * m + 3]).then_inc(s_c0, 1)
                        if m >= 1:
                            i = m - 1
                            p = P if i < KC else 64
                            src = cx[:, i, :] if i < KC else cB[:, i - KC, :]
                            wait(act, s_c1, g * 6 + i + 1)
                            if i < 2:
                                wait(act, s_zs, g * 4 + 4)
                            else:
                                wait(act, s_cx, g * 6 + i - 1)
                            act.activation(tn[0:p, i % 2, :], src, ACT.Tanh).then_inc(s_th, 1)
                    wait(act, s_dv, g * 2 + 1)
                    act.activation(dv[:, 1, :], dv[:, 1, :], ACT.Exp, scale=-1.0)
                    act.drain()
                    act.activation(dv[:, 2, :], dv[:, 1, :], ACT.Ln, bias=1.0).then_inc(s_sp, 1)
                    for t in range(NT):
                        n = g * NT + t
                        wait(act, s_seg, n + 1)
                        wait(act, s_W, n)
                        wait(act, s_Wp, n)
                        act.activation(Dec[:, :], PS[:, 4, :], ACT.Exp).then_inc(s_Dec, 1)
                    wait(act, s_yg, g * 2 + 2)
                    act.activation(sq, ygT, ACT.Square).then_inc(s_sq, 1)
                    wait(act, s_ms, g + 1)
                    act.activation(R8[:, :], R8[:, :], ACT.Sqrt).then_inc(s_sd, 1)
                    for i in range(KC):
                        m = (i + 1) % KC
                        wait(act, s_ot, g * 4 + i + 1)
                        act.copy(otT[:, m, :], PS[:, 4 + m, :]).then_inc(s_otT, 1)
                    wait(act, s_R8, g + 1)
                    for j in range(GB):
                        b = g * GB + j
                        wait(act, s_U, b + 1)
                        wait(act, s_o, b - 1)
                        act.mul(UU[0:64, j % 2, :], PS[0:64, 2 * (j % 2), :], R8[0:64, j:j + 1]).then_inc(s_UU, 1)
                groups(act, body)


def gnn1(C):
    nc, io, B, NQ, sem, tile, PS = C["nc"], C["io"], C["B"], C["NQ"], C["sem"], C["tile"], C["PS"]
    IDF = C["IDF"]
    WC = P + 2
    with ExitStack() as ctx:
        VS = tile(ctx, "c_VS", [P, B * WC])
        V3 = VS[:, :].rearrange("p (b w) -> p b w", w=WC)
        cf = tile(ctx, "c_cf", [P, B])
        bf = tile(ctx, "c_bf", [P, B])
        KT = tile(ctx, "c_KT", [P, NQ * P], BF16)
        sel = tile(ctx, "c_sel", [P, 4 * P], BF16)
        MT = tile(ctx, "c_MT", [P, P])
        adj = tile(ctx, "c_adj", [P, P], I32)
        mf = tile(ctx, "c_mf", [P, P])
        av = tile(ctx, "c_av", [P, 2 * P])
        tmp = tile(ctx, "c_tmp", [P, P])
        WT = tile(ctx, "c_WT", [P, P])
        s_wd, s_m3, s_mt, s_mc, s_wt, s_sl = (sem("c_" + x) for x in ("wd", "m3", "mt", "mc", "wt", "sl"))

        class Load:
            count, zcount = 16, 1

            def __call__(self, block, W, s_w, s_wz):
                self.W, self.s_w, self.s_wz = W, s_w, s_wz

                @block.sync
                def _(sp):
                    sp.dma_start(W[:, 0:P], io["cW"]).then_inc(s_w, 16)
                    sp.dma_start(av[:, :], io["ca"].partition_broadcast(P)).then_inc(s_wd, 16)
                    sp.dma_start(adj[:, :], io["adj"]).then_inc(s_wd, 16)
                    sp.dma_start(sel[:, :], io["c_sel"][:, 0:4 * P]).then_inc(s_sl, 16)
                    sp.wait_ge(s_sl, 16)

            def vector(self, dve):
                dve.wait_ge(self.s_w, 16)
                dve.wait_ge(s_wd, 32)
                for k in range(2):
                    dve.tensor_tensor(tmp[:, :], self.W[:, 0:P], av[:, k * P:(k + 1) * P], ALU.mult)
                    dve.drain()
                    dve.tensor_reduce(self.W[:, P + k:P + k + 1], tmp[:, :], AX.X, ALU.add)
                    dve.drain()
                dve.sem_inc(self.s_wz, 1)
                dve.tensor_copy(mf[:, :], adj[:, :])
                dve.drain()
                dve.tensor_scalar(mf[:, :], mf[:, :], 0.0, None, ALU.is_gt)

        project(C, "c_", ctx, WC, Load(), VS)
        with nc.Block() as block:
            @block.tensor
            def _(pe):
                pe.transpose(PS[:, 0, 0:P], mf[:, :], IDF[:, :]).then_inc(s_mt, 1)

            @block.vector
            def _(dve):
                dve.wait_ge(s_mt, 1)
                dve.tensor_copy(MT[:, :], PS[:, 0, 0:P])
        with ExitStack() as c2:
            factors(C, "c_", c2, V3[:, :, P:P + 1], V3[:, :, P + 1:P + 2], 1, cf[:, :], bf[:, :], KT)

        with ExitStack() as c2:
            VX = tile(c2, "c_VX", [P, 2, P + 1])
            PT = tile(c2, "c_PT", [P, 2, P])
            rec = tile(c2, "c_rec", [P, 2, 1])
            neg = tile(c2, "c_neg", [P, 2, P])
            ex = tile(c2, "c_ex", [P, 2, P])
            pos = tile(c2, "c_pos", [P, 2, P])
            s_vx, s_K, s_pt, s_av, s_ng, s_ex, s_res = (
                sem("c2_" + x) for x in ("vx", "K", "pt", "av", "ng", "ex", "res"))
            with nc.Block() as block:
                @block.gpsimd
                def _(pool):
                    def values(b, r):
                        wait(pool, s_av, b - 1)
                        bb = bf[:, ds(b, 1)]
                        pool.tensor_tensor(VX[:, r % 2, 0:P], VS[:, ds(b * WC, P)], bb.broadcast_to([P, P]), ALU.mult)
                        pool.tensor_copy(VX[:, r % 2, P:P + 1], bb)
                        pool.drain().then_inc(s_vx, 1)
                    pipelined(pool, B, 2, [(0, values)])

                @block.tensor
                def _(pe):
                    def spread(b, r):
                        wait(pe, s_pt, b - 1)
                        pe.matmul(PS[:, r % 2, 0:P], sel[0:96, r * P:(r + 1) * P],
                                  KT[0:96, ds((b - r) * (P // 4), P)], start=True, stop=True).then_inc(s_K, 1)

                    def attend(b, r):
                        wait(pe, s_pt, b + 1)
                        wait(pe, s_vx, b + 1)
                        wait(pe, s_ex, b - 1)
                        wait(pe, s_ng, b - 1)
                        pe.matmul(PS[:, 4 + r % 2, 0:P + 1], PT[:, r % 2, :], VX[:, r % 2, :],
                                  start=True, stop=True).then_inc(s_av, 1)
                    pipelined(pe, B, 4, [(0, spread), (1, attend)])

                @block.vector
                def _(dve):
                    def weights(b, r):
                        wait(dve, s_K, b + 1)
                        wait(dve, s_av, b - 1)
                        dve.scalar_tensor_tensor(PT[:, r % 2, :], PS[:, r % 2, 0:P], cf[:, ds(b, 1)], MT[:, :],
                                                 ALU.max, ALU.mult).then_inc(s_pt, 1)

                    def norm(b, r):
                        wait(dve, s_av, b + 1)
                        wait(dve, s_ex, b - 1)
                        dve.reciprocal(rec[:, r % 2, :], PS[:, 4 + r % 2, P:P + 1])
                        dve.drain()
                        dve.tensor_scalar(neg[:, r % 2, :], PS[:, 4 + r % 2, 0:P], rec[:, r % 2, :], 0.0,
                                          ALU.mult, ALU.min).then_inc(s_ng, 1)

                    def residual(b, r):
                        wait(dve, s_ex, b + 1)
                        dve.scalar_tensor_tensor(pos[:, r % 2, :], ex[:, r % 2, :], -1.0, pos[:, r % 2, :],
                                                 ALU.add, ALU.add)
                        dve.drain()
                        dve.tensor_tensor(C["xs"](b), C["xs"](b), pos[:, r % 2, :], ALU.add)
                        dve.drain().then_inc(s_res, 1)
                        dve.bn_stats(C["ST"][:, ds(b * 6, 6)], C["xs"](b))
                    pipelined(dve, B, 2, [(0, weights), (1, norm), (2, residual)])

                @block.scalar
                def _(act):
                    def parts(b, r):
                        wait(act, s_ng, b + 1)
                        wait(act, s_res, b - 1)
                        act.activation(ex[:, r % 2, :], neg[:, r % 2, :], ACT.Exp)
                        act.activation(pos[:, r % 2, :], PS[:, 4 + r % 2, 0:P], ACT.Relu,
                                       scale=rec[:, r % 2, :])
                        act.drain().then_inc(s_ex, 1)
                    pipelined(act, B, 2, [(0, parts)])


def moe(C, out):
    nc, io, B, sem, tile, PS = C["nc"], C["io"], C["B"], C["sem"], C["tile"], C["PS"]
    IDF = C["IDF"]
    NTG = B // 4
    NH1 = E8 * HID
    with ExitStack() as ctx:
        gates = tile(ctx, "d_gates", [P, B * E8])
        wh = tile(ctx, "d_wh", [P, 2, NH1], BF16)
        wl = tile(ctx, "d_wl", [P, 2, NH1], BF16)
        w2h = tile(ctx, "d_w2h", [P, E8 * 3 * P], BF16)
        w2l = tile(ctx, "d_w2l", [P, E8 * 3 * P], BF16)
        s_rt = sem("d_rt")

        with ExitStack() as c2:
            LG = tile(c2, "d_LG", [P, B * E8])
            mm = tile(c2, "d_mm", [P, B])
            m1 = tile(c2, "d_m1", [P, B])
            m2 = tile(c2, "d_m2", [P, B])
            oh = tile(c2, "d_oh", [P, 2, B * E8])
            sc = tile(c2, "d_sc", [P, B * E8])
            r8 = tile(c2, "d_r8", [P, E8])
            wst = tile(c2, "d_wst", [P, 3, E8 * 3 * P])
            s_r8, s_wst, s_e0, s_e1 = (sem("d_" + x) for x in ("r8", "wst", "e0", "e1"))

            class Load:
                count, zcount = 16, 0

                def __call__(self, block, W, s_w, s_wz):
                    @block.sync
                    def _(sp):
                        sp.dma_start(W[:, :], io["drw"]).then_inc(s_w, 16)
                        sp.dma_start(r8[:, :], io["c_r8"].partition_broadcast(P)).then_inc(s_wst, 16)
                        sp.dma_start(wst[:, 0, 0:NH1], io["dw1"]).then_inc(s_wst, 16)
                        sp.dma_start(wst[:, 1, 0:NH1], io["dw3"]).then_inc(s_wst, 16)
                        sp.dma_start(wst[:, 2, :], io["dw2"]).then_inc(s_wst, 16)
                        sp.wait_ge(s_wst, 64)

                def vector(self, dve):
                    pass
            project(C, "d_", c2, E8, Load(), LG)

            with nc.Block() as block:
                @block.vector
                def _(dve):
                    def by(a):
                        return a[:, :].unsqueeze(2).broadcast_to([P, B, E8])

                    def v(a):
                        return a.rearrange("p (b e) -> p b e", e=E8)
                    L, S = v(LG[:, :]), v(sc[:, :])
                    r8b = r8[:, :].unsqueeze(1).broadcast_to([P, B, E8])
                    dve.tensor_reduce(mm[:, :], L, AX.X, ALU.max)
                    dve.drain()
                    dve.tensor_tensor(L, L, by(mm), ALU.subtract)
                    dve.drain().then_inc(s_e0, 1)
                    for k in range(2):
                        dve.tensor_copy(wh[:, k, :], wst[:, k, 0:NH1])
                        dve.drain()
                        dve.tensor_tensor(wl[:, k, :], wst[:, k, 0:NH1], wh[:, k, :], ALU.subtract)
                    dve.wait_ge(s_e1, 1)
                    dve.tensor_reduce(mm[:, :], L, AX.X, ALU.add)
                    dve.drain()
                    dve.reciprocal(mm[:, :], mm[:, :])
                    dve.drain()
                    dve.tensor_tensor(L, L, by(mm), ALU.mult)
                    dve.drain()
                    for k, m in enumerate((m1, m2)):
                        o = v(oh[:, k, :])
                        dve.tensor_reduce(m[:, :], L, AX.X, ALU.max)
                        dve.drain()
                        dve.tensor_tensor(S, L, by(m), ALU.is_equal)
                        dve.drain()
                        dve.tensor_tensor(S, S, r8b, ALU.mult)
                        dve.drain()
                        dve.tensor_reduce(mm[:, :], S, AX.X, ALU.max)
                        dve.drain()
                        dve.tensor_tensor(o, S, by(mm), ALU.is_equal)
                        dve.drain()
                        if k == 0:
                            dve.scalar_tensor_tensor(LG[:, :], oh[:, 0, :], -2.0, LG[:, :], ALU.mult, ALU.add)
                            dve.drain()
                    dve.scalar_tensor_tensor(mm[:, :], m1[:, :], 1e-9, m2[:, :], ALU.add, ALU.add)
                    dve.drain()
                    dve.reciprocal(mm[:, :], mm[:, :])
                    dve.drain()
                    for k, m in enumerate((m1, m2)):
                        dve.tensor_tensor(m[:, :], m[:, :], mm[:, :], ALU.mult)
                        dve.drain()
                        dve.tensor_tensor(v(oh[:, k, :]), v(oh[:, k, :]), by(m), ALU.mult)
                    dve.drain()
                    dve.tensor_tensor(gates[:, :], oh[:, 0, :], oh[:, 1, :], ALU.add)

                @block.scalar
                def _(act):
                    act.wait_ge(s_e0, 1)
                    act.activation(LG[:, :], LG[:, :], ACT.Exp).then_inc(s_e1, 1)

                @block.gpsimd
                def _(pool):
                    pool.tensor_copy(w2h[:, :], wst[:, 2, :])
                    pool.drain()
                    pool.tensor_tensor(w2l[:, :], wst[:, 2, :], w2h[:, :], ALU.subtract)

        xn = tile(ctx, "d_xn2", [P, 4, P])
        xh = tile(ctx, "d_xh", [P, 2, 512], BF16)
        xl = tile(ctx, "d_xl", [P, 2, 512], BF16)
        sg = tile(ctx, "d_sg", [P, 2, 512])
        hf = tile(ctx, "d_hf", [P, 2, 512])
        hh = tile(ctx, "d_hh", [P, 2, 3, 512], BF16)
        hl = tile(ctx, "d_hl", [P, 2, 3, 512], BF16)
        s_xn, s_tr, s_xh, s_xl, s_up, s_sg, s_hf, s_hh, s_hl, s_y, s_acc, s_out = (
            sem("d2_" + x) for x in "xn tr xh xl up sg hf hh hl y acc out".split())
        NU = E8 * 3

        def groups(eng, body):
            body(0, NTG == 1)
            if NTG > 2:
                with eng.Fori(1, NTG - 1) as g:
                    body(g, False)
            if NTG > 1:
                body(NTG - 1, True)

        with nc.Block() as block:
            @block.tensor
            def _(pe):
                def prep(g):
                    wait(pe, s_xn, g * 4 + 4)
                    wait(pe, s_xl, g)
                    for j in range(4):
                        last = pe.transpose(PS[:, 6, j * P:(j + 1) * P], xn[:, j, :], IDF[:, :])
                    last.then_inc(s_tr, 1)

                def up(g, e, gp):
                    for k in range(3):
                        i = e * 3 + k
                        w = HCH[k]
                        cols = slice(e * HID + 128 * k, e * HID + 128 * k + w)
                        wait(pe, s_hf, g * NU + i - 1)
                        if i == 0:
                            wait(pe, s_xl, g + 1)
                        for m in range(2):
                            o = PS[0:w, 2 * (i % 2) + m, :]
                            pe.matmul(o, wh[:, m, cols], gp(xh), start=True, stop=False)
                            pe.matmul(o, wh[:, m, cols], gp(xl), start=False, stop=False)
                            last = pe.matmul(o, wl[:, m, cols], gp(xh), start=False, stop=True)
                        last.then_inc(s_up, 1)

                def down(n, e):
                    wait(pe, s_hl, n * 3 + 3)
                    wait(pe, s_hh, n * 3 + 3)
                    wait(pe, s_acc, n - 1)
                    for t in range(4):
                        o = PS[:, 4 + e % 2, t * P:(t + 1) * P]
                        q = slice(t * P, (t + 1) * P)
                        for k in range(3):
                            w = HCH[k]
                            wc = slice((e * 3 + k) * P, (e * 3 + k + 1) * P)
                            pe.matmul(o, hh[0:w, e % 2, k, q], w2h[0:w, wc], start=(k == 0), stop=False)
                            pe.matmul(o, hh[0:w, e % 2, k, q], w2l[0:w, wc], start=False, stop=False)
                            last = pe.matmul(o, hl[0:w, e % 2, k, q], w2h[0:w, wc], start=False, stop=(k == 2))
                    last.then_inc(s_y, 1)

                def body(g, end):
                    def gp(a):
                        return a[:, :, :].rearrange("p a n -> p (a n)")[:, ds((g % 2) * 512, 512)]
                    for e in range(E8):
                        up(g, e, gp)
                        if e > 0 or not (isinstance(g, int) and g == 0):
                            down(g * E8 + (e - 1), (e - 1) % E8)
                        if e == 4 and not end:
                            prep(g + 1)
                    if end:
                        down(g * E8 + E8 - 1, E8 - 1)
                prep(0)
                groups(pe, body)

            @block.vector
            def _(dve):
                def prep(g):
                    wait(dve, s_tr, g)
                    for j in range(4):
                        normalise(C, dve, xn[:, j, :], g * 4 + j).then_inc(s_xn, 1)

                def split(g):
                    wait(dve, s_tr, g + 1)
                    wait(dve, s_up, (g - 1) * NU)
                    def gp(a):
                        return a[:, :, :].rearrange("p a n -> p (a n)")[:, ds((g % 2) * 512, 512)]
                    dve.tensor_copy(gp(xh), PS[:, 6, :])
                    dve.drain()
                    dve.tensor_tensor(gp(xl), PS[:, 6, :], gp(xh), ALU.subtract).then_inc(s_xl, 1)

                def hidden(g, i):
                    w = HCH[i % 3]
                    n = g * NU + i
                    wait(dve, s_sg, n + 1)
                    wait(dve, s_hh, n - 1)
                    wait(dve, s_hl, n - 1)
                    dve.tensor_tensor(hf[0:w, i % 2, :], sg[0:w, i % 2, :], PS[0:w, 2 * (i % 2) + 1, :],
                                      ALU.mult).then_inc(s_hf, 1)

                def low(g, i):
                    w = HCH[i % 3]
                    e = i // 3
                    n = g * NU + i
                    wait(dve, s_hh, n + 1)
                    if i % 3 == 0:
                        wait(dve, s_y, g * E8 + (e - 1))
                    dve.tensor_tensor(hl[0:w, e % 2, i % 3, :], hf[0:w, i % 2, :], hh[0:w, e % 2, i % 3, :],
                                      ALU.subtract).then_inc(s_hl, 1)

                def add(g, n, e):
                    wait(dve, s_y, n + 1)
                    for t in range(4):
                        b = g * 4 + t
                        last = dve.scalar_tensor_tensor(C["xs"](b), PS[:, 4 + e % 2, t * P:(t + 1) * P],
                                                        gates[:, ds(b * E8 + e, 1)], C["xs"](b), ALU.mult, ALU.add)
                    dve.drain().then_inc(s_acc, 1)

                def body(g, end):
                    first = isinstance(g, int) and g == 0
                    for e in range(E8):
                        for k in range(3):
                            i = e * 3 + k
                            hidden(g, i)
                            if i > 0:
                                low(g, i - 1)
                            elif not first:
                                low(g - 1, NU - 1)
                        if e > 1:
                            add(g, g * E8 + (e - 2), e - 2)
                        elif not first:
                            add(g - 1, g * E8 + (e - 2), E8 + e - 2)
                        if e == 2 and not end:
                            prep(g + 1)
                        if e == 6 and not end:
                            split(g + 1)
                    if end:
                        low(g, NU - 1)
                        add(g, g * E8 + 6, 6)
                        add(g, g * E8 + 7, 7)
                prep(0)
                split(0)
                groups(dve, body)

            @block.scalar
            def _(act):
                def silu(g, i):
                    w = HCH[i % 3]
                    n = g * NU + i
                    wait(act, s_up, n + 1)
                    wait(act, s_hf, n - 1)
                    act.activation(sg[0:w, i % 2, :], PS[0:w, 2 * (i % 2), :], ACT.Silu).then_inc(s_sg, 1)

                def high(g, i):
                    w = HCH[i % 3]
                    e = i // 3
                    n = g * NU + i
                    wait(act, s_hf, n + 1)
                    if i % 3 == 0:
                        wait(act, s_y, g * E8 + (e - 1))
                    act.copy(hh[0:w, e % 2, i % 3, :], hf[0:w, i % 2, :]).then_inc(s_hh, 1)

                def body(g, end):
                    first = isinstance(g, int) and g == 0
                    for i in range(NU):
                        silu(g, i)
                        if i > 0:
                            high(g, i - 1)
                        elif not first:
                            high(g - 1, NU - 1)
                    if end:
                        high(g, NU - 1)
                groups(act, body)

            @block.sync
            def _(sp):
                o = out.rearrange("b p d -> p b d")

                def body(g, end):
                    wait(sp, s_acc, g * E8 + E8)
                    sp.dma_start(o[:, ds(g * 4, 4), :], C["X3"][:, ds(g * 4, 4), :]).then_inc(s_out, 16)
                groups(sp, body)
                sp.wait_ge(s_out, 16 * NTG)


def host_inputs(a):
    import numpy as np
    c = np.ascontiguousarray

    def bits(ones):
        return c((ones != 0).astype(np.uint16) * np.uint16(0x3F80))
    sel = np.zeros((128, 32, 128), np.float32)
    for r in range(32):
        for t in range(3):
            sel[32 * t + r, r, :] = 1.0
    io = {
        "x": c(a["x"]), "adj": c(a["adj"]),
        "gW": c(np.transpose(a["L0_gnn_W"], (1, 0, 2)).reshape(128, 128)),
        "g_as": c(a["L0_gnn_a_src"].reshape(128)), "g_ad": c(a["L0_gnn_a_dst"].reshape(128)),
        "beta": c(a["L0_gnn_beta_tilde"].reshape(1)), "gWoT": c(a["L0_gnn_W_out"].T),
        "c_id": np.eye(128, dtype=np.float32), "c_idb": bits(np.eye(128)),
        "c_sel": bits(sel.reshape(128, 32 * 128)),
    }
    hw, ho, ow = a["L0_ffn_hy_in_w"], a["L0_ffn_hy_out_w"], a["L0_ffn_out_w"]

    def chunked(wT):
        return c(wT.reshape(-1, 128, wT.shape[1]).transpose(1, 0, 2).reshape(128, -1))

    def conv(w):
        o = np.zeros((128, 6, w.shape[1]), w.dtype)
        o[:, 0:4] = w[0:512].reshape(4, 128, -1).transpose(1, 0, 2)
        o[0:64, 4:6] = w[512:640].reshape(2, 64, -1).transpose(1, 0, 2)
        return o.reshape(128, -1)
    m = np.arange(64)
    bfm = np.zeros((2, 8, 4, 4, 2, 64), np.float32)
    rm = np.zeros((8, 4, 8), np.float32)
    for h2 in range(2):
        for ch in range(4):
            bfm[h2, :, ch, ch, h2, :] = 1.0
    for b in range(8):
        rm[b, :, b] = 1.0
    lt = np.tile((m[:, None] < m[None, :]).astype(np.float32), (2, 1))
    ut = np.tile((m[:, None] > m[None, :]).astype(np.float32), (2, 1))
    io.update({
        "bWxR": c(a["L0_ffn_W_x"].reshape(8, 64, 128).transpose(1, 0, 2).reshape(64, 1024)),
        "bWsT": c(a["L0_ffn_W_slice"].T), "bbx": c(a["L0_ffn_b_x"].reshape(8, 64).T),
        "btemp": c(a["L0_ffn_temperature"].reshape(8)), "bbs": c(a["L0_ffn_b_slice"].reshape(1, 64)),
        "bob": c(a["L0_ffn_out_b"].reshape(1, 128)), "bWin": chunked(hw.T), "bWho": chunked(ho.T),
        "bWfx": c(a["L0_ffn_W_fx"].T), "bWo2": chunked(ow.T), "bfc": chunked(a["L0_ffn_hy_fcD_w"].T),
        "c_bfm": bits(bfm.reshape(64, 512)), "c_rm": rm.reshape(32, 8),
        "c_selh": bits(np.repeat(np.eye(8), 64, axis=1)),
        "c_lt": lt, "c_ut": ut, "c_uf": np.kron(np.eye(2, dtype=np.float32), ut[:64]),
        "c_ub": np.kron(np.eye(2, dtype=np.float32), lt[:64]),
        "bnw": c(a["L0_ffn_hy_norm_w"].reshape(4, 128).T), "bbfx": c(a["L0_ffn_b_fx"]),
        "bdtb": c(a["L0_ffn_hy_dt_bias"]), "bAl": c(a["L0_ffn_hy_A_log"]), "bD": c(a["L0_ffn_hy_D"]),
        "bcw": conv(a["L0_ffn_hy_conv_w"]), "bcb": conv(a["L0_ffn_hy_conv_b"].reshape(640, 1)),
    })
    io.update({"cW": c(a["L1_gnn_W"]), "ca": c(a["L1_gnn_a"].reshape(256))})
    w2 = np.zeros((8, 384, 128), np.float32)
    w2[:, 0:341] = a["L1_ffn_w2"].transpose(0, 2, 1)
    io.update({
        "drw": c(a["L1_ffn_router_w"].T), "c_r8": np.arange(8, 0, -1).astype(np.float32),
        "dw1": c(a["L1_ffn_w1"].reshape(2728, 128).T), "dw3": c(a["L1_ffn_w3"].reshape(2728, 128).T),
        "dw2": c(w2.reshape(8, 3, 128, 128).transpose(2, 0, 1, 3).reshape(128, 3072)),
    })
    return io


def kernel(**inputs):
    import numpy as _np
    import concourse.bacc as _bacc
    from concourse import mybir as _mybir
    from concourse.bass_utils import run_bass_kernel_spmd as _run

    nc = _bacc.Bacc("TRN2", target_bir_lowering=False, num_devices=1)
    arrays = {f"in_{k}": v for k, v in host_inputs({k: _np.asarray(v) for k, v in inputs.items()}).items()}
    io = {k[3:]: nc.dram_tensor(k, v.shape, _mybir.dt.from_np(v.dtype), kind="ExternalInput").ap()
          for k, v in arrays.items()}
    out = nc.dram_tensor("out_x", inputs["x"].shape, _mybir.dt.float32, kind="ExternalOutput").ap()
    build(nc, io, out)
    r = _run(nc, [arrays], core_ids=[0])
    return r.results[0]["out_x"]
```

```python
from contextlib import ExitStack

import concourse.bass as bass
from concourse import mybir

F32 = mybir.dt.float32
BF16 = mybir.dt.bfloat16
I32 = mybir.dt.int32
ALU = mybir.AluOpType
ACT = mybir.ActivationFunctionType
AX = mybir.AxisListType
ds = bass.ds

P = 128
H0, DH = 8, 16
HF, PF = 8, 64
G = 64
NS = 64
DI = HF * PF
CD = DI + 2 * NS
KC = DI // P
E8, HID = 8, 341
HCH = [128, 128, 85]
GB = 8


def wait(eng, sem, n):
    if isinstance(n, int) and n <= 0:
        return
    eng.wait_ge(sem, n)


def pipelined(eng, total, unroll, stages):
    last = max(lag for lag, _ in stages)
    head = min(total, unroll * -(-(last + 2) // unroll))
    for t in range(head):
        for lag, emit in stages:
            if 0 <= t - lag:
                emit(t - lag, (t - lag) % unroll)
    if total > head:
        with eng.Fori(head // unroll, total // unroll) as q:
            for r in range(unroll):
                for lag, emit in stages:
                    emit(q * unroll + (r - lag), (r - lag) % unroll)
    for t in range(total, total + last):
        for lag, emit in stages:
            if t - lag < total:
                emit(t - lag, (t - lag) % unroll)


def build(nc, io, out, stop=99, start=0):
    B = io["x"].shape[0]
    io = {k: v.bitcast(BF16) if v.dtype == mybir.dt.uint16 else v for k, v in io.items()}
    NQ = B // 4
    with ExitStack() as root:
        held = []

        def sem(name):
            held.append(nc.alloc_semaphore(name=name))
            return held[-1]

        def end_layer():
            nc.clear_and_free_semaphores(held)
            nc.all_engine_barrier()
            held.clear()

        def tile(ctx, name, shape, dt=F32):
            return ctx.enter_context(nc.sbuf_tensor("t_" + name, shape, dt))

        X = tile(root, "X", [P, B * P])
        X3 = X[:, :].rearrange("p (b d) -> p b d", d=P)
        ST = tile(root, "ST", [P, B * 6])
        MU = tile(root, "MU", [P, B])
        RS = tile(root, "RS", [P, B])
        LT6 = tile(root, "LT6", [P, 3 * B])
        IDF = tile(root, "IDF", [P, P])
        IDB = tile(root, "IDB", [P, P], BF16)
        PS = root.enter_context(nc.psum_tensor("PS", [P, 8, 512], F32))

        def bank(k, n=512, parts=P, col=0):
            return PS[0:parts, k, col:col + n]

        def xs(b):
            return X[:, ds(b * P, P)]

        s_const = sem("s_const")
        s_x = [sem(f"s_x{c}") for c in range(B // 8)]
        C = dict(nc=nc, io=io, sem=sem, tile=tile, X=X, X3=X3, ST=ST, MU=MU, RS=RS, LT6=LT6, IDF=IDF, IDB=IDB,
                 PS=PS, bank=bank, xs=xs, B=B, NQ=NQ)

        load_x(C, s_const, s_x)
        end_layer()
        if stop > 0 and start < 1:
            gnn0(C)
            end_layer()
        if stop > 1 and start < 2:
            ffn0(C)
            end_layer()
        if stop > 2 and start < 3:
            gnn1(C)
            end_layer()
        if stop > 3:
            moe(C, out)
        else:
            store_x(C, out)


def load_x(C, s_const, s_x):
    nc, io, X, B, sem = C["nc"], C["io"], C["X"], C["B"], C["sem"]
    CH = 8
    with nc.Block() as block:
        @block.sync
        def _(sp):
            sp.dma_start(C["IDF"][:, :], io["c_id"]).then_inc(s_const, 16)
            sp.dma_start(C["IDB"][:, :], io["c_idb"]).then_inc(s_const, 16)
            for c in range(B // CH):
                sp.dma_start(X[:, c * CH * P:(c + 1) * CH * P],
                             io["x"][c * CH:(c + 1) * CH].rearrange("b p d -> p b d")).then_inc(s_x[c], 16)
            sp.wait_ge(s_const, 32)

        @block.vector
        def _(dve):
            for c in range(B // CH):
                dve.wait_ge(s_x[c], 16)
                for b in range(c * CH, (c + 1) * CH):
                    dve.bn_stats(C["ST"][:, ds(b * 6, 6)], C["xs"](b))


def store_x(C, out):
    nc, X, B = C["nc"], C["X"], C["B"]
    s_out = C["sem"]("s_out")
    with nc.Block() as block:
        @block.sync
        def _(sp):
            for h in range(4):
                w = B // 4
                sp.dma_start(out[h * w:(h + 1) * w].rearrange("b p d -> p b d"),
                             C["X3"][:, h * w:(h + 1) * w]).then_inc(s_out, 16)
            sp.wait_ge(s_out, 64)


def ln_vector(C, dve, s_var, s_std):
    st = C["ST"][:, :].rearrange("p (b s) -> p b s", s=6)
    B = C["B"]
    dif, var, std = (C["LT6"][:, k * B:(k + 1) * B] for k in range(3))
    MU, RS = C["MU"][:, :], C["RS"][:, :]
    dve.drain()
    dve.tensor_tensor(MU, st[:, :, 1], st[:, :, 4], ALU.add)
    dve.tensor_tensor(dif, st[:, :, 1], st[:, :, 4], ALU.subtract)
    dve.tensor_tensor(var, st[:, :, 2], st[:, :, 5], ALU.add)
    dve.drain()
    dve.tensor_scalar(MU, MU, 0.5, None, ALU.mult)
    dve.tensor_tensor(dif, dif, dif, ALU.mult)
    dve.tensor_scalar(var, var, 1.0 / P, 1e-5, ALU.mult, ALU.add)
    dve.drain()
    dve.scalar_tensor_tensor(var, dif, 0.25, var, ALU.mult, ALU.add).then_inc(s_var, 1)
    dve.wait_ge(s_std, 1)
    dve.reciprocal(RS, std)
    dve.drain()


def ln_scalar(C, act, s_var, s_std):
    B = C["B"]
    act.wait_ge(s_var, 1)
    act.activation(C["LT6"][:, 2 * B:3 * B], C["LT6"][:, B:2 * B], ACT.Sqrt).then_inc(s_std, 1)


def normalise(C, dve, dst, b):
    return dve.tensor_scalar(dst, C["xs"](b), C["MU"][:, ds(b, 1)], C["RS"][:, ds(b, 1)], ALU.subtract, ALU.mult)


def project(C, tag, ctx, wcols, load, VS):
    nc, B, NQ, sem, tile, PS = C["nc"], C["B"], C["NQ"], C["sem"], C["tile"], C["PS"]
    W = tile(ctx, tag + "W", [P, wcols])
    xn = tile(ctx, tag + "xn", [P, 2, 4, P])
    xnT = tile(ctx, tag + "xnT", [P, 2, 4 * P])
    s_w, s_wz, s_var, s_std = (sem(tag + n) for n in ("w", "wz", "var", "std"))
    s_xn, s_tr, s_xnT, s_pr, s_vs = (sem(tag + n) for n in ("xn", "tr", "xnT", "pr", "vs"))
    with nc.Block() as block:
        load(block, W, s_w, s_wz)

        @block.vector
        def _(dve):
            load.vector(dve)
            ln_vector(C, dve, s_var, s_std)

            def norm(q, r):
                wait(dve, s_tr, q - 1)
                for j in range(4):
                    last = normalise(C, dve, xn[:, r % 2, j, :], q * 4 + j)
                last.then_inc(s_xn, 1)
            pipelined(dve, NQ, 2, [(0, norm)])

        @block.scalar
        def _(act):
            ln_scalar(C, act, s_var, s_std)

            def evac_t(q, r):
                act.wait_ge(s_tr, q + 1)
                wait(act, s_pr, q - 1)
                act.copy(xnT[:, r % 2, :], PS[:, r % 2, :]).then_inc(s_xnT, 1)

            def evac_p(q, r):
                act.wait_ge(s_pr, q + 1)
                act.copy(VS[:, ds(q * 4 * wcols, 4 * wcols)].rearrange("p (k n) -> p k n", k=2),
                         PS[:, 2 + 2 * (r % 2):4 + 2 * (r % 2), 0:2 * wcols]).then_inc(s_vs, 1)
            pipelined(act, NQ, 2, [(0, evac_t), (1, evac_p)])

        @block.tensor
        def _(pe):
            def trans(q, r):
                pe.wait_ge(s_xn, q + 1)
                wait(pe, s_xnT, q - 1)
                for j in range(4):
                    last = pe.transpose(PS[:, r % 2, j * P:(j + 1) * P], xn[:, r % 2, j, :], C["IDF"][:, :])
                last.then_inc(s_tr, 1)

            def prod(q, r):
                pe.wait_ge(s_xnT, q + 1)
                wait(pe, s_vs, q - 1)
                for j in range(4):
                    o = PS[:, 2 + 2 * (r % 2) + j // 2, (j % 2) * wcols:(j % 2 + 1) * wcols]
                    last = pe.matmul(o, xnT[:, r % 2, j * P:(j + 1) * P], W[:, :], start=True, stop=True)
                last.then_inc(s_pr, 1)
            pe.wait_ge(s_w, load.count)
            wait(pe, s_wz, load.zcount)
            pipelined(pe, NQ, 2, [(0, trans), (1, prod)])


def factors(C, tag, ctx, S, Dd, NH, cf, bf, KT):
    nc, B, NQ, sem, tile, PS = C["nc"], C["B"], C["NQ"], C["sem"], C["tile"], C["PS"]
    n = B * NH
    nch = -(-n // P)
    w = min(n, P)
    dc = tile(ctx, tag + "dc", [P, n])
    dmax = tile(ctx, tag + "dmax", [P, nch])
    diag = tile(ctx, tag + "diag", [P, nch * w])
    z = tile(ctx, tag + "z", [P, n])
    Kf = tile(ctx, tag + "Kf", [P, n])
    Kp = tile(ctx, tag + "Kp", [P, NQ * 128], BF16)
    ones = tile(ctx, tag + "ones", [P, P])
    KpV = Kp[:, :].rearrange("p (q t r) -> p q t r", t=4, r=32)
    s_c, s_t, s_m, s_bc, s_e, s_k, s_kp, s_kt = (sem(tag + x) for x in
                                               ("fc", "ft", "fm", "fbc", "fe", "fk", "fkp", "fkt"))
    psb = PS[:, 4:8, :].rearrange("p k n -> p (k n)").bitcast(BF16)
    with nc.Block() as block:
        @block.vector
        def _(dve):
            dve.memset(ones[:, :], 1.0)
            dve.memset(Kp[:, :], 0.0)
            dve.tensor_copy(dc[:, :].rearrange("p (b h) -> p b h", h=NH), Dd).then_inc(s_c, 1)
            dve.wait_ge(s_t, 1)
            for c in range(nch):
                dve.tensor_reduce(dmax[0:w, c:c + 1], PS[0:w, 0, c * P:(c + 1) * P], AX.X, ALU.max)
            dve.drain()
            for c in range(nch):
                dve.tensor_scalar(diag[0:w, c * w:(c + 1) * w], C["IDF"][0:w, 0:w], dmax[0:w, c:c + 1], None, ALU.mult)
            dve.drain().then_inc(s_m, 1)
            dve.wait_ge(s_bc, 1)
            zv = z[:, :].rearrange("p (b h) -> p b h", h=NH)
            Dv = PS[:, 1, 0:n].rearrange("p (b h) -> p b h", h=NH)
            dve.tensor_tensor(dc[:, :], dc[:, :], PS[:, 1, 0:n], ALU.subtract)
            dve.tensor_tensor(zv, S, Dv, ALU.add)
            dve.drain()
            dve.tensor_scalar(z[:, :], z[:, :], -0.8, 0.0, ALU.mult, ALU.min)
            dve.drain().then_inc(s_e, 1)
            dve.wait_ge(s_k, 1)
            kk = Kf[:, :].rearrange("p (q r) -> p q r", q=NQ)
            wq = n // NQ
            dve.tensor_copy(KpV[:, :, 0, 0:wq], kk)
            dve.drain()
            dve.tensor_tensor(kk, kk, KpV[:, :, 0, 0:wq], ALU.subtract)
            dve.drain()
            dve.tensor_copy(KpV[:, :, 1, 0:wq], kk)
            dve.drain()
            dve.tensor_tensor(kk, kk, KpV[:, :, 1, 0:wq], ALU.subtract)
            dve.drain()
            dve.tensor_copy(KpV[:, :, 2, 0:wq], kk)
            dve.drain().then_inc(s_kp, 1)
            dve.wait_ge(s_kt, 1)
            dve.tensor_copy(KT[:, :], psb[:, 0:NQ * P])

        @block.scalar
        def _(act):
            act.wait_ge(s_e, 1)
            act.activation(cf, dc[:, :], ACT.Exp, scale=0.8)
            act.activation(bf, dc[:, :], ACT.Exp, scale=0.2)
            act.activation(Kf[:, :], z[:, :], ACT.Exp).then_inc(s_k, 1)

        @block.tensor
        def _(pe):
            pe.wait_ge(s_c, 1)
            for c in range(nch):
                last = pe.transpose(PS[0:w, 0, c * P:(c + 1) * P], dc[:, c * w:(c + 1) * w], C["IDF"][:, :])
            last.then_inc(s_t, 1)
            pe.wait_ge(s_m, 1)
            for c in range(nch):
                last = pe.matmul(PS[:, 1, c * w:(c + 1) * w], ones[0:w, :], diag[0:w, c * w:(c + 1) * w],
                                 start=True, stop=True)
            last.then_inc(s_bc, 1)
            pe.wait_ge(s_kp, 1)
            for q in range(NQ):
                last = pe.transpose(psb[:, q * P:(q + 1) * P], Kp[:, q * P:(q + 1) * P], C["IDB"][:, :])
            last.then_inc(s_kt, 1)


def gnn0(C):
    nc, io, B, NQ, sem, tile, PS = C["nc"], C["io"], C["B"], C["NQ"], C["sem"], C["tile"], C["PS"]
    IDF = C["IDF"]
    WC = P + 2 * H0
    with ExitStack() as ctx:
        VS = tile(ctx, "a_VS", [P, B * WC])
        V3 = VS[:, :].rearrange("p (b w) -> p b w", w=WC)
        cf = tile(ctx, "a_cf", [P, B * H0])
        bf = tile(ctx, "a_bf", [P, B * H0])
        KT = tile(ctx, "a_KT", [P, NQ * P], BF16)
        sel = tile(ctx, "a_sel", [P, 32 * P], BF16)
        MT = tile(ctx, "a_MT", [P, P])
        WoT = tile(ctx, "a_WoT", [P, P])
        adj = tile(ctx, "a_adj", [P, P], I32)
        mf = tile(ctx, "a_mf", [P, P])
        lb = tile(ctx, "a_lb", [P, P])
        msk = tile(ctx, "a_msk", [P, P])
        beta = tile(ctx, "a_beta", [P, 4])
        av = tile(ctx, "a_av", [P, 2 * P])
        tmp = tile(ctx, "a_tmp", [P, P])
        s_wd, s_w2, s_m1, s_m2, s_m3, s_mt, s_mc = (sem("a_" + x) for x in
                                                  ("wd", "w2", "m1", "m2", "m3", "mt", "mc"))

        class Load:
            count, zcount = 16, 1

            def __call__(self, block, W, s_w, s_wz):
                self.W, self.s_w, self.s_wz = W, s_w, s_wz

                @block.sync
                def _(sp):
                    sp.dma_start(W[:, 0:P], io["gW"]).then_inc(s_w, 16)
                    sp.dma_start(av[:, 0:P], io["g_as"].partition_broadcast(P)).then_inc(s_wd, 16)
                    sp.dma_start(av[:, P:2 * P], io["g_ad"].partition_broadcast(P)).then_inc(s_wd, 16)
                    sp.dma_start(adj[:, :], io["adj"]).then_inc(s_w2, 16)
                    sp.dma_start(beta[:, 0:1], io["beta"].partition_broadcast(P)).then_inc(s_w2, 16)
                    sp.dma_start(WoT[:, :], io["gWoT"]).then_inc(s_w2, 16)
                    sp.dma_start(sel[:, :], io["c_sel"]).then_inc(s_w2, 16)
                    sp.wait_ge(s_w2, 64)

            def vector(self, dve):
                dve.wait_ge(self.s_w, 16)
                dve.wait_ge(s_wd, 32)
                for k in range(2):
                    dve.tensor_tensor(tmp[:, :], self.W[:, 0:P], av[:, k * P:(k + 1) * P], ALU.mult)
                    dve.drain()
                    dve.tensor_reduce(self.W[:, P + k * H0:P + (k + 1) * H0],
                                      tmp[:, :].rearrange("p (h f) -> p h f", f=DH), AX.X, ALU.add)
                    dve.drain()
                dve.sem_inc(self.s_wz, 1)

        project(C, "a_", ctx, WC, Load(), VS)

        with nc.Block() as block:
            @block.vector
            def _(dve):
                dve.tensor_copy(mf[:, :], adj[:, :])
                dve.drain()
                dve.tensor_scalar(msk[:, :], mf[:, :], 0.0, None, ALU.is_gt)
                dve.tensor_scalar(mf[:, :], mf[:, :], 0.0, 1e-6, ALU.max, ALU.add)
                dve.scalar_tensor_tensor(beta[:, 1:2], beta[:, 0:1], -1.0, beta[:, 0:1], ALU.mult, ALU.max)
                dve.drain().then_inc(s_m1, 1)
                dve.wait_ge(s_m2, 1)
                dve.scalar_tensor_tensor(beta[:, 3:4], beta[:, 0:1], 0.0, beta[:, 2:3], ALU.max, ALU.add)
                dve.drain()
                dve.tensor_scalar(lb[:, :], lb[:, :], beta[:, 3:4], None, ALU.mult)
                dve.drain()
                dve.tensor_reduce(beta[:, 1:2], lb[:, :], AX.X, ALU.max, negate=True)
                dve.drain().then_inc(s_m1, 1)
                dve.wait_ge(s_m2, 2)
                dve.tensor_tensor(lb[:, :], lb[:, :], msk[:, :], ALU.mult).then_inc(s_m3, 1)
                dve.wait_ge(s_mt, 1)
                dve.tensor_copy(MT[:, :], PS[:, 0, 0:P])

            @block.scalar
            def _(act):
                act.wait_ge(s_m1, 1)
                act.activation(beta[:, 2:3], beta[:, 1:2], ACT.Exp, scale=-1.0)
                act.drain()
                act.activation(beta[:, 2:3], beta[:, 2:3], ACT.Ln, bias=1.0)
                act.activation(lb[:, :], mf[:, :], ACT.Ln).then_inc(s_m2, 1)
                act.wait_ge(s_m1, 2)
                act.activation(lb[:, :], lb[:, :], ACT.Exp, bias=beta[:, 1:2]).then_inc(s_m2, 1)

            @block.tensor
            def _(pe):
                pe.wait_ge(s_m3, 1)
                pe.transpose(PS[:, 0, 0:P], lb[:, :], IDF[:, :]).then_inc(s_mt, 1)

        with ExitStack() as c2:
            factors(C, "a_", c2, V3[:, :, P:P + H0], V3[:, :, P + H0:P + 2 * H0], H0, cf[:, :], bf[:, :], KT)

        with ExitStack() as c2:
            W32 = 32
            VX = tile(c2, "a_VX", [P, 2, H0 * W32])
            PT = tile(c2, "a_PT", [P, 2, H0 * P])
            AV = tile(c2, "a_AV", [P, 2, 2 * P])
            rec = tile(c2, "a_rec", [P, 2, H0])
            hn = tile(c2, "a_hn", [P, 2, P])
            hnT = tile(c2, "a_hnT", [P, 2, P])
            s_z, s_vx, s_K, s_pt, s_av, s_ac, s_bk, s_hn, s_ht, s_hc, s_y, s_res = (
                sem("a2_" + x) for x in ("z", "vx", "K", "pt", "av", "ac", "bk", "hn", "ht", "hc", "y", "res"))
            with nc.Block() as block:
                @block.gpsimd
                def _(pool):
                    pool.memset(VX[:, :, :], 0.0)
                    pool.drain()

                    def values(b, r):
                        wait(pool, s_av, b - 1)
                        vx = VX[:, r % 2, :].rearrange("p (h w) -> p h w", w=W32)
                        bb = bf[:, ds(b * H0, H0)]
                        pool.tensor_tensor(vx[:, :, 0:DH],
                                           VS[:, ds(b * WC, P)].rearrange("p (h f) -> p h f", f=DH),
                                           bb.unsqueeze(2).broadcast_to([P, H0, DH]), ALU.mult)
                        pool.tensor_copy(vx[:, :, DH], bb)
                        pool.drain().then_inc(s_vx, 1)
                    pipelined(pool, B, 2, [(0, values)])

                @block.tensor
                def _(pe):
                    def spread(b, r):
                        wait(pe, s_pt, b - 1)
                        col = (b - r) * (P // 4)
                        for h in range(H0):
                            o = PS[:, 2 * (r % 2) + h // 4, (h % 4) * P:(h % 4 + 1) * P]
                            k = (r * H0 + h) * P
                            last = pe.matmul(o, sel[0:96, k:k + P], KT[0:96, ds(col, P)], start=True, stop=True)
                        last.then_inc(s_K, 1)

                    def attend(b, r):
                        pe.wait_ge(s_pt, b + 1)
                        pe.wait_ge(s_vx, b + 1)
                        wait(pe, s_ac, b)
                        for h in range(H0):
                            q = 32 * (h % 4)
                            last = pe.matmul(PS[q:q + 32, 4, (h // 4) * P:(h // 4 + 1) * P],
                                             VX[:, r % 2, h * W32:(h + 1) * W32], PT[:, r % 2, h * P:(h + 1) * P],
                                             start=True, stop=True, tile_position=(0, q))
                        last.then_inc(s_av, 1)

                    def turn(b, r):
                        pe.wait_ge(s_ac, b + 1)
                        wait(pe, s_hn, b)
                        for k in range(2):
                            last = pe.transpose(PS[:, 5, k * P:(k + 1) * P], AV[:, r % 2, k * P:(k + 1) * P], IDF[:, :])
                        last.then_inc(s_bk, 1)

                    def trans(b, r):
                        pe.wait_ge(s_hn, b + 1)
                        wait(pe, s_hc, b)
                        pe.transpose(PS[:, 6, 0:P], hn[:, r % 2, :], IDF[:, :]).then_inc(s_ht, 1)

                    def mix(b, r):
                        pe.wait_ge(s_hc, b + 1)
                        wait(pe, s_res, b)
                        pe.matmul(PS[:, 7, 0:P], hnT[:, r % 2, :], WoT[:, :], start=True, stop=True).then_inc(s_y, 1)
                    pipelined(pe, B, 4, [(0, spread), (1, attend), (2, turn), (3, trans), (4, mix)])

                @block.vector
                def _(dve):
                    def weights(b, r):
                        dve.wait_ge(s_K, b + 1)
                        wait(dve, s_av, b - 1)
                        for h in range(H0):
                            last = dve.scalar_tensor_tensor(
                                PT[:, r % 2, h * P:(h + 1) * P],
                                PS[:, 2 * (r % 2) + h // 4, (h % 4) * P:(h % 4 + 1) * P],
                                cf[:, ds(b * H0 + h, 1)], MT[:, :], ALU.max, ALU.mult)
                        last.then_inc(s_pt, 1)

                    def norm(b, r):
                        dve.wait_ge(s_bk, b + 1)
                        wait(dve, s_ht, b - 1)
                        o = PS[:, 5, 0:H0 * W32].rearrange("p (h w) -> p h w", w=W32)
                        dve.reciprocal(rec[:, r % 2, :], o[:, :, DH])
                        dve.drain()
                        dve.tensor_tensor(hn[:, r % 2, :].rearrange("p (h f) -> p h f", f=DH), o[:, :, 0:DH],
                                          rec[:, r % 2, :].unsqueeze(2).broadcast_to([P, H0, DH]),
                                          ALU.mult).then_inc(s_hn, 1)

                    def residual(b, r):
                        dve.wait_ge(s_y, b + 1)
                        dve.tensor_tensor(C["xs"](b), PS[:, 7, 0:P], C["xs"](b), ALU.add).then_inc(s_res, 1)
                        dve.drain()
                        dve.bn_stats(C["ST"][:, ds(b * 6, 6)], C["xs"](b))
                    pipelined(dve, B, 4, [(0, weights), (2, norm), (4, residual)])

                @block.scalar
                def _(act):
                    def copy_a(b, r):
                        act.wait_ge(s_av, b + 1)
                        wait(act, s_bk, b - 1)
                        act.copy(AV[:, r % 2, :], PS[:, 4, 0:2 * P]).then_inc(s_ac, 1)

                    def copy_t(b, r):
                        act.wait_ge(s_ht, b + 1)
                        wait(act, s_y, b - 1)
                        act.copy(hnT[:, r % 2, :], PS[:, 6, 0:P]).then_inc(s_hc, 1)
                    pipelined(act, B, 4, [(1, copy_a), (3, copy_t)])


def ffn0(C):
    nc, io, B, sem, tile, PS = C["nc"], C["io"], C["B"], C["sem"], C["tile"], C["PS"]
    IDF, IDB = C["IDF"], C["IDB"]
    NG = B // GB
    NW2 = 21
    NT = GB // 2
    N = GB * G
    with ExitStack() as ctx:
        def T(name, shape, dt=F32):
            return tile(ctx, "b_" + name, shape, dt)
        WXS = T("WXS", [P, DI])
        WfxT = T("WfxT", [P, DI])
        WI = 1168
        winh = T("winh", [P, KC, WI], BF16)
        winl = T("winl", [P, KC, WI], BF16)
        whoh = T("whoh", [P, KC, DI], BF16)
        whol = T("whol", [P, KC, DI], BF16)
        WoT2 = T("WoT2", [P, KC * P])
        fcT = T("fcT", [P, KC * 8])
        BFX = T("BFX", [64, KC * P])
        BFM = T("BFM", [64, KC * P], BF16)
        Rm = T("Rm", [32, 8])
        LBP = T("LBP", [96, DI], BF16)
        OBP = T("OBP", [96, P], BF16)
        ONB = T("ONB", [96, P], BF16)
        SELH = T("SELH", [8, DI], BF16)
        ON1 = T("ON1", [P, 1])
        LTM = T("LTM", [P, G])
        UTM = T("UTM", [P, G])
        UF = T("UF", [P, P])
        UB = T("UB", [P, P])
        cw = T("cw", [P, 5 * 3])
        cb = T("cb", [P, 5])
        nA = T("nA", [P, 16])
        dtb = T("dtb", [P, 16])
        Dp = T("Dp", [P, 8])
        nw = T("nw", [P, KC])
        rt = T("rt", [P, 8])
        s_w, s_w2 = sem("b_w"), sem("b_w2")
        s_p0, s_p1, s_p2, s_var, s_std = (sem("b_" + x) for x in ("p0", "p1", "p2", "var", "std"))

        with ExitStack() as c2, nc.Block() as block:
            WinT = tile(c2, "b_WinT", [P, KC * WI])
            WhoT = tile(c2, "b_WhoT", [P, KC * DI])
            Win = WinT[:, :].rearrange("p (k n) -> p k n", k=KC)
            Who = WhoT[:, :].rearrange("p (k n) -> p k n", k=KC)
            WxR = tile(c2, "b_WxR", [64, 8 * P])
            WsT = tile(c2, "b_WsT", [64, G])
            bxc = tile(c2, "b_bxc", [64, 8])
            row = tile(c2, "b_row", [1, DI])
            rob = tile(c2, "b_rob", [1, DI], BF16)
            bsl = tile(c2, "b_bsl", [1, G])
            obr = tile(c2, "b_obr", [1, P])

            @block.sync
            def _(sp):
                n = [0]

                def ld(dst, src, s=s_w2):
                    sp.dma_start(dst, src).then_inc(s, 16)
                    n[0] += 1
                for dst, key in ((WxR, "bWxR"), (WsT, "bWsT"), (bxc, "bbx")):
                    ld(dst[:, :], io[key], s_w)
                ld(rt[:, :], io["btemp"].partition_broadcast(P), s_w)
                ld(bsl[:, :], io["bbs"], s_w)
                ld(obr[:, :], io["bob"], s_w)
                for dst, key in ((WinT, "bWin"), (WhoT, "bWho"), (WfxT, "bWfx"), (WoT2, "bWo2"), (fcT, "bfc"),
                                 (BFM, "c_bfm"), (Rm, "c_rm"), (SELH, "c_selh"), (LTM, "c_lt"), (UTM, "c_ut"),
                                 (UF, "c_uf"), (UB, "c_ub"), (nw, "bnw")):
                    ld(dst[:, :], io[key])
                ld(BFX[:, :], io["bbfx"].partition_broadcast(64))
                for c in range(2):
                    ld(dtb[:, 8 * c:8 * c + 8], io["bdtb"].partition_broadcast(P))
                    ld(nA[:, 8 * c:8 * c + 8], io["bAl"].partition_broadcast(P))
                ld(Dp[:, :], io["bD"].partition_broadcast(P))
                ld(cw[:, :], io["bcw"])
                ld(cb[:, :], io["bcb"])
                assert n[0] - 6 == NW2
                sp.wait_ge(s_w2, 16 * (n[0] - 6))

            @block.tensor
            def _(pe):
                pe.wait_ge(s_w, 96)
                for h in range(HF):
                    pe.matmul(PS[:, 0, h * G:(h + 1) * G], WxR[:, h * P:(h + 1) * P], WsT[:, :], start=True, stop=True)
                for h in range(HF):
                    last = pe.matmul(PS[0:1, 1, h * G:(h + 1) * G], bxc[:, h:h + 1], WsT[:, :], start=True, stop=True)
                last.then_inc(s_p0, 1)

            @block.vector
            def _(dve):
                dve.memset(LBP[:, :], 0.0)
                dve.memset(OBP[:, :], 0.0)
                dve.memset(ONB[:, :], 1.0)
                dve.memset(ON1[:, :], 1.0)
                dve.wait_ge(s_w, 96)
                dve.tensor_scalar(rt[:, :], rt[:, :], 1e-6, None, ALU.max)
                dve.drain()
                dve.reciprocal(rt[:, :], rt[:, :])
                dve.wait_ge(s_p0, 1)
                dve.drain()

                def by_head(ap, parts):
                    return ap.unsqueeze(2).broadcast_to([parts, HF, G])
                dve.tensor_tensor(WXS[:, :].rearrange("p (h g) -> p h g", g=G),
                                  PS[:, 0, :].rearrange("p (h g) -> p h g", g=G), by_head(rt[:, :], P), ALU.mult)
                r3 = row[:, :].rearrange("p (h g) -> p h g", g=G)
                dve.tensor_tensor(r3, PS[0:1, 1, :].rearrange("p (h g) -> p h g", g=G),
                                  bsl[:, :].unsqueeze(1).broadcast_to([1, HF, G]), ALU.add)
                dve.drain()
                dve.tensor_tensor(r3, r3, by_head(rt[0:1, :], 1), ALU.mult)
                dve.drain()
                for src, w, dst in ((row, DI, LBP), (obr, P, OBP)):
                    for k in range(3):
                        dve.tensor_copy(rob[:, 0:w], src[:, 0:w])
                        dve.drain()
                        dve.tensor_copy(dst[32 * k:32 * k + 1, 0:w], rob[:, 0:w])
                        dve.tensor_tensor(src[:, 0:w], src[:, 0:w], rob[:, 0:w], ALU.subtract)
                        dve.drain()
                dve.wait_ge(s_w2, 16 * NW2)
                dve.tensor_tensor(BFX[:, :], BFX[:, :], BFM[:, :], ALU.mult)
                dve.tensor_scalar(Win[:, :, 0:DI], Win[:, :, 0:DI], 0.5, None, ALU.mult)
                for k in range(KC):
                    dve.tensor_scalar(Who[:, k, :], Who[:, k, :], nw[:, k:k + 1], None, ALU.mult)
                dve.tensor_scalar(cw[:, :], cw[:, :], 0.5, None, ALU.mult)
                dve.tensor_scalar(cb[:, :], cb[:, :], 0.5, None, ALU.mult)
                dve.drain()
                for f, hi, lo in ((Win, winh, winl), (Who, whoh, whol)):
                    dve.tensor_copy(hi[:, :, :], f)
                    dve.drain()
                    dve.tensor_tensor(lo[:, :, :], f, hi[:, :, :], ALU.subtract)
                dve.wait_ge(s_p1, 1)
                dve.tensor_scalar(nA[:, :], nA[:, :], -1.0, None, ALU.mult)
                ln_vector(C, dve, s_var, s_std)

            @block.scalar
            def _(act):
                act.wait_ge(s_w2, 16 * NW2)
                act.activation(nA[:, :], nA[:, :], ACT.Exp).then_inc(s_p1, 1)
                ln_scalar(C, act, s_var, s_std)

        xn = T("xn", [P, 2, P + 1])
        xnT = T("xnT", [P, P])
        nm = T("nm", [P, HF], BF16)
        mT = T("mT", [8, P], BF16)
        E = T("E", [P, DI])
        Z = T("Z", [P, HF])
        rZ = T("rZ", [P, HF])
        sw = T("sw", [P, 2, DI])
        swT = T("swT", [P, 2, GB, DI])
        rs = T("rs", [P, 4])
        sn = T("sn", [P, 4])
        RT = T("RT", [P, GB * KC])
        Tn = T("Tn", [P, DI])
        TT = T("TT", [P, GB, DI])
        R = T("R", [64, N])
        sth = T("sth", [P, KC, N], BF16)
        stl = T("stl", [P, KC, N], BF16)
        zs = T("zs", [P, KC, N])
        cx = T("cx", [P, KC, N])
        cB = T("cB", [64, 2, N])
        tn = T("tn", [P, 2, N])
        dv = T("dv", [P, 3, NT * 16])
        dtA = T("dtA", [P, NT * 16])
        xd = T("xd", [P, NT * 8])
        Rf = T("Rf", [P, 2, N])
        Dec = T("Dec", [P, N])
        CBl = T("CBl", [P, NT, G])
        CBu = T("CBu", [P, NT, G])
        Wl = T("Wl", [P, N])
        Wu = T("Wu", [P, N])
        XX = T("XX", [P, 3, N])
        R8 = T("R8", [P, GB])
        UU = T("UU", [P, 2, DI])
        ygh, ygl, sq, otT = sth, stl, cx, cx

        (s_xn, s_tr, s_xnT, s_lg, s_nm, s_mt, s_mT, s_lm, s_E, s_sw, s_T, s_swt, s_swT, s_Tn, s_Tt, s_TT, s_rt, s_R,
         s_st, s_sth, s_stl, s_z, s_tz, s_zs, s_u, s_c0, s_c1, s_tc, s_cx, s_dt, s_v, s_sp, s_dv, s_Rf, s_seg, s_Dec,
         s_cb, s_CB, s_W, s_Wp, s_xt, s_xd, s_xdv, s_XX, s_Y, s_yg, s_ygh, s_ygl, s_sq, s_ss, s_ms, s_sd, s_R8, s_ot,
         s_otT, s_U, s_UU, s_UV, s_o, s_X, s_null) = (sem("b2_" + x) for x in
                      ("xn tr xnT lg nm mt mT lm E sw T swt swT Tn Tt TT rt R st sth stl z tz zs u c0 c1 tc cx dt v sp "
                       "dv Rf seg Dec cb CB W Wp xt xd xdv XX Y yg ygh ygl sq ss ms sd R8 ot otT U UU UV o X null").split())

        POINTS = 4 * GB + 4

        def groups(eng, front, back):
            for k in range(POINTS):
                front(0, k, 0)
            if NG == 1:
                back(0, 0, False)
                return
            back(0, 0, True)
            mid = NG - 2
            if mid >= 2:
                with eng.Fori(0, mid // 2) as q:
                    back(q * 2 + 1, 1, True)
                    back(q * 2 + 2, 0, True)
            if mid % 2:
                back(NG - 2, (NG - 2) % 2, True)
            back(NG - 1, (NG - 1) % 2, False)

        def pair_cols(a, t):
            return a[:, :, t * P:(t + 1) * P]

        with nc.Block() as block:
            @block.tensor
            def _(pe):
                def front(g, k, par):
                    j, p = k // 4, k % 4
                    b = g * GB + j
                    if p == 0 and j < GB:
                        pe.wait_ge(s_xn, b + 1)
                        wait(pe, s_mT, b)
                        pe.transpose(PS[:, 4, 0:P], xn[:, j % 2, 0:P], IDF[:, :]).then_inc(s_tr, 1)
                    if p == 1:
                        if j < GB:
                            pe.wait_ge(s_xnT, b + 1)
                            wait(pe, s_E, b)
                            pe.matmul(PS[:, 5, :], xnT[:, :], WXS[:, :], start=True, stop=False)
                            pe.matmul(PS[:, 5, :], ONB[:, :], LBP[:, :], start=False, stop=True).then_inc(s_lg, 1)
                        if j >= 1:
                            wait(pe, s_sw, b)
                            wait(pe, s_Tn, b - 1)
                            wait(pe, s_TT, b - 1)
                            for c in range(KC):
                                o = PS[:, 6, c * 129:(c + 1) * 129] if c < 3 else PS[:, 4, 256:256 + 129]
                                last = pe.matmul(o, sw[:, (j - 1) % 2, c * P:(c + 1) * P], xn[:, (j - 1) % 2, :],
                                                 start=True, stop=True)
                            last.then_inc(s_T, 1)
                            for c in range(KC):
                                last = pe.transpose(PS[:, 7, c * P:(c + 1) * P], sw[:, (j - 1) % 2, c * P:(c + 1) * P],
                                                    IDF[:, :])
                            last.then_inc(s_swt, 1)
                    if p == 2 and j < GB:
                        pe.wait_ge(s_nm, b + 1)
                        wait(pe, s_Tn, b)
                        pe.transpose(PS[0:8, 4, 0:P // 2].bitcast(BF16), nm[:, :], IDB[:, :]).then_inc(s_mt, 1)
                    if p == 3:
                        if j < GB:
                            pe.wait_ge(s_mT, b + 1)
                            pe.matmul(PS[:, 5, :], mT[:, :], SELH[:, :], start=False, stop=True,
                                      skip_group_check=True).then_inc(s_lm, 1)
                        if j >= 1:
                            wait(pe, s_Tn, b)
                            wait(pe, s_swT, b)
                            for c in range(KC):
                                last = pe.transpose(PS[:, 7, c * P:(c + 1) * P], Tn[:, c * P:(c + 1) * P], IDF[:, :])
                            last.then_inc(s_Tt, 1)

                def back(g, par, more):
                    pts = [0]

                    def point():
                        if more and pts[0] < POINTS:
                            front(g + 1, pts[0], 1 - par)
                        pts[0] += 1

                    def split3(o, wh_, wl_, xh_, xl_, s, n=KC):
                        for k in range(n):
                            pe.matmul(o, wh_(k), xh_(k), start=(k == 0), stop=False)
                            pe.matmul(o, wh_(k), xl_(k), start=False, stop=False)
                            last = pe.matmul(o, wl_(k), xh_(k), start=False, stop=(k == n - 1))
                        if s is not None:
                            last.then_inc(s, 1)
                        return last

                    wait(pe, s_X, g * GB)
                    pe.sem_inc(s_null, 1)
                    pe.transpose(PS[0:32, 2, 0:64], RT[0:64, :], IDF[0:64, 0:64])
                    pe.transpose(PS[0:32, 3, 0:64], RT[64:128, :], IDF[64:128, 64:128]).then_inc(s_rt, 1)
                    wait(pe, s_TT, g * GB + GB)
                    wait(pe, s_UU, g * GB)
                    wait(pe, s_UV, g * GB)

                    def tokens(c):
                        for h2 in range(2):
                            h = 2 * c + h2
                            pe.matmul(PS[64 * h2:64 * h2 + 64, c, :], WfxT[:, h * 64:h * 64 + 64],
                                      TT[:, :, h * G:(h + 1) * G], start=True, stop=False)

                    def bias(c):
                        pe.matmul(PS[:, c, :], BFX[:, c * P:(c + 1) * P], R[:, :], start=False,
                                  stop=True).then_inc(s_st, 1)
                    tokens(0)
                    tokens(1)
                    pe.wait_ge(s_R, g + 1)
                    bias(0)
                    bias(1)
                    point()
                    for c in (2, 3):
                        tokens(c)
                        bias(c)
                    point()
                    for m in range(9):
                        if m < 4:
                            pe.wait_ge(s_stl, g * 4 + 4)
                        elif m < 8:
                            wait(pe, s_zs, g * 4 + m - 3)
                        else:
                            pe.wait_ge(s_c1, g * 5 + 1)
                        split3(PS[:, m % 4, :], lambda k: winh[:, k, m * P:(m + 1) * P],
                               lambda k: winl[:, k, m * P:(m + 1) * P], lambda k: sth[:, k, :],
                               lambda k: stl[:, k, :], s_z if m < 4 else s_u)
                        point()
                    pe.wait_ge(s_c1, g * 5 + 2)
                    for t in range(NT):
                        q = slice(t * P, (t + 1) * P)
                        last = split3(PS[:, 1, t * 16:(t + 1) * 16], lambda k: sth[:, k, q], lambda k: stl[:, k, q],
                                      lambda k: winh[:, k, 1152:1168], lambda k: winl[:, k, 1152:1168], None)
                    last.then_inc(s_dt, 1)
                    pe.wait_ge(s_cx, g * 5 + 4)
                    for t in range(NT):
                        for k in range(KC):
                            last = pe.matmul(PS[:, 2, t * 8:(t + 1) * 8], cx[:, k, t * P:(t + 1) * P],
                                             fcT[:, k * 8:(k + 1) * 8], start=(k == 0), stop=(k == KC - 1))
                    last.then_inc(s_xd, 1)
                    point()
                    pe.wait_ge(s_cx, g * 5 + 5)
                    pe.sem_inc(s_null, 1)
                    for j in range(GB):
                        last = pe.matmul(PS[64 * (j % 2):64 * (j % 2) + 64, 3, (j // 2) * G:(j // 2 + 1) * G],
                                         cB[:, 0, j * G:(j + 1) * G], cB[:, 1, j * G:(j + 1) * G], start=True, stop=True)
                    last.then_inc(s_cb, 1)
                    point()
                    for t in range(NT):
                        n = g * NT + t
                        pe.wait_ge(s_Rf, n + 1)
                        wait(pe, s_Dec, n)
                        pe.matmul(PS[:, 0, :], UF[:, :], Rf[:, 0, :], start=True, stop=False)
                        pe.matmul(PS[:, 0, :], UB[:, :], Rf[:, 1, :], start=False, stop=True).then_inc(s_seg, 1)
                        wait(pe, s_XX, n)
                        pe.wait_ge(s_v, g + 1)
                        for c in range(KC):
                            last = pe.transpose(PS[:, 1, c * P:(c + 1) * P], cx[:, c, t * P:(t + 1) * P], IDF[:, :])
                        last.then_inc(s_xt, 1)
                        point()
                        pe.wait_ge(s_XX, n + 1)
                        pe.wait_ge(s_W, n + 1)
                        pe.wait_ge(s_Wp, n + 1)
                        if t == 0:
                            pe.wait_ge(s_CB, g + 1)
                        for r in range(2):
                            wait(pe, s_yg, (n - 1) * 2 + r + 1)
                            q = slice(64 * r, 64 * r + 64)
                            for c in range(KC):
                                col = c * G
                                pe.matmul(PS[:, 2 + r, col:col + G], XX[q, 2, c * P:(c + 1) * P],
                                          IDF[q, 64 * r:64 * r + 64], start=True, stop=False)
                                for h2 in range(2):
                                    h = 2 * c + h2
                                    o = PS[64 * h2:64 * h2 + 64, 2 + r, col:col + G]
                                    pe.matmul(o, XX[q, 0, h * 64:(h + 1) * 64], Wl[q, h * G:(h + 1) * G],
                                              start=False, stop=False)
                                    last = pe.matmul(o, XX[q, 1, h * 64:(h + 1) * 64], Wu[q, h * G:(h + 1) * G],
                                                     start=False, stop=True)
                            last.then_inc(s_Y, 1)
                            point()
                        point()
                    wait(pe, s_sq, g * NT + NT)
                    for w in range(-1, GB):
                        lo, hi = max(w, 0), min(w + 2, GB)
                        q = slice(64 * (lo - w), 64 * (hi - w))
                        for k in range(KC):
                            last = pe.matmul(PS[q, 0, w + 1:w + 2], sq[:, k, lo * G:hi * G], ON1[:, :],
                                             start=(k == 0), stop=(k == KC - 1))
                    last.then_inc(s_ss, 1)
                    wait(pe, s_ygl, g * NT + NT)
                    for i in range(KC):
                        m = (i + 1) % KC
                        if m == 0:
                            pe.wait_ge(s_ms, g + 1)
                        split3(PS[:, m, :], lambda k: whoh[:, k, m * P:(m + 1) * P],
                               lambda k: whol[:, k, m * P:(m + 1) * P], lambda k: ygh[:, k, :],
                               lambda k: ygl[:, k, :], s_ot)
                        point()
                    pe.wait_ge(s_otT, g * 4 + 4)
                    for j in range(GB + 1):
                        if j < GB:
                            b = g * GB + j
                            wait(pe, s_UU, b)
                            wait(pe, s_UV, b)
                            pe.sem_inc(s_null, 1)
                            for h2 in range(2):
                                q = slice(64 * h2, 64 * h2 + 64)
                                for c in range(KC):
                                    last = pe.matmul(PS[q, h2, c * P:(c + 1) * P], otT[q, c, j * G:(j + 1) * G],
                                                     WoT2[q, c * P:(c + 1) * P], start=True, stop=True)
                            last.then_inc(s_U, 1)
                            point()
                        if j >= 1:
                            b = g * GB + j - 1
                            pe.wait_ge(s_UU, b + 1)
                            pe.wait_ge(s_UV, b + 1)
                            wait(pe, s_X, b - 1)
                            o = PS[:, 2 + (j - 1) % 2, 0:P]
                            pe.matmul(o, ONB[:, :], OBP[:, :], start=True, stop=False)
                            for c in range(KC):
                                last = pe.matmul(o, swT[:, par, j - 1, c * P:(c + 1) * P],
                                                 UU[:, (j - 1) % 2, c * P:(c + 1) * P], start=False, stop=(c == KC - 1))
                            last.then_inc(s_o, 1)
                    assert pts[0] >= POINTS
                groups(pe, front, back)

            @block.vector
            def _(dve):
                dve.memset(xn[:, :, P:P + 1], 1.0)
                dve.memset(CBl[:, :, :], 0.0)
                dve.memset(CBu[:, :, :], 0.0)
                dve.drain()

                def norm(g, j):
                    b = g * GB + j
                    wait(dve, s_T, b - 1)
                    normalise(C, dve, xn[:, j % 2, 0:P], b).then_inc(s_xn, 1)

                def front(g, k, par):
                    j, p = k // 4, k % 4
                    b = g * GB + j
                    if p == 0:
                        if j == 0:
                            norm(g, 0)
                        if j >= 1:
                            i = (j - 1) % 2
                            wait(dve, s_E, b)
                            e3 = E[:, :].rearrange("p (h g) -> p h g", g=G)
                            dve.tensor_reduce(Z[:, :], e3, AX.X, ALU.add)
                            dve.drain()
                            dve.reciprocal(rZ[:, :], Z[:, :])
                            dve.drain()
                            wait(dve, s_swt, b - 2)
                            dve.tensor_tensor(sw[:, i, :].rearrange("p (h g) -> p h g", g=G), e3,
                                              rZ[:, :].unsqueeze(2).broadcast_to([P, HF, G]), ALU.mult).then_inc(s_sw, 1)
                    if p == 1 and j < GB:
                        dve.wait_ge(s_lg, b + 1)
                        wait(dve, s_mt, b)
                        dve.tensor_reduce(nm[:, :], PS[:, 5, :].rearrange("p (h g) -> p h g", g=G),
                                          AX.X, ALU.max, negate=True).then_inc(s_nm, 1)
                    if p == 2 and j >= 1:
                        wait(dve, s_T, b)
                        t3 = PS[:, 6, 0:387].rearrange("p (c n) -> p c n", n=129)
                        dve.tensor_copy(sn[:, 0:3], t3[:, :, P])
                        dve.tensor_copy(sn[:, 3:4], PS[:, 4, 256 + P:257 + P])
                        dve.drain()
                        dve.tensor_scalar(rs[:, :], sn[:, :], 1e-5, None, ALU.add)
                        dve.drain()
                        dve.reciprocal(rs[:, :], rs[:, :])
                        dve.drain()
                        wait(dve, s_Tt, b - 1)
                        dve.tensor_tensor(Tn[:, 0:384].rearrange("p (c n) -> p c n", n=P), t3[:, :, 0:P],
                                          rs[:, 0:3].unsqueeze(2).broadcast_to([P, 3, P]), ALU.mult)
                        dve.tensor_scalar(Tn[:, 384:512], PS[:, 4, 256:256 + P], rs[:, 3:4], None, ALU.mult)
                        if j == 1:
                            wait(dve, s_rt, g)
                        dve.tensor_tensor(RT[:, (j - 1) * KC:j * KC], sn[:, :], rs[:, :], ALU.mult)
                        dve.drain().then_inc(s_Tn, 1)
                    if p == 3 and j < GB - 1:
                        norm(g, j + 1)

                def back(g, par, more):
                    pts = [0]

                    def point():
                        if more and pts[0] < POINTS:
                            front(g + 1, pts[0], 1 - par)
                        pts[0] += 1

                    dve.wait_ge(s_rt, g + 1)
                    wait(dve, s_st, g * 4)
                    for h2 in range(2):
                        last = dve.tensor_tensor(R[32 * h2:32 * h2 + 32, :].rearrange("p (b g) -> p b g", g=G),
                                                 PS[0:32, 2 + h2, 0:G].unsqueeze(1).broadcast_to([32, GB, G]),
                                                 Rm[:, :].unsqueeze(2).broadcast_to([32, GB, G]), ALU.mult)
                    last.then_inc(s_R, 1)

                    def token_low(c):
                        dve.wait_ge(s_sth, g * 4 + c + 1)
                        dve.tensor_tensor(stl[:, c, :], PS[:, c, :], sth[:, c, :], ALU.subtract).then_inc(s_stl, 1)
                    token_low(0)
                    token_low(1)
                    point()
                    token_low(2)
                    token_low(3)
                    point()

                    def gate(m):
                        dve.wait_ge(s_tz, g * 4 + m + 1)
                        dve.scalar_tensor_tensor(zs[:, m, :], tn[:, m % 2, :], 1.0, PS[:, m, :], ALU.add, ALU.mult)\
                           .then_inc(s_zs, 1)

                    def taps(m):
                        dve.wait_ge(s_c0, g * 5 + m + 1)
                        u = PS[:, m % 4, :].rearrange("p (b l) -> p b l", l=G)
                        dst = (cx[:, m, :] if m < KC else Dec[:, :]).rearrange("p (b l) -> p b l", l=G)
                        dve.scalar_tensor_tensor(dst[:, :, 1:], u[:, :, 0:G - 1], cw[:, 3 * m + 1:3 * m + 2],
                                                 dst[:, :, 1:], ALU.mult, ALU.add)
                        dve.drain()
                        dve.scalar_tensor_tensor(dst[:, :, 2:], u[:, :, 0:G - 2], cw[:, 3 * m:3 * m + 1],
                                                 dst[:, :, 2:], ALU.mult, ALU.add)
                        dve.drain().then_inc(s_c1, 1)

                    def silu(m):
                        dve.wait_ge(s_tc, g * 5 + m + 1)
                        if m < KC:
                            dve.scalar_tensor_tensor(cx[:, m, :], tn[:, m % 2, :], 1.0, cx[:, m, :], ALU.add, ALU.mult)\
                               .then_inc(s_cx, 1)
                        else:
                            for i in range(2):
                                q = slice(64 * i, 64 * i + 64)
                                last = dve.scalar_tensor_tensor(cB[:, i, :], tn[q, m % 2, :], 1.0, Dec[q, :],
                                                                ALU.add, ALU.mult)
                            dve.drain().then_inc(s_cx, 1)
                    for m in range(4):
                        point()
                        gate(m)
                    for m in range(5):
                        point()
                        taps(m)
                        if m >= 1:
                            silu(m - 1)
                    silu(4)
                    dve.wait_ge(s_dt, g + 1)
                    wait(dve, s_Rf, g * NT)
                    v, e, l = dv[:, 0, :], dv[:, 1, :], dv[:, 2, :]
                    v3 = v.rearrange("p (t h) -> p t h", h=16)
                    dve.tensor_tensor(v3, PS[:, 1, 0:NT * 16].rearrange("p (t h) -> p t h", h=16),
                                      dtb[:, :].unsqueeze(1).broadcast_to([P, NT, 16]), ALU.add)
                    dve.drain().then_inc(s_v, 1)
                    dve.scalar_tensor_tensor(e, v, -1.0, v, ALU.mult, ALU.max)
                    dve.drain().then_inc(s_dv, 1)
                    dve.wait_ge(s_sp, g + 1)
                    dve.scalar_tensor_tensor(v, v, 0.0, l, ALU.max, ALU.add)
                    dve.drain()
                    dve.tensor_tensor(dtA[:, :].rearrange("p (t h) -> p t h", h=16), v3,
                                      nA[:, :].unsqueeze(1).broadcast_to([P, NT, 16]), ALU.mult)
                    dve.drain().then_inc(s_dv, 1)
                    dve.wait_ge(s_xd, g + 1)
                    dve.tensor_tensor(xd[:, :].rearrange("p (t h) -> p t h", h=8),
                                      PS[:, 2, 0:NT * 8].rearrange("p (t h) -> p t h", h=8),
                                      Dp[:, :].unsqueeze(1).broadcast_to([P, NT, 8]), ALU.add)
                    point()
                    dve.wait_ge(s_cb, g + 1)
                    wait(dve, s_Wp, g * NT)
                    cbp = PS[:, 3, 0:NT * G].rearrange("p (t l) -> p t l", l=G)
                    dve.tensor_tensor(CBl[:, :, 1:], cbp[:, :, 0:G - 1],
                                      LTM[:, 1:].unsqueeze(1).broadcast_to([P, NT, G - 1]), ALU.mult)
                    dve.tensor_tensor(CBu[:, :, 0:G - 1], cbp[:, :, 1:],
                                      UTM[:, 0:G - 1].unsqueeze(1).broadcast_to([P, NT, G - 1]), ALU.mult)
                    dve.drain().then_inc(s_CB, 1)
                    point()
                    for t in range(NT):
                        n = g * NT + t
                        dve.wait_ge(s_xt, n + 1)
                        wait(dve, s_Y, n * 2)
                        x3 = PS[:, 1, :].rearrange("p (h c) -> p h c", c=64)
                        for i, s in enumerate((v[:, t * 16:t * 16 + 8], v[:, t * 16 + 8:t * 16 + 16],
                                               xd[:, t * 8:t * 8 + 8])):
                            last = dve.tensor_tensor(XX[:, i, :].rearrange("p (h c) -> p h c", c=64), x3,
                                                     s.unsqueeze(2).broadcast_to([P, 8, 64]), ALU.mult)
                        last.then_inc(s_XX, 1)
                        dve.wait_ge(s_Dec, n + 1)
                        dve.tensor_tensor(Wl[:, :].rearrange("p (h l) -> p h l", l=G),
                                          Dec[:, :].rearrange("p (h l) -> p h l", l=G),
                                          CBl[:, t, :].unsqueeze(1).broadcast_to([P, 8, G]), ALU.mult).then_inc(s_W, 1)
                        point()
                        point()
                        for r in range(2):
                            dve.wait_ge(s_Y, n * 2 + r + 1)
                            z4 = zs[:, :, (2 * t + r) * G:(2 * t + r + 1) * G]
                            dve.tensor_tensor(z4, PS[:, 2 + r, 0:256].rearrange("p (c l) -> p c l", l=G), z4,
                                              ALU.mult).then_inc(s_yg, 1)
                        point()
                        point()
                    dve.wait_ge(s_ss, g + 1)
                    wait(dve, s_UU, g * GB)
                    for h2 in range(2):
                        q = slice(64 * h2, 64 * h2 + 64)
                        dve.tensor_scalar(R8[q, :], PS[q, 0, 1 - h2:1 - h2 + GB], 1.0 / DI, 1e-5, ALU.mult, ALU.add)
                    dve.drain().then_inc(s_ms, 1)
                    for i in range(KC):
                        point()
                        if i == 0:
                            dve.wait_ge(s_sd, g + 1)
                            dve.reciprocal(R8[:, :], R8[:, :])
                            dve.drain().then_inc(s_R8, 1)
                    for j in range(GB + 1):
                        if j < GB:
                            b = g * GB + j
                            dve.wait_ge(s_U, b + 1)
                            wait(dve, s_o, b - 1)
                            dve.tensor_scalar(UU[64:128, j % 2, :], PS[64:128, 1, :], R8[64:128, j:j + 1],
                                              None, ALU.mult).then_inc(s_UV, 1)
                            point()
                        if j >= 1:
                            b = g * GB + j - 1
                            dve.wait_ge(s_o, b + 1)
                            dve.tensor_tensor(C["xs"](b), PS[:, 2 + (j - 1) % 2, 0:P], C["xs"](b), ALU.add).then_inc(s_X, 1)
                            dve.drain()
                            dve.bn_stats(C["ST"][:, ds(b * 6, 6)], C["xs"](b))
                groups(dve, front, back)

            @block.gpsimd
            def _(pool):
                def back(g):
                    for t in range(NT):
                        n = g * NT + t
                        if t == 0:
                            pool.wait_ge(s_dv, g * 2 + 2)
                        wait(pool, s_seg, n)
                        for d, M in enumerate((LTM, UTM)):
                            last = pool.tensor_tensor(
                                Rf[:, d, :].rearrange("p (h l) -> p h l", l=G),
                                dtA[:, t * 16 + 8 * d:t * 16 + 8 * d + 8].unsqueeze(2).broadcast_to([P, 8, G]),
                                M[:, :].unsqueeze(1).broadcast_to([P, 8, G]), ALU.mult)
                        pool.drain().then_inc(s_Rf, 1)
                        if t == 0:
                            pool.wait_ge(s_CB, g + 1)
                        pool.wait_ge(s_Dec, n + 1)
                        wait(pool, s_Y, n * 2)
                        pool.tensor_tensor(Wu[:, :].rearrange("p (h l) -> p h l", l=G),
                                           Dec[:, :].rearrange("p (h l) -> p h l", l=G),
                                           CBu[:, t, :].unsqueeze(1).broadcast_to([P, 8, G]), ALU.mult).then_inc(s_Wp, 1)
                        if t >= 1:
                            low(n - 1, t - 1)
                    low(g * NT + NT - 1, NT - 1)

                def low(n, t):
                    pool.wait_ge(s_ygh, n + 1)
                    pool.tensor_tensor(pair_cols(ygl, t), pair_cols(zs, t), pair_cols(ygh, t),
                                       ALU.subtract).then_inc(s_ygl, 1)
                back(0)
                if NG > 1:
                    with pool.Fori(1, NG) as g:
                        back(g)

            @block.scalar
            def _(act):
                def front(g, k, par):
                    j, p = k // 4, k % 4
                    b = g * GB + j
                    if p == 0 and j < GB:
                        act.wait_ge(s_tr, b + 1)
                        wait(act, s_lg, b)
                        act.copy(xnT[:, :], PS[:, 4, 0:P]).then_inc(s_xnT, 1)
                    if p == 1 and j >= 1:
                        wait(act, s_swt, b)
                        if j == 1:
                            wait(act, s_o, (g - 1) * GB)
                        act.copy(swT[:, par, j - 1, :], PS[:, 7, :]).then_inc(s_swT, 1)
                    if p == 2 and j < GB:
                        act.wait_ge(s_mt, b + 1)
                        wait(act, s_lm, b)
                        act.copy(mT[:, :], PS[0:8, 4, 0:P // 2].bitcast(BF16)).then_inc(s_mT, 1)
                    if p == 3:
                        if j < GB:
                            act.wait_ge(s_lm, b + 1)
                            wait(act, s_sw, b)
                            act.activation(E[:, :], PS[:, 5, :], ACT.Exp).then_inc(s_E, 1)
                        if j >= 1:
                            wait(act, s_Tt, b)
                            if j == 1:
                                wait(act, s_st, g * 4)
                            act.copy(TT[:, j - 1, :], PS[:, 7, :]).then_inc(s_TT, 1)

                def back(g, par, more):
                    pts = [0]

                    def point():
                        if more and pts[0] < POINTS:
                            front(g + 1, pts[0], 1 - par)
                        pts[0] += 1

                    for c in range(KC):
                        act.wait_ge(s_st, g * 4 + c + 1)
                        wait(act, s_ot, g * 4)
                        act.copy(sth[:, c, :], PS[:, c, :]).then_inc(s_sth, 1)
                        if c % 2:
                            point()
                    for m in range(KC):
                        act.wait_ge(s_z, g * 4 + m + 1)
                        if m < 2:
                            wait(act, s_cx, g * 5)
                        else:
                            wait(act, s_zs, g * 4 + m - 1)
                        act.activation(tn[:, m % 2, :], PS[:, m, :], ACT.Tanh).then_inc(s_tz, 1)
                        point()

                    def tap(m):
                        act.wait_ge(s_u, g * 5 + m + 1)
                        if m < KC:
                            wait(act, s_U, g * GB)
                        else:
                            wait(act, s_W, g * NT)
                            wait(act, s_Wp, g * NT)
                        act.activation(cx[:, m, :] if m < KC else Dec[:, :], PS[:, m % 4, :], ACT.Identity,
                                       bias=cb[:, m:m + 1], scale=cw[:, 3 * m + 2:3 * m + 3]).then_inc(s_c0, 1)

                    def tanh(m):
                        act.wait_ge(s_c1, g * 5 + m + 1)
                        if m < 2:
                            act.wait_ge(s_zs, g * 4 + m + 3)
                        else:
                            wait(act, s_cx, g * 5 + m - 1)
                        act.activation(tn[:, m % 2, :], cx[:, m, :] if m < KC else Dec[:, :], ACT.Tanh).then_inc(s_tc, 1)
                    for m in range(5):
                        tap(m)
                        if m >= 1:
                            tanh(m - 1)
                        point()
                    tanh(4)
                    act.wait_ge(s_dv, g * 2 + 1)
                    act.activation(dv[:, 1, :], dv[:, 1, :], ACT.Exp, scale=-1.0)
                    act.drain()
                    act.activation(dv[:, 2, :], dv[:, 1, :], ACT.Ln, bias=1.0).then_inc(s_sp, 1)
                    point()
                    point()
                    for t in range(NT):
                        n = g * NT + t
                        act.wait_ge(s_seg, n + 1)
                        wait(act, s_W, n)
                        wait(act, s_Wp, n)
                        act.activation(Dec[:, :], PS[:, 0, :], ACT.Exp).then_inc(s_Dec, 1)
                        for r in range(4):
                            point()
                        act.wait_ge(s_yg, n * 2 + 2)
                        act.activation(pair_cols(sq, t), pair_cols(zs, t), ACT.Square).then_inc(s_sq, 1)
                        act.copy(pair_cols(ygh, t), pair_cols(zs, t)).then_inc(s_ygh, 1)
                    act.wait_ge(s_ms, g + 1)
                    act.activation(R8[:, :], R8[:, :], ACT.Sqrt).then_inc(s_sd, 1)
                    for i in range(KC):
                        m = (i + 1) % KC
                        act.wait_ge(s_ot, g * 4 + i + 1)
                        act.copy(otT[:, m, :], PS[:, m, :]).then_inc(s_otT, 1)
                        point()
                    for j in range(GB):
                        b = g * GB + j
                        act.wait_ge(s_U, b + 1)
                        if j == 0:
                            act.wait_ge(s_R8, g + 1)
                        wait(act, s_o, b - 1)
                        act.mul(UU[0:64, j % 2, :], PS[0:64, 0, :], R8[0:64, j:j + 1]).then_inc(s_UU, 1)
                        point()
                groups(act, front, back)


def gnn1(C):
    nc, io, B, NQ, sem, tile, PS = C["nc"], C["io"], C["B"], C["NQ"], C["sem"], C["tile"], C["PS"]
    IDF = C["IDF"]
    WC = P + 2
    with ExitStack() as ctx:
        VS = tile(ctx, "c_VS", [P, B * WC])
        V3 = VS[:, :].rearrange("p (b w) -> p b w", w=WC)
        cf = tile(ctx, "c_cf", [P, B])
        bf = tile(ctx, "c_bf", [P, B])
        KT = tile(ctx, "c_KT", [P, NQ * P], BF16)
        sel = tile(ctx, "c_sel", [P, 4 * P], BF16)
        MT = tile(ctx, "c_MT", [P, P])
        adj = tile(ctx, "c_adj", [P, P], I32)
        mf = tile(ctx, "c_mf", [P, P])
        av = tile(ctx, "c_av", [P, 2 * P])
        tmp = tile(ctx, "c_tmp", [P, P])
        WT = tile(ctx, "c_WT", [P, P])
        s_wd, s_m3, s_mt, s_mc, s_wt, s_sl = (sem("c_" + x) for x in ("wd", "m3", "mt", "mc", "wt", "sl"))

        class Load:
            count, zcount = 16, 1

            def __call__(self, block, W, s_w, s_wz):
                self.W, self.s_w, self.s_wz = W, s_w, s_wz

                @block.sync
                def _(sp):
                    sp.dma_start(W[:, 0:P], io["cW"]).then_inc(s_w, 16)
                    sp.dma_start(av[:, :], io["ca"].partition_broadcast(P)).then_inc(s_wd, 16)
                    sp.dma_start(adj[:, :], io["adj"]).then_inc(s_wd, 16)
                    sp.dma_start(sel[:, :], io["c_sel"][:, 0:4 * P]).then_inc(s_sl, 16)
                    sp.wait_ge(s_sl, 16)

            def vector(self, dve):
                dve.wait_ge(self.s_w, 16)
                dve.wait_ge(s_wd, 32)
                for k in range(2):
                    dve.tensor_tensor(tmp[:, :], self.W[:, 0:P], av[:, k * P:(k + 1) * P], ALU.mult)
                    dve.drain()
                    dve.tensor_reduce(self.W[:, P + k:P + k + 1], tmp[:, :], AX.X, ALU.add)
                    dve.drain()
                dve.sem_inc(self.s_wz, 1)
                dve.tensor_copy(mf[:, :], adj[:, :])
                dve.drain()
                dve.tensor_scalar(mf[:, :], mf[:, :], 0.0, None, ALU.is_gt)

        project(C, "c_", ctx, WC, Load(), VS)
        with nc.Block() as block:
            @block.tensor
            def _(pe):
                pe.transpose(PS[:, 0, 0:P], mf[:, :], IDF[:, :]).then_inc(s_mt, 1)

            @block.vector
            def _(dve):
                dve.wait_ge(s_mt, 1)
                dve.tensor_copy(MT[:, :], PS[:, 0, 0:P])
        with ExitStack() as c2:
            factors(C, "c_", c2, V3[:, :, P:P + 1], V3[:, :, P + 1:P + 2], 1, cf[:, :], bf[:, :], KT)

        with ExitStack() as c2:
            W1 = P + 1
            VX = tile(c2, "c_VX", [P, 2, 4 * W1])
            PT = tile(c2, "c_PT", [P, 2, 4 * P])
            rec = tile(c2, "c_rec", [P, 2, 4])
            ex = tile(c2, "c_ex", [P, 2, 4 * P])
            pos = tile(c2, "c_pos", [P, 2, 4 * P])
            s_vx, s_K, s_pt, s_av, s_rc, s_ex, s_res = (
                sem("c2_" + x) for x in ("vx", "K", "pt", "av", "rc", "ex", "res"))

            def sums(r):
                return PS[:, 2 + 2 * (r % 2):4 + 2 * (r % 2), 0:2 * W1].rearrange("p k (j w) -> p k j w", w=W1)

            with nc.Block() as block:
                @block.gpsimd
                def _(pool):
                    def values(q, r):
                        wait(pool, s_av, q - 1)
                        vx = VX[:, r % 2, :].rearrange("p (j w) -> p j w", w=W1)
                        v = VS[:, ds(q * 4 * WC, 4 * WC)].rearrange("p (j w) -> p j w", w=WC)
                        bb = bf[:, ds(q * 4, 4)]
                        pool.tensor_tensor(vx[:, :, 0:P], v[:, :, 0:P], bb.unsqueeze(2).broadcast_to([P, 4, P]),
                                           ALU.mult)
                        pool.tensor_copy(vx[:, :, P], bb)
                        pool.drain().then_inc(s_vx, 1)
                    pipelined(pool, NQ, 2, [(0, values)])

                @block.tensor
                def _(pe):
                    def spread(q, r):
                        wait(pe, s_pt, q - 1)
                        for j in range(4):
                            last = pe.matmul(PS[:, r % 2, j * P:(j + 1) * P], sel[0:96, j * P:(j + 1) * P],
                                             KT[0:96, ds(q * P, P)], start=True, stop=True)
                        last.then_inc(s_K, 1)

                    def attend(q, r):
                        pe.wait_ge(s_pt, q + 1)
                        pe.wait_ge(s_vx, q + 1)
                        wait(pe, s_ex, q - 1)
                        for j in range(4):
                            last = pe.matmul(PS[:, 2 + 2 * (r % 2) + j // 2, (j % 2) * W1:(j % 2 + 1) * W1],
                                             PT[:, r % 2, j * P:(j + 1) * P], VX[:, r % 2, j * W1:(j + 1) * W1],
                                             start=True, stop=True)
                        last.then_inc(s_av, 1)
                    pipelined(pe, NQ, 2, [(0, spread), (1, attend)])

                @block.vector
                def _(dve):
                    def weights(q, r):
                        dve.wait_ge(s_K, q + 1)
                        wait(dve, s_av, q - 1)
                        for j in range(4):
                            last = dve.scalar_tensor_tensor(PT[:, r % 2, j * P:(j + 1) * P],
                                                            PS[:, r % 2, j * P:(j + 1) * P], cf[:, ds(q * 4 + j, 1)],
                                                            MT[:, :], ALU.max, ALU.mult)
                        last.then_inc(s_pt, 1)

                    def recip(q, r):
                        dve.wait_ge(s_av, q + 1)
                        wait(dve, s_ex, q - 1)
                        dve.reciprocal(rec[:, r % 2, :].rearrange("p (k j) -> p k j", j=2),
                                       sums(r)[:, :, :, P]).then_inc(s_rc, 1)

                    def elu(q, r):
                        dve.wait_ge(s_ex, q + 1)
                        dve.scalar_tensor_tensor(pos[:, r % 2, :], ex[:, r % 2, :], 1.0, pos[:, r % 2, :],
                                                 ALU.min, ALU.add)
                        dve.drain()
                        xq = C["X"][:, ds(q * 4 * P, 4 * P)]
                        dve.scalar_tensor_tensor(xq, pos[:, r % 2, :], -1.0, xq, ALU.add, ALU.add)
                        dve.drain().then_inc(s_res, 1)
                        for j in range(4):
                            dve.bn_stats(C["ST"][:, ds((q * 4 + j) * 6, 6)], C["xs"](q * 4 + j))
                    pipelined(dve, NQ, 2, [(0, weights), (1, recip), (2, elu)])

                @block.scalar
                def _(act):
                    def parts(q, r):
                        act.wait_ge(s_rc, q + 1)
                        wait(act, s_res, q - 1)
                        for j in range(4):
                            h, o = sums(r)[:, j // 2, j % 2, 0:P], slice(j * P, (j + 1) * P)
                            act.activation(ex[:, r % 2, o], h, ACT.Exp, scale=rec[:, r % 2, j:j + 1])
                            act.activation(pos[:, r % 2, o], h, ACT.Relu, scale=rec[:, r % 2, j:j + 1])
                        act.drain().then_inc(s_ex, 1)
                    pipelined(act, NQ, 2, [(0, parts)])


def moe(C, out):
    nc, io, B, sem, tile, PS = C["nc"], C["io"], C["B"], C["sem"], C["tile"], C["PS"]
    IDF = C["IDF"]
    NTG = B // 4
    NH1 = E8 * HID
    with ExitStack() as ctx:
        gates = tile(ctx, "d_gates", [P, B * E8])
        wh = tile(ctx, "d_wh", [P, 2, NH1], BF16)
        wl = tile(ctx, "d_wl", [P, 2, NH1], BF16)
        w2h = tile(ctx, "d_w2h", [P, E8 * 3 * P], BF16)
        w2l = tile(ctx, "d_w2l", [P, E8 * 3 * P], BF16)
        s_rt = sem("d_rt")

        with ExitStack() as c2:
            LG = tile(c2, "d_LG", [P, B * E8])
            mm = tile(c2, "d_mm", [P, B])
            m1 = tile(c2, "d_m1", [P, B])
            m2 = tile(c2, "d_m2", [P, B])
            oh = tile(c2, "d_oh", [P, 2, B * E8])
            sc = tile(c2, "d_sc", [P, B * E8])
            r8 = tile(c2, "d_r8", [P, E8])
            wst = tile(c2, "d_wst", [P, 3, E8 * 3 * P])
            s_r8, s_wst, s_e0, s_e1 = (sem("d_" + x) for x in ("r8", "wst", "e0", "e1"))

            class Load:
                count, zcount = 16, 0

                def __call__(self, block, W, s_w, s_wz):
                    @block.sync
                    def _(sp):
                        sp.dma_start(W[:, :], io["drw"]).then_inc(s_w, 16)
                        sp.dma_start(r8[:, :], io["c_r8"].partition_broadcast(P)).then_inc(s_wst, 16)
                        sp.dma_start(wst[:, 0, 0:NH1], io["dw1"]).then_inc(s_wst, 16)
                        sp.dma_start(wst[:, 1, 0:NH1], io["dw3"]).then_inc(s_wst, 16)
                        sp.dma_start(wst[:, 2, :], io["dw2"]).then_inc(s_wst, 16)
                        sp.wait_ge(s_wst, 64)

                def vector(self, dve):
                    pass
            project(C, "d_", c2, E8, Load(), LG)

            with nc.Block() as block:
                @block.vector
                def _(dve):
                    def by(a):
                        return a[:, :].unsqueeze(2).broadcast_to([P, B, E8])

                    def v(a):
                        return a.rearrange("p (b e) -> p b e", e=E8)
                    L, S = v(LG[:, :]), v(sc[:, :])
                    r8b = r8[:, :].unsqueeze(1).broadcast_to([P, B, E8])
                    dve.tensor_reduce(mm[:, :], L, AX.X, ALU.max)
                    dve.drain()
                    dve.tensor_tensor(L, L, by(mm), ALU.subtract)
                    dve.drain().then_inc(s_e0, 1)
                    for k in range(2):
                        dve.tensor_copy(wh[:, k, :], wst[:, k, 0:NH1])
                        dve.drain()
                        dve.tensor_tensor(wl[:, k, :], wst[:, k, 0:NH1], wh[:, k, :], ALU.subtract)
                    dve.wait_ge(s_e1, 1)
                    dve.tensor_reduce(mm[:, :], L, AX.X, ALU.add)
                    dve.drain()
                    dve.reciprocal(mm[:, :], mm[:, :])
                    dve.drain()
                    dve.tensor_tensor(L, L, by(mm), ALU.mult)
                    dve.drain()
                    for k, m in enumerate((m1, m2)):
                        o = v(oh[:, k, :])
                        dve.tensor_reduce(m[:, :], L, AX.X, ALU.max)
                        dve.drain()
                        dve.tensor_tensor(S, L, by(m), ALU.is_equal)
                        dve.drain()
                        dve.tensor_tensor(S, S, r8b, ALU.mult)
                        dve.drain()
                        dve.tensor_reduce(mm[:, :], S, AX.X, ALU.max)
                        dve.drain()
                        dve.tensor_tensor(o, S, by(mm), ALU.is_equal)
                        dve.drain()
                        if k == 0:
                            dve.scalar_tensor_tensor(LG[:, :], oh[:, 0, :], -2.0, LG[:, :], ALU.mult, ALU.add)
                            dve.drain()
                    dve.scalar_tensor_tensor(mm[:, :], m1[:, :], 1e-9, m2[:, :], ALU.add, ALU.add)
                    dve.drain()
                    dve.reciprocal(mm[:, :], mm[:, :])
                    dve.drain()
                    for k, m in enumerate((m1, m2)):
                        dve.tensor_tensor(m[:, :], m[:, :], mm[:, :], ALU.mult)
                        dve.drain()
                        dve.tensor_tensor(v(oh[:, k, :]), v(oh[:, k, :]), by(m), ALU.mult)
                    dve.drain()
                    dve.tensor_tensor(gates[:, :], oh[:, 0, :], oh[:, 1, :], ALU.add)

                @block.scalar
                def _(act):
                    act.wait_ge(s_e0, 1)
                    act.activation(LG[:, :], LG[:, :], ACT.Exp).then_inc(s_e1, 1)

                @block.gpsimd
                def _(pool):
                    pool.tensor_copy(w2h[:, :], wst[:, 2, :])
                    pool.drain()
                    pool.tensor_tensor(w2l[:, :], wst[:, 2, :], w2h[:, :], ALU.subtract)

        xn = tile(ctx, "d_xn2", [P, 4, P])
        xh = tile(ctx, "d_xh", [P, 2, 512], BF16)
        xl = tile(ctx, "d_xl", [P, 2, 512], BF16)
        sg = tile(ctx, "d_sg", [P, 2, 512])
        hf = tile(ctx, "d_hf", [P, 3, 512])
        hh = tile(ctx, "d_hh", [P, 2, 3, 512], BF16)
        hl = tile(ctx, "d_hl", [P, 2, 3, 512], BF16)
        s_xn, s_tr, s_xh, s_xl, s_up, s_sg, s_hf, s_hh, s_hl, s_y, s_acc, s_out = (
            sem("d2_" + x) for x in "xn tr xh xl up sg hf hh hl y acc out".split())
        NU = E8 * 3

        def groups(eng, body):
            body(0, NTG == 1)
            if NTG > 2:
                with eng.Fori(1, NTG - 1) as g:
                    body(g, False)
            if NTG > 1:
                body(NTG - 1, True)

        with nc.Block() as block:
            @block.tensor
            def _(pe):
                def prep(g):
                    pe.wait_ge(s_xn, g * 4 + 4)
                    wait(pe, s_xl, g)
                    for j in range(4):
                        last = pe.transpose(PS[:, 7, j * P:(j + 1) * P], xn[:, j, :], IDF[:, :])
                    last.then_inc(s_tr, 1)

                def up(g, e, gp):
                    for k in range(3):
                        i = e * 3 + k
                        w = HCH[k]
                        cols = slice(e * HID + 128 * k, e * HID + 128 * k + w)
                        wait(pe, s_hf, g * NU + i - 2)
                        if i == 0:
                            pe.wait_ge(s_xl, g + 1)
                        for m in range(2):
                            o = PS[0:w, 2 * k + m, :]
                            pe.matmul(o, wh[:, m, cols], gp(xh), start=True, stop=False)
                            pe.matmul(o, wh[:, m, cols], gp(xl), start=False, stop=False)
                            last = pe.matmul(o, wl[:, m, cols], gp(xh), start=False, stop=True)
                        last.then_inc(s_up, 1)

                def down(n, e):
                    pe.wait_ge(s_hl, n * 3 + 3)
                    pe.wait_ge(s_hh, n * 3 + 3)
                    wait(pe, s_acc, n)
                    for t in range(4):
                        o = PS[:, 6, t * P:(t + 1) * P]
                        q = slice(t * P, (t + 1) * P)
                        for k in range(3):
                            w = HCH[k]
                            wc = slice((e * 3 + k) * P, (e * 3 + k + 1) * P)
                            pe.matmul(o, hh[0:w, e % 2, k, q], w2h[0:w, wc], start=(k == 0), stop=False)
                            pe.matmul(o, hh[0:w, e % 2, k, q], w2l[0:w, wc], start=False, stop=False)
                            last = pe.matmul(o, hl[0:w, e % 2, k, q], w2h[0:w, wc], start=False, stop=(k == 2))
                    last.then_inc(s_y, 1)

                def body(g, end):
                    def gp(a):
                        return a[:, :, :].rearrange("p a n -> p (a n)")[:, ds((g % 2) * 512, 512)]
                    for e in range(E8):
                        up(g, e, gp)
                        if e > 0 or not (isinstance(g, int) and g == 0):
                            down(g * E8 + (e - 1), (e - 1) % E8)
                        if e == 4 and not end:
                            prep(g + 1)
                    if end:
                        down(g * E8 + E8 - 1, E8 - 1)
                prep(0)
                groups(pe, body)

            @block.vector
            def _(dve):
                def prep(g):
                    wait(dve, s_tr, g)
                    for j in range(4):
                        normalise(C, dve, xn[:, j, :], g * 4 + j).then_inc(s_xn, 1)

                def split(g):
                    dve.wait_ge(s_tr, g + 1)
                    wait(dve, s_up, (g - 1) * NU)
                    def gp(a):
                        return a[:, :, :].rearrange("p a n -> p (a n)")[:, ds((g % 2) * 512, 512)]
                    dve.tensor_copy(gp(xh), PS[:, 7, :])
                    dve.drain()
                    dve.tensor_tensor(gp(xl), PS[:, 7, :], gp(xh), ALU.subtract).then_inc(s_xl, 1)

                def hidden(g, i):
                    w = HCH[i % 3]
                    n = g * NU + i
                    dve.wait_ge(s_sg, n + 1)
                    wait(dve, s_hh, n - 2)
                    wait(dve, s_hl, n - 2)
                    dve.tensor_tensor(hf[0:w, i % 3, :], sg[0:w, i % 2, :], PS[0:w, 2 * (i % 3) + 1, :],
                                      ALU.mult).then_inc(s_hf, 1)

                def add(g, n, e):
                    dve.wait_ge(s_y, n + 1)
                    for t in range(4):
                        b = g * 4 + t
                        last = dve.scalar_tensor_tensor(C["xs"](b), PS[:, 6, t * P:(t + 1) * P],
                                                        gates[:, ds(b * E8 + e, 1)], C["xs"](b), ALU.mult, ALU.add)
                    dve.drain().then_inc(s_acc, 1)

                def body(g, end):
                    first = isinstance(g, int) and g == 0
                    for e in range(E8):
                        for k in range(3):
                            i = e * 3 + k
                            hidden(g, i)
                        if e > 0:
                            add(g, g * E8 + (e - 1), e - 1)
                        elif not first:
                            add(g - 1, g * E8 - 1, E8 - 1)
                        if e == 2 and not end:
                            prep(g + 1)
                        if e == 6 and not end:
                            split(g + 1)
                    if end:
                        add(g, g * E8 + 7, 7)
                prep(0)
                split(0)
                groups(dve, body)

            @block.gpsimd
            def _(pool):
                def low(g, i):
                    w = HCH[i % 3]
                    e = i // 3
                    n = g * NU + i
                    pool.wait_ge(s_hh, n + 1)
                    if i % 3 == 0:
                        wait(pool, s_y, g * E8 + (e - 1))
                    pool.tensor_tensor(hl[0:w, e % 2, i % 3, :], hf[0:w, i % 3, :], hh[0:w, e % 2, i % 3, :],
                                      ALU.subtract).then_inc(s_hl, 1)

                def body(g, end):
                    for i in range(NU):
                        low(g, i)
                groups(pool, body)

            @block.scalar
            def _(act):
                def silu(g, i):
                    w = HCH[i % 3]
                    n = g * NU + i
                    act.wait_ge(s_up, n + 1)
                    wait(act, s_hf, n - 1)
                    act.activation(sg[0:w, i % 2, :], PS[0:w, 2 * (i % 3), :], ACT.Silu).then_inc(s_sg, 1)

                def high(g, i):
                    w = HCH[i % 3]
                    e = i // 3
                    n = g * NU + i
                    act.wait_ge(s_hf, n + 1)
                    if i % 3 == 0:
                        wait(act, s_y, g * E8 + (e - 1))
                    act.copy(hh[0:w, e % 2, i % 3, :], hf[0:w, i % 3, :]).then_inc(s_hh, 1)

                def body(g, end):
                    first = isinstance(g, int) and g == 0
                    for i in range(NU):
                        silu(g, i)
                        if i > 0:
                            high(g, i - 1)
                        elif not first:
                            high(g - 1, NU - 1)
                    if end:
                        high(g, NU - 1)
                groups(act, body)

            @block.sync
            def _(sp):
                o = out.rearrange("b p d -> p b d")

                def body(g, end):
                    wait(sp, s_acc, g * E8 + E8)
                    sp.dma_start(o[:, ds(g * 4, 4), :], C["X3"][:, ds(g * 4, 4), :]).then_inc(s_out, 16)
                groups(sp, body)
                sp.wait_ge(s_out, 16 * NTG)


def host_inputs(a):
    import numpy as np
    c = np.ascontiguousarray

    def bits(ones):
        return c((ones != 0).astype(np.uint16) * np.uint16(0x3F80))
    sel = np.zeros((128, 32, 128), np.float32)
    for r in range(32):
        for t in range(3):
            sel[32 * t + r, r, :] = 1.0
    io = {
        "x": c(a["x"]), "adj": c(a["adj"]),
        "gW": c(np.transpose(a["L0_gnn_W"], (1, 0, 2)).reshape(128, 128)),
        "g_as": c(a["L0_gnn_a_src"].reshape(128)), "g_ad": c(a["L0_gnn_a_dst"].reshape(128)),
        "beta": c(a["L0_gnn_beta_tilde"].reshape(1)), "gWoT": c(a["L0_gnn_W_out"].T),
        "c_id": np.eye(128, dtype=np.float32), "c_idb": bits(np.eye(128)),
        "c_sel": bits(sel.reshape(128, 32 * 128)),
    }
    hw, ho, ow = a["L0_ffn_hy_in_w"], a["L0_ffn_hy_out_w"], a["L0_ffn_out_w"]

    def chunked(wT):
        return c(wT.reshape(-1, 128, wT.shape[1]).transpose(1, 0, 2).reshape(128, -1))

    def conv(w):
        return c(w.reshape(5, 128, -1).transpose(1, 0, 2).reshape(128, -1))
    m = np.arange(64)
    bfm = np.zeros((2, 8, 4, 4, 2, 64), np.float32)
    rm = np.zeros((8, 4, 8), np.float32)
    for h2 in range(2):
        for ch in range(4):
            bfm[h2, :, ch, ch, h2, :] = 1.0
    for b in range(8):
        rm[b, :, b] = 1.0
    lt = np.tile((m[:, None] < m[None, :]).astype(np.float32), (2, 1))
    ut = np.tile((m[:, None] > m[None, :]).astype(np.float32), (2, 1))
    io.update({
        "bWxR": c(a["L0_ffn_W_x"].reshape(8, 64, 128).transpose(1, 0, 2).reshape(64, 1024)),
        "bWsT": c(a["L0_ffn_W_slice"].T), "bbx": c(a["L0_ffn_b_x"].reshape(8, 64).T),
        "btemp": c(a["L0_ffn_temperature"].reshape(8)), "bbs": c(a["L0_ffn_b_slice"].reshape(1, 64)),
        "bob": c(a["L0_ffn_out_b"].reshape(1, 128)), "bWin": chunked(hw.T), "bWho": chunked(ho.T),
        "bWfx": c(a["L0_ffn_W_fx"].T), "bWo2": chunked(ow.T), "bfc": chunked(a["L0_ffn_hy_fcD_w"].T),
        "c_bfm": bits(bfm.reshape(64, 512)), "c_rm": rm.reshape(32, 8),
        "c_selh": bits(np.repeat(np.eye(8), 64, axis=1)),
        "c_lt": lt, "c_ut": ut, "c_uf": np.kron(np.eye(2, dtype=np.float32), ut[:64]),
        "c_ub": np.kron(np.eye(2, dtype=np.float32), lt[:64]),
        "bnw": c(a["L0_ffn_hy_norm_w"].reshape(4, 128).T), "bbfx": c(a["L0_ffn_b_fx"]),
        "bdtb": c(a["L0_ffn_hy_dt_bias"]), "bAl": c(a["L0_ffn_hy_A_log"]), "bD": c(a["L0_ffn_hy_D"]),
        "bcw": conv(a["L0_ffn_hy_conv_w"]), "bcb": conv(a["L0_ffn_hy_conv_b"].reshape(640, 1)),
    })
    io.update({"cW": c(a["L1_gnn_W"]), "ca": c(a["L1_gnn_a"].reshape(256))})
    w2 = np.zeros((8, 384, 128), np.float32)
    w2[:, 0:341] = a["L1_ffn_w2"].transpose(0, 2, 1)
    io.update({
        "drw": c(a["L1_ffn_router_w"].T), "c_r8": np.arange(8, 0, -1).astype(np.float32),
        "dw1": c(a["L1_ffn_w1"].reshape(2728, 128).T), "dw3": c(a["L1_ffn_w3"].reshape(2728, 128).T),
        "dw2": c(w2.reshape(8, 3, 128, 128).transpose(2, 0, 1, 3).reshape(128, 3072)),
    })
    return io


def kernel(**inputs):
    import numpy as _np
    import concourse.bacc as _bacc
    from concourse import mybir as _mybir
    from concourse.bass_utils import run_bass_kernel_spmd as _run

    nc = _bacc.Bacc("TRN2", target_bir_lowering=False, num_devices=1)
    arrays = {f"in_{k}": v for k, v in host_inputs({k: _np.asarray(v) for k, v in inputs.items()}).items()}
    io = {k[3:]: nc.dram_tensor(k, v.shape, _mybir.dt.from_np(v.dtype), kind="ExternalInput").ap()
          for k, v in arrays.items()}
    out = nc.dram_tensor("out_x", inputs["x"].shape, _mybir.dt.float32, kind="ExternalOutput").ap()
    build(nc, io, out)
    r = _run(nc, [arrays], core_ids=[0])
    return r.results[0]["out_x"]
```

```python
from contextlib import ExitStack

import concourse.bass as bass
from concourse import mybir

F32 = mybir.dt.float32
BF16 = mybir.dt.bfloat16
I32 = mybir.dt.int32
ALU = mybir.AluOpType
ACT = mybir.ActivationFunctionType
AX = mybir.AxisListType
ds = bass.ds

P = 128
H0, DH = 8, 16
HF, PF = 8, 64
G = 64
NS = 64
DI = HF * PF
CD = DI + 2 * NS
KC = DI // P
E8, HID = 8, 341
HCH = [128, 128, 85]
NH1 = E8 * HID
GB = 8


def wait(eng, sem, n):
    if isinstance(n, int) and n <= 0:
        return
    eng.wait_ge(sem, n)


def pipelined(eng, total, unroll, stages):
    last = max(lag for lag, _ in stages)
    head = min(total, unroll * -(-(last + 2) // unroll))
    for t in range(head):
        for lag, emit in stages:
            if 0 <= t - lag:
                emit(t - lag, (t - lag) % unroll)
    if total > head:
        with eng.Fori(head // unroll, total // unroll) as q:
            for r in range(unroll):
                for lag, emit in stages:
                    emit(q * unroll + (r - lag), (r - lag) % unroll)
    for t in range(total, total + last):
        for lag, emit in stages:
            if 0 <= t - lag < total:
                emit(t - lag, (t - lag) % unroll)


def build(nc, io, out):
    B = io["x"].shape[0]
    io = {k: v.bitcast(BF16) if v.dtype == mybir.dt.uint16 else v for k, v in io.items()}
    NQ = B // 4
    with ExitStack() as root:
        held = []

        def sem(name):
            held.append(nc.alloc_semaphore(name=name))
            return held[-1]

        def end_layer():
            nc.clear_and_free_semaphores(held)
            nc.all_engine_barrier()
            held.clear()

        def tile(ctx, name, shape, dt=F32):
            return ctx.enter_context(nc.sbuf_tensor("t_" + name, shape, dt))

        X = tile(root, "X", [P, B * P])
        X3 = X[:, :].rearrange("p (b d) -> p b d", d=P)
        ST = tile(root, "ST", [P, B * 6])
        MU = tile(root, "MU", [P, B])
        RS = tile(root, "RS", [P, B])
        LT6 = tile(root, "LT6", [P, 3 * B])
        IDF = tile(root, "IDF", [P, P])
        IDB = tile(root, "IDB", [P, P], BF16)
        PS = root.enter_context(nc.psum_tensor("PS", [P, 8, 512], F32))

        def bank(k, n=512, parts=P, col=0):
            return PS[0:parts, k, col:col + n]

        def xs(b):
            return X[:, ds(b * P, P)]

        s_const = sem("s_const")
        s_x = [sem(f"s_x{c}") for c in range(B // 8)]
        C = dict(nc=nc, io=io, sem=sem, tile=tile, X=X, X3=X3, ST=ST, MU=MU, RS=RS, LT6=LT6, IDF=IDF, IDB=IDB,
                 PS=PS, bank=bank, xs=xs, B=B, NQ=NQ)

        load_x(C, s_const, s_x)
        end_layer()
        gnn0(C)
        end_layer()
        ffn0(C)
        end_layer()
        expert_tiles(C, root)
        gnn1(C)
        end_layer()
        moe(C, out)


def load_x(C, s_const, s_x):
    nc, io, X, B, sem = C["nc"], C["io"], C["X"], C["B"], C["sem"]
    CH = 8
    with nc.Block() as block:
        @block.sync
        def _(sp):
            sp.dma_start(C["IDF"][:, :], io["c_id"]).then_inc(s_const, 16)
            sp.dma_start(C["IDB"][:, :], io["c_idb"]).then_inc(s_const, 16)
            for c in range(B // CH):
                sp.dma_start(X[:, c * CH * P:(c + 1) * CH * P],
                             io["x"][c * CH:(c + 1) * CH].rearrange("b p d -> p b d")).then_inc(s_x[c], 16)
            sp.wait_ge(s_const, 32)

        @block.vector
        def _(dve):
            for c in range(B // CH):
                dve.wait_ge(s_x[c], 16)
                for b in range(c * CH, (c + 1) * CH):
                    dve.bn_stats(C["ST"][:, ds(b * 6, 6)], C["xs"](b))


def ln_vector(C, dve, s_var, s_std):
    st = C["ST"][:, :].rearrange("p (b s) -> p b s", s=6)
    B = C["B"]
    dif, var, std = (C["LT6"][:, k * B:(k + 1) * B] for k in range(3))
    MU, RS = C["MU"][:, :], C["RS"][:, :]
    dve.drain()
    dve.tensor_tensor(MU, st[:, :, 1], st[:, :, 4], ALU.add)
    dve.tensor_tensor(dif, st[:, :, 1], st[:, :, 4], ALU.subtract)
    dve.tensor_tensor(var, st[:, :, 2], st[:, :, 5], ALU.add)
    dve.drain()
    dve.tensor_scalar(MU, MU, 0.5, None, ALU.mult)
    dve.tensor_tensor(dif, dif, dif, ALU.mult)
    dve.tensor_scalar(var, var, 1.0 / P, 1e-5, ALU.mult, ALU.add)
    dve.drain()
    dve.scalar_tensor_tensor(var, dif, 0.25, var, ALU.mult, ALU.add).then_inc(s_var, 1)
    dve.wait_ge(s_std, 1)
    dve.reciprocal(RS, std)
    dve.drain()


def ln_scalar(C, act, s_var, s_std):
    B = C["B"]
    act.wait_ge(s_var, 1)
    act.activation(C["LT6"][:, 2 * B:3 * B], C["LT6"][:, B:2 * B], ACT.Sqrt).then_inc(s_std, 1)


def normalise(C, dve, dst, b):
    return dve.tensor_scalar(dst, C["xs"](b), C["MU"][:, ds(b, 1)], C["RS"][:, ds(b, 1)], ALU.subtract, ALU.mult)


def project(C, tag, ctx, wcols, load, VS):
    nc, B, NQ, sem, tile, PS = C["nc"], C["B"], C["NQ"], C["sem"], C["tile"], C["PS"]
    W = tile(ctx, tag + "W", [P, wcols])
    xn = tile(ctx, tag + "xn", [P, 2, 4, P])
    xnT = tile(ctx, tag + "xnT", [P, 2, 4 * P])
    s_w, s_wz, s_var, s_std = (sem(tag + n) for n in ("w", "wz", "var", "std"))
    s_xn, s_tr, s_xnT, s_pr, s_vs = (sem(tag + n) for n in ("xn", "tr", "xnT", "pr", "vs"))
    with nc.Block() as block:
        load(block, W, s_w, s_wz)

        @block.vector
        def _(dve):
            load.vector(dve)
            ln_vector(C, dve, s_var, s_std)

            def norm(q, r):
                wait(dve, s_tr, q - 1)
                for j in range(4):
                    last = normalise(C, dve, xn[:, r % 2, j, :], q * 4 + j)
                last.then_inc(s_xn, 1)
            pipelined(dve, NQ, 2, [(0, norm)])

        @block.scalar
        def _(act):
            ln_scalar(C, act, s_var, s_std)

            def evac_t(q, r):
                act.wait_ge(s_tr, q + 1)
                wait(act, s_pr, q - 1)
                act.copy(xnT[:, r % 2, :], PS[:, r % 2, :]).then_inc(s_xnT, 1)

            def evac_p(q, r):
                act.wait_ge(s_pr, q + 1)
                act.copy(VS[:, ds(q * 4 * wcols, 4 * wcols)].rearrange("p (k n) -> p k n", k=2),
                         PS[:, 2 + 2 * (r % 2):4 + 2 * (r % 2), 0:2 * wcols]).then_inc(s_vs, 1)
            pipelined(act, NQ, 2, [(0, evac_t), (1, evac_p)])

        @block.tensor
        def _(pe):
            def trans(q, r):
                pe.wait_ge(s_xn, q + 1)
                wait(pe, s_xnT, q - 1)
                for j in range(4):
                    last = pe.transpose(PS[:, r % 2, j * P:(j + 1) * P], xn[:, r % 2, j, :], C["IDF"][:, :])
                last.then_inc(s_tr, 1)

            def prod(q, r):
                pe.wait_ge(s_xnT, q + 1)
                wait(pe, s_vs, q - 1)
                for j in range(4):
                    o = PS[:, 2 + 2 * (r % 2) + j // 2, (j % 2) * wcols:(j % 2 + 1) * wcols]
                    last = pe.matmul(o, xnT[:, r % 2, j * P:(j + 1) * P], W[:, :], start=True, stop=True)
                last.then_inc(s_pr, 1)
            pe.wait_ge(s_w, load.count)
            wait(pe, s_wz, load.zcount)
            pipelined(pe, NQ, 2, [(0, trans), (1, prod)])


def factors(C, tag, ctx, S, Dd, NH, cf, bf, KT):
    nc, B, NQ, sem, tile, PS = C["nc"], C["B"], C["NQ"], C["sem"], C["tile"], C["PS"]
    n = B * NH
    nch = -(-n // P)
    w = min(n, P)
    dc = tile(ctx, tag + "dc", [P, n])
    dmax = tile(ctx, tag + "dmax", [P, nch])
    diag = tile(ctx, tag + "diag", [P, nch * w])
    z = tile(ctx, tag + "z", [P, n])
    Kf = tile(ctx, tag + "Kf", [P, n])
    Kp = tile(ctx, tag + "Kp", [P, NQ * 128], BF16)
    ones = tile(ctx, tag + "ones", [P, P])
    KpV = Kp[:, :].rearrange("p (q t r) -> p q t r", t=4, r=32)
    s_c, s_t, s_m, s_bc, s_e, s_k, s_kp, s_kt = (sem(tag + x) for x in
                                               ("fc", "ft", "fm", "fbc", "fe", "fk", "fkp", "fkt"))
    psb = PS[:, 4:8, :].rearrange("p k n -> p (k n)").bitcast(BF16)
    with nc.Block() as block:
        @block.vector
        def _(dve):
            dve.memset(ones[:, :], 1.0)
            dve.memset(Kp[:, :], 0.0)
            dve.tensor_copy(dc[:, :].rearrange("p (b h) -> p b h", h=NH), Dd).then_inc(s_c, 1)
            dve.wait_ge(s_t, 1)
            for c in range(nch):
                dve.tensor_reduce(dmax[0:w, c:c + 1], PS[0:w, 0, c * P:(c + 1) * P], AX.X, ALU.max)
            dve.drain()
            for c in range(nch):
                dve.tensor_scalar(diag[0:w, c * w:(c + 1) * w], C["IDF"][0:w, 0:w], dmax[0:w, c:c + 1], None, ALU.mult)
            dve.drain().then_inc(s_m, 1)
            dve.wait_ge(s_bc, 1)
            zv = z[:, :].rearrange("p (b h) -> p b h", h=NH)
            Dv = PS[:, 1, 0:n].rearrange("p (b h) -> p b h", h=NH)
            dve.tensor_tensor(dc[:, :], dc[:, :], PS[:, 1, 0:n], ALU.subtract)
            dve.tensor_tensor(zv, S, Dv, ALU.add)
            dve.drain()
            dve.tensor_scalar(z[:, :], z[:, :], -0.8, 0.0, ALU.mult, ALU.min)
            dve.drain().then_inc(s_e, 1)
            dve.wait_ge(s_k, 1)
            kk = Kf[:, :].rearrange("p (q r) -> p q r", q=NQ)
            wq = n // NQ
            dve.tensor_copy(KpV[:, :, 0, 0:wq], kk)
            dve.drain()
            dve.tensor_tensor(kk, kk, KpV[:, :, 0, 0:wq], ALU.subtract)
            dve.drain()
            dve.tensor_copy(KpV[:, :, 1, 0:wq], kk)
            dve.drain()
            dve.tensor_tensor(kk, kk, KpV[:, :, 1, 0:wq], ALU.subtract)
            dve.drain()
            dve.tensor_copy(KpV[:, :, 2, 0:wq], kk)
            dve.drain().then_inc(s_kp, 1)
            dve.wait_ge(s_kt, 1)
            dve.tensor_copy(KT[:, :], psb[:, 0:NQ * P])

        @block.scalar
        def _(act):
            act.wait_ge(s_e, 1)
            act.activation(cf, dc[:, :], ACT.Exp, scale=0.8)
            act.activation(bf, dc[:, :], ACT.Exp, scale=0.2)
            act.activation(Kf[:, :], z[:, :], ACT.Exp).then_inc(s_k, 1)

        @block.tensor
        def _(pe):
            pe.wait_ge(s_c, 1)
            for c in range(nch):
                last = pe.transpose(PS[0:w, 0, c * P:(c + 1) * P], dc[:, c * w:(c + 1) * w], C["IDF"][:, :])
            last.then_inc(s_t, 1)
            pe.wait_ge(s_m, 1)
            for c in range(nch):
                last = pe.matmul(PS[:, 1, c * w:(c + 1) * w], ones[0:w, :], diag[0:w, c * w:(c + 1) * w],
                                 start=True, stop=True)
            last.then_inc(s_bc, 1)
            pe.wait_ge(s_kp, 1)
            for q in range(NQ):
                last = pe.transpose(psb[:, q * P:(q + 1) * P], Kp[:, q * P:(q + 1) * P], C["IDB"][:, :])
            last.then_inc(s_kt, 1)


def gnn0(C):
    nc, io, B, NQ, sem, tile, PS = C["nc"], C["io"], C["B"], C["NQ"], C["sem"], C["tile"], C["PS"]
    IDF = C["IDF"]
    WC = P + 2 * H0
    with ExitStack() as ctx:
        VS = tile(ctx, "a_VS", [P, B * WC])
        V3 = VS[:, :].rearrange("p (b w) -> p b w", w=WC)
        cf = tile(ctx, "a_cf", [P, B * H0])
        bf = tile(ctx, "a_bf", [P, B * H0])
        KT = tile(ctx, "a_KT", [P, NQ * P], BF16)
        sel = tile(ctx, "a_sel", [P, 32 * P], BF16)
        MT = tile(ctx, "a_MT", [P, P])
        WoT = tile(ctx, "a_WoT", [P, P])
        adj = tile(ctx, "a_adj", [P, P], I32)
        mf = tile(ctx, "a_mf", [P, P])
        lb = tile(ctx, "a_lb", [P, P])
        msk = tile(ctx, "a_msk", [P, P])
        beta = tile(ctx, "a_beta", [P, 4])
        av = tile(ctx, "a_av", [P, 2 * P])
        tmp = tile(ctx, "a_tmp", [P, P])
        s_wd, s_w2, s_m1, s_m2, s_m3, s_mt, s_mc = (sem("a_" + x) for x in
                                                  ("wd", "w2", "m1", "m2", "m3", "mt", "mc"))

        class Load:
            count, zcount = 16, 1

            def __call__(self, block, W, s_w, s_wz):
                self.W, self.s_w, self.s_wz = W, s_w, s_wz

                @block.sync
                def _(sp):
                    sp.dma_start(W[:, 0:P], io["gW"]).then_inc(s_w, 16)
                    sp.dma_start(av[:, 0:P], io["g_as"].partition_broadcast(P)).then_inc(s_wd, 16)
                    sp.dma_start(av[:, P:2 * P], io["g_ad"].partition_broadcast(P)).then_inc(s_wd, 16)
                    sp.dma_start(adj[:, :], io["adj"]).then_inc(s_w2, 16)
                    sp.dma_start(beta[:, 0:1], io["beta"].partition_broadcast(P)).then_inc(s_w2, 16)
                    sp.dma_start(WoT[:, :], io["gWoT"]).then_inc(s_w2, 16)
                    sp.dma_start(sel[:, :], io["c_sel"]).then_inc(s_w2, 16)
                    sp.wait_ge(s_w2, 64)

            def vector(self, dve):
                dve.wait_ge(self.s_w, 16)
                dve.wait_ge(s_wd, 32)
                for k in range(2):
                    dve.tensor_tensor(tmp[:, :], self.W[:, 0:P], av[:, k * P:(k + 1) * P], ALU.mult)
                    dve.drain()
                    dve.tensor_reduce(self.W[:, P + k * H0:P + (k + 1) * H0],
                                      tmp[:, :].rearrange("p (h f) -> p h f", f=DH), AX.X, ALU.add)
                    dve.drain()
                dve.sem_inc(self.s_wz, 1)

        project(C, "a_", ctx, WC, Load(), VS)

        with nc.Block() as block:
            @block.vector
            def _(dve):
                dve.tensor_copy(mf[:, :], adj[:, :])
                dve.drain()
                dve.tensor_scalar(msk[:, :], mf[:, :], 0.0, None, ALU.is_gt)
                dve.tensor_scalar(mf[:, :], mf[:, :], 0.0, 1e-6, ALU.max, ALU.add)
                dve.scalar_tensor_tensor(beta[:, 1:2], beta[:, 0:1], -1.0, beta[:, 0:1], ALU.mult, ALU.max)
                dve.drain().then_inc(s_m1, 1)
                dve.wait_ge(s_m2, 1)
                dve.scalar_tensor_tensor(beta[:, 3:4], beta[:, 0:1], 0.0, beta[:, 2:3], ALU.max, ALU.add)
                dve.drain()
                dve.tensor_scalar(lb[:, :], lb[:, :], beta[:, 3:4], None, ALU.mult)
                dve.drain()
                dve.tensor_reduce(beta[:, 1:2], lb[:, :], AX.X, ALU.max, negate=True)
                dve.drain().then_inc(s_m1, 1)
                dve.wait_ge(s_m2, 2)
                dve.tensor_tensor(lb[:, :], lb[:, :], msk[:, :], ALU.mult).then_inc(s_m3, 1)
                dve.wait_ge(s_mt, 1)
                dve.tensor_copy(MT[:, :], PS[:, 0, 0:P])

            @block.scalar
            def _(act):
                act.wait_ge(s_m1, 1)
                act.activation(beta[:, 2:3], beta[:, 1:2], ACT.Exp, scale=-1.0)
                act.drain()
                act.activation(beta[:, 2:3], beta[:, 2:3], ACT.Ln, bias=1.0)
                act.activation(lb[:, :], mf[:, :], ACT.Ln).then_inc(s_m2, 1)
                act.wait_ge(s_m1, 2)
                act.activation(lb[:, :], lb[:, :], ACT.Exp, bias=beta[:, 1:2]).then_inc(s_m2, 1)

            @block.tensor
            def _(pe):
                pe.wait_ge(s_m3, 1)
                pe.transpose(PS[:, 0, 0:P], lb[:, :], IDF[:, :]).then_inc(s_mt, 1)

        with ExitStack() as c2:
            factors(C, "a_", c2, V3[:, :, P:P + H0], V3[:, :, P + H0:P + 2 * H0], H0, cf[:, :], bf[:, :], KT)

        with ExitStack() as c2:
            W32 = 32
            HS = 4
            CV = tile(c2, "a_CV", [P, 2, HS * W32])
            ncf = tile(c2, "a_ncf", [P, B * H0])
            VX = tile(c2, "a_VX", [P, 2, H0 * W32])
            PT = tile(c2, "a_PT", [P, 2, H0 * P])
            AV = tile(c2, "a_AV", [P, 2, 2 * P])
            rec = tile(c2, "a_rec", [P, 2, H0])
            hn = tile(c2, "a_hn", [P, 2, P])
            hnT = tile(c2, "a_hnT", [P, 2, P])
            s_nc, s_ra, s_pa, s_vx, s_K, s_pt, s_av, s_ac, s_bk, s_hn, s_ht, s_hc, s_y, s_res = (
                sem("a2_" + x) for x in ("nc", "ra", "pa", "vx", "K", "pt", "av", "ac", "bk", "hn", "ht", "hc", "y", "res"))
            with nc.Block() as block:
                @block.gpsimd
                def _(pool):
                    pool.memset(VX[:, :, :], 0.0)
                    pool.drain()

                    def values(b, r):
                        wait(pool, s_av, b - 1)
                        vx = VX[:, r % 2, :].rearrange("p (h w) -> p h w", w=W32)
                        bb = bf[:, ds(b * H0, H0)]
                        pool.tensor_tensor(vx[:, :, 0:DH],
                                           VS[:, ds(b * WC, P)].rearrange("p (h f) -> p h f", f=DH),
                                           bb.unsqueeze(2).broadcast_to([P, H0, DH]), ALU.mult)
                        pool.tensor_copy(vx[:, :, DH], bb)
                        pool.drain()
                        cc = cf[:, ds(b * H0, HS)]
                        pool.tensor_tensor(CV[:, r % 2, :].rearrange("p (h w) -> p h w", w=W32), vx[:, 0:HS, :],
                                           cc.unsqueeze(2).broadcast_to([P, HS, W32]), ALU.mult).then_inc(s_vx, 1)

                    def edges(b, r):
                        pool.wait_ge(s_ra, b + 1)
                        pt = PT[:, r % 2, 0:HS * P].rearrange("p (h i) -> p h i", i=P)
                        pool.tensor_tensor(pt, pt, MT[:, :].unsqueeze(1).broadcast_to([P, HS, P]),
                                           ALU.mult).then_inc(s_pa, 1)
                    pipelined(pool, B, 4, [(0, values), (0, edges)])

                @block.tensor
                def _(pe):
                    def spread(b, r):
                        wait(pe, s_pt, b - 1)
                        wait(pe, s_ra, b - 1)
                        col = (b - r) * (P // 4)
                        for h in range(H0):
                            o = PS[:, 2 * (r % 2) + h // 4, (h % 4) * P:(h % 4 + 1) * P]
                            k = (r * H0 + h) * P
                            last = pe.matmul(o, sel[0:96, k:k + P], KT[0:96, ds(col, P)], start=True, stop=True)
                        last.then_inc(s_K, 1)

                    def attend(b, r):
                        pe.wait_ge(s_pt, b + 1)
                        pe.wait_ge(s_pa, b + 1)
                        pe.wait_ge(s_vx, b + 1)
                        wait(pe, s_ac, b)
                        for h in range(H0):
                            q = 32 * (h % 4)
                            o = PS[q:q + 32, 4, (h // 4) * P:(h // 4 + 1) * P]
                            last = pe.matmul(o, VX[:, r % 2, h * W32:(h + 1) * W32], PT[:, r % 2, h * P:(h + 1) * P],
                                             start=True, stop=(h >= HS), tile_position=(0, q))
                            if h < HS:
                                pe.matmul(o, CV[:, r % 2, h * W32:(h + 1) * W32], MT[:, :], start=False, stop=True,
                                          tile_position=(0, q))
                        last.then_inc(s_av, 1)

                    def turn(b, r):
                        pe.wait_ge(s_ac, b + 1)
                        wait(pe, s_hn, b)
                        for k in range(2):
                            last = pe.transpose(PS[:, 5, k * P:(k + 1) * P], AV[:, r % 2, k * P:(k + 1) * P], IDF[:, :])
                        last.then_inc(s_bk, 1)

                    def trans(b, r):
                        pe.wait_ge(s_hn, b + 1)
                        wait(pe, s_hc, b)
                        pe.transpose(PS[:, 6, 0:P], hn[:, r % 2, :], IDF[:, :]).then_inc(s_ht, 1)

                    def mix(b, r):
                        pe.wait_ge(s_hc, b + 1)
                        wait(pe, s_res, b)
                        pe.matmul(PS[:, 7, 0:P], hnT[:, r % 2, :], WoT[:, :], start=True, stop=True).then_inc(s_y, 1)
                    pipelined(pe, B, 4, [(0, spread), (1, attend), (2, turn), (3, trans), (4, mix)])

                @block.vector
                def _(dve):
                    dve.tensor_scalar(ncf[:, :], cf[:, :], -1.0, None, ALU.mult).then_inc(s_nc, 1)

                    def weights(b, r):
                        dve.wait_ge(s_K, b + 1)
                        wait(dve, s_av, b - 1)
                        for h in range(HS, H0):
                            last = dve.scalar_tensor_tensor(
                                PT[:, r % 2, h * P:(h + 1) * P],
                                PS[:, 2 * (r % 2) + h // 4, (h % 4) * P:(h % 4 + 1) * P],
                                cf[:, ds(b * H0 + h, 1)], MT[:, :], ALU.max, ALU.mult)
                        last.then_inc(s_pt, 1)

                    def norm(b, r):
                        dve.wait_ge(s_bk, b + 1)
                        wait(dve, s_ht, b - 1)
                        o = PS[:, 5, 0:H0 * W32].rearrange("p (h w) -> p h w", w=W32)
                        dve.reciprocal(rec[:, r % 2, :], o[:, :, DH])
                        dve.drain()
                        dve.tensor_tensor(hn[:, r % 2, :].rearrange("p (h f) -> p h f", f=DH), o[:, :, 0:DH],
                                          rec[:, r % 2, :].unsqueeze(2).broadcast_to([P, H0, DH]),
                                          ALU.mult).then_inc(s_hn, 1)

                    def residual(b, r):
                        dve.wait_ge(s_y, b + 1)
                        dve.tensor_tensor(C["xs"](b), PS[:, 7, 0:P], C["xs"](b), ALU.add).then_inc(s_res, 1)
                        dve.drain()
                        dve.bn_stats(C["ST"][:, ds(b * 6, 6)], C["xs"](b))
                    pipelined(dve, B, 4, [(0, weights), (2, norm), (4, residual)])

                @block.scalar
                def _(act):
                    def copy_a(b, r):
                        act.wait_ge(s_av, b + 1)
                        wait(act, s_bk, b - 1)
                        act.copy(AV[:, r % 2, :], PS[:, 4, 0:2 * P]).then_inc(s_ac, 1)

                    def copy_t(b, r):
                        act.wait_ge(s_ht, b + 1)
                        wait(act, s_y, b - 1)
                        act.copy(hnT[:, r % 2, :], PS[:, 6, 0:P]).then_inc(s_hc, 1)

                    def over(b, r):
                        act.wait_ge(s_K, b + 1)
                        wait(act, s_av, b - 1)
                        for h in range(HS):
                            last = act.activation(PT[:, r % 2, h * P:(h + 1) * P],
                                                  PS[:, 2 * (r % 2), h * P:(h + 1) * P], ACT.Relu,
                                                  bias=ncf[:, ds(b * H0 + h, 1)])
                        last.then_inc(s_ra, 1)
                    act.wait_ge(s_nc, 1)
                    pipelined(act, B, 4, [(0, over), (1, copy_a), (3, copy_t)])


def ffn0(C):
    nc, io, B, sem, tile, PS = C["nc"], C["io"], C["B"], C["sem"], C["tile"], C["PS"]
    IDF, IDB = C["IDF"], C["IDB"]
    NG = B // GB
    NW2 = 18
    NT = GB // 2
    N = GB * G
    with ExitStack() as ctx:
        def T(name, shape, dt=F32):
            return tile(ctx, "b_" + name, shape, dt)
        WXS = T("WXS", [P, DI])
        WfxT = T("WfxT", [P, DI])
        WI = 1168
        winh = T("winh", [P, KC, WI], BF16)
        winl = T("winl", [P, KC, WI], BF16)
        whoh = T("whoh", [P, KC, DI], BF16)
        whol = T("whol", [P, KC, DI], BF16)
        WoT2 = T("WoT2", [P, KC * P])
        fcT = T("fcT", [P, KC * 8])
        BFX = T("BFX", [64, KC * P])
        BFM = T("BFM", [64, KC * P], BF16)
        Rm = T("Rm", [32, 8])
        LBP = T("LBP", [96, DI], BF16)
        OBP = T("OBP", [96, P], BF16)
        ONB = T("ONB", [96, P], BF16)
        SELH = T("SELH", [8, DI], BF16)
        ON1 = T("ON1", [P, 1])
        LTM = T("LTM", [P, G])
        UTM = T("UTM", [P, G])
        UF = T("UF", [P, P])
        UB = T("UB", [P, P])
        cw = T("cw", [P, 5 * 3])
        cb = T("cb", [P, 5])
        nA = T("nA", [P, 16])
        dtb = T("dtb", [P, 16])
        Dp = T("Dp", [P, 8])
        nw = T("nw", [P, KC])
        rt = T("rt", [P, 8])
        s_w, s_w2, s_w3, s_row = (sem("b_" + x) for x in ("w", "w2", "w3", "row"))
        s_p0, s_p1, s_p2, s_var, s_std = (sem("b_" + x) for x in ("p0", "p1", "p2", "var", "std"))

        with ExitStack() as c2, nc.Block() as block:
            WinT = tile(c2, "b_WinT", [P, KC * WI])
            WhoT = tile(c2, "b_WhoT", [P, KC * DI])
            Win = WinT[:, :].rearrange("p (k n) -> p k n", k=KC)
            Who = WhoT[:, :].rearrange("p (k n) -> p k n", k=KC)
            WxR = tile(c2, "b_WxR", [64, 8 * P])
            WsT = tile(c2, "b_WsT", [64, G])
            bxc = tile(c2, "b_bxc", [64, 8])
            row = tile(c2, "b_row", [1, DI])
            rob = tile(c2, "b_rob", [1, DI], BF16)
            bsl = tile(c2, "b_bsl", [1, G])
            obr = tile(c2, "b_obr", [1, P])

            @block.sync
            def _(sp):
                n = [0]

                def ld(dst, src, s=s_w2):
                    sp.dma_start(dst, src).then_inc(s, 16)
                    n[0] += 1
                for dst, key in ((WxR, "bWxR"), (WsT, "bWsT"), (bxc, "bbx")):
                    ld(dst[:, :], io[key], s_w)
                ld(rt[:, :], io["btemp"].partition_broadcast(P), s_w)
                ld(bsl[:, :], io["bbs"], s_w)
                ld(obr[:, :], io["bob"], s_w)
                for dst, key in ((WinT, "bWin"), (nw, "bnw"), (WhoT, "bWho")):
                    ld(dst[:, :], io[key], s_w3)
                for dst, key in ((WfxT, "bWfx"), (WoT2, "bWo2"), (fcT, "bfc"),
                                 (BFM, "c_bfm"), (Rm, "c_rm"), (SELH, "c_selh"), (LTM, "c_lt"), (UTM, "c_ut"),
                                 (UF, "c_uf"), (UB, "c_ub")):
                    ld(dst[:, :], io[key])
                ld(BFX[:, :], io["bbfx"].partition_broadcast(64))
                for c in range(2):
                    ld(dtb[:, 8 * c:8 * c + 8], io["bdtb"].partition_broadcast(P))
                    ld(nA[:, 8 * c:8 * c + 8], io["bAl"].partition_broadcast(P))
                ld(Dp[:, :], io["bD"].partition_broadcast(P))
                ld(cw[:, :], io["bcw"])
                ld(cb[:, :], io["bcb"])
                assert n[0] - 9 == NW2
                sp.wait_ge(s_w2, 16 * NW2)

            @block.tensor
            def _(pe):
                pe.wait_ge(s_w, 96)
                for h in range(HF):
                    pe.matmul(PS[:, 0, h * G:(h + 1) * G], WxR[:, h * P:(h + 1) * P], WsT[:, :], start=True, stop=True)
                for h in range(HF):
                    last = pe.matmul(PS[0:1, 1, h * G:(h + 1) * G], bxc[:, h:h + 1], WsT[:, :], start=True, stop=True)
                last.then_inc(s_p0, 1)

            @block.vector
            def _(dve):
                dve.memset(LBP[:, :], 0.0)
                dve.memset(OBP[:, :], 0.0)
                dve.memset(ONB[:, :], 1.0)
                dve.memset(ON1[:, :], 1.0)
                dve.wait_ge(s_w, 96)
                dve.tensor_scalar(rt[:, :], rt[:, :], 1e-6, None, ALU.max)
                dve.drain()
                dve.reciprocal(rt[:, :], rt[:, :])
                dve.wait_ge(s_p0, 1)
                dve.drain()

                def by_head(ap, parts):
                    return ap.unsqueeze(2).broadcast_to([parts, HF, G])
                dve.tensor_tensor(WXS[:, :].rearrange("p (h g) -> p h g", g=G),
                                  PS[:, 0, :].rearrange("p (h g) -> p h g", g=G), by_head(rt[:, :], P), ALU.mult)
                r3 = row[:, :].rearrange("p (h g) -> p h g", g=G)
                dve.tensor_tensor(r3, PS[0:1, 1, :].rearrange("p (h g) -> p h g", g=G),
                                  bsl[:, :].unsqueeze(1).broadcast_to([1, HF, G]), ALU.add)
                dve.drain()
                dve.tensor_tensor(r3, r3, by_head(rt[0:1, :], 1), ALU.mult)
                dve.drain().then_inc(s_row, 1)
                dve.wait_ge(s_w3, 48)
                for k in range(KC):
                    dve.wait_ge(s_p2, 2 * k + 1)
                    dve.scalar_tensor_tensor(winl[:, k, 0:DI], Win[:, k, 0:DI], 0.5, winh[:, k, 0:DI],
                                             ALU.mult, ALU.subtract)
                    dve.tensor_tensor(winl[:, k, DI:], Win[:, k, DI:], winh[:, k, DI:], ALU.subtract)
                    dve.wait_ge(s_p2, 2 * k + 2)
                    dve.scalar_tensor_tensor(whol[:, k, :], Who[:, k, :], nw[:, k:k + 1], whoh[:, k, :],
                                             ALU.mult, ALU.subtract)
                dve.wait_ge(s_w2, 16 * NW2)
                dve.tensor_tensor(BFX[:, :], BFX[:, :], BFM[:, :], ALU.mult)
                dve.tensor_scalar(cw[:, :], cw[:, :], 0.5, None, ALU.mult)
                dve.tensor_scalar(cb[:, :], cb[:, :], 0.5, None, ALU.mult)
                dve.drain()
                dve.wait_ge(s_p1, 1)
                dve.tensor_scalar(nA[:, :], nA[:, :], -1.0, None, ALU.mult)
                ln_vector(C, dve, s_var, s_std)

            @block.gpsimd
            def _(pool):
                pool.wait_ge(s_row, 1)
                for src, w, dst in ((row, DI, LBP), (obr, P, OBP)):
                    for k in range(3):
                        pool.tensor_copy(rob[:, 0:w], src[:, 0:w])
                        pool.drain()
                        pool.tensor_copy(dst[32 * k:32 * k + 1, 0:w], rob[:, 0:w])
                        pool.tensor_tensor(src[:, 0:w], src[:, 0:w], rob[:, 0:w], ALU.subtract)
                        pool.drain()

            @block.scalar
            def _(act):
                act.wait_ge(s_w3, 48)
                for k in range(KC):
                    act.mul(winh[:, k, 0:DI], Win[:, k, 0:DI], 0.5)
                    act.copy(winh[:, k, DI:], Win[:, k, DI:]).then_inc(s_p2, 1)
                    act.mul(whoh[:, k, :], Who[:, k, :], nw[:, k:k + 1]).then_inc(s_p2, 1)
                act.wait_ge(s_w2, 16 * NW2)
                act.activation(nA[:, :], nA[:, :], ACT.Exp).then_inc(s_p1, 1)
                ln_scalar(C, act, s_var, s_std)

        xn = T("xn", [P, 2, P + 1])
        xnT = T("xnT", [P, P])
        nm = T("nm", [P, HF], BF16)
        mT = T("mT", [8, P], BF16)
        E = T("E", [P, DI])
        Z = T("Z", [P, HF])
        rZ = T("rZ", [P, HF])
        sw = T("sw", [P, 2, DI])
        swT = T("swT", [P, 2, GB, DI])
        rs = T("rs", [P, 4])
        sn = T("sn", [P, 4])
        RT = T("RT", [P, GB * KC])
        Tn = T("Tn", [P, DI])
        TT = T("TT", [P, GB, DI])
        R = T("R", [64, N])
        sth = T("sth", [P, KC, N], BF16)
        stl = T("stl", [P, KC, N], BF16)
        zs = T("zs", [P, KC, N])
        cx = T("cx", [P, KC, N])
        cB = T("cB", [64, 2, N])
        tn = T("tn", [P, 2, N])
        dv = T("dv", [P, 3, NT * 16])
        dtA = T("dtA", [P, NT * 16])
        xd = T("xd", [P, NT * 8])
        xdh = T("xdh", [8, N])
        Rf = T("Rf", [P, 2, N])
        Dec = T("Dec", [P, N])
        CBl = T("CBl", [P, NT, G])
        CBu = T("CBu", [P, NT, G])
        Wl = T("Wl", [P, N])
        Wu = T("Wu", [P, N])
        XX = T("XX", [P, 3, N])
        R8 = T("R8", [P, GB])
        UU = T("UU", [P, 2, DI])
        ygh, ygl, sq, otT = sth, stl, cx, cx

        (s_xn, s_tr, s_xnT, s_lg, s_nm, s_mt, s_mT, s_lm, s_E, s_sw, s_T, s_swt, s_swT, s_Tn, s_Tt, s_TT, s_rt, s_R,
         s_st, s_sth, s_stl, s_z, s_tz, s_zs, s_u, s_c0, s_c1, s_tc, s_cx, s_dt, s_v, s_sp, s_dv, s_Rf, s_seg, s_Dec,
         s_cb, s_CB, s_W, s_Wp, s_xt, s_xd, s_xq, s_xs, s_XX, s_Y, s_yg, s_ygh, s_ygl, s_ygd, s_sq, s_sqs, s_ss, s_ms, s_sd, s_R8, s_ot,
         s_otT, s_U, s_UU, s_UV, s_o, s_X, s_null) = (sem("b2_" + x) for x in
                      ("xn tr xnT lg nm mt mT lm E sw T swt swT Tn Tt TT rt R st sth stl z tz zs u c0 c1 tc cx dt v sp "
                       "dv Rf seg Dec cb CB W Wp xt xd xq xs XX Y yg ygh ygl ygd sq sqs ss ms sd R8 ot otT U UU UV o X null").split())

        POINTS = 4 * GB + 4

        def groups(eng, front, back):
            for k in range(POINTS):
                front(0, k, 0)
            if NG == 1:
                back(0, 0, False)
                return
            back(0, 0, True)
            mid = NG - 2
            if mid >= 2:
                with eng.Fori(0, mid // 2) as q:
                    back(q * 2 + 1, 1, True)
                    back(q * 2 + 2, 0, True)
            if mid % 2:
                back(NG - 2, (NG - 2) % 2, True)
            back(NG - 1, (NG - 1) % 2, False)

        def pair_cols(a, t):
            return a[:, :, t * P:(t + 1) * P]

        with nc.Block() as block:
            @block.tensor
            def _(pe):
                def front(g, k, par):
                    j, p = k // 4, k % 4
                    b = g * GB + j
                    if p == 0 and j < GB:
                        pe.wait_ge(s_xn, b + 1)
                        wait(pe, s_mT, b)
                        pe.transpose(PS[:, 4, 0:P], xn[:, j % 2, 0:P], IDF[:, :]).then_inc(s_tr, 1)
                    if p == 1:
                        if j < GB:
                            pe.wait_ge(s_xnT, b + 1)
                            wait(pe, s_E, b)
                            pe.matmul(PS[:, 5, :], xnT[:, :], WXS[:, :], start=True, stop=False)
                            pe.matmul(PS[:, 5, :], ONB[:, :], LBP[:, :], start=False, stop=True).then_inc(s_lg, 1)
                        if j >= 1:
                            wait(pe, s_sw, b)
                            wait(pe, s_Tn, b - 1)
                            wait(pe, s_TT, b - 1)
                            for c in range(KC):
                                o = PS[:, 6, c * 129:(c + 1) * 129] if c < 3 else PS[:, 4, 256:256 + 129]
                                last = pe.matmul(o, sw[:, (j - 1) % 2, c * P:(c + 1) * P], xn[:, (j - 1) % 2, :],
                                                 start=True, stop=True)
                            last.then_inc(s_T, 1)
                            for c in range(KC):
                                last = pe.transpose(PS[:, 7, c * P:(c + 1) * P], sw[:, (j - 1) % 2, c * P:(c + 1) * P],
                                                    IDF[:, :])
                            last.then_inc(s_swt, 1)
                    if p == 2 and j < GB:
                        pe.wait_ge(s_nm, b + 1)
                        wait(pe, s_Tn, b)
                        pe.transpose(PS[0:8, 4, 0:P // 2].bitcast(BF16), nm[:, :], IDB[:, :]).then_inc(s_mt, 1)
                    if p == 3:
                        if j >= 1:
                            wait(pe, s_Tn, b)
                            wait(pe, s_swT, b)
                            for c in range(KC):
                                last = pe.transpose(PS[:, 7, c * P:(c + 1) * P], Tn[:, c * P:(c + 1) * P], IDF[:, :])
                            last.then_inc(s_Tt, 1)
                        if j < GB:
                            pe.wait_ge(s_mT, b + 1)
                            pe.matmul(PS[:, 5, :], mT[:, :], SELH[:, :], start=False, stop=True,
                                      skip_group_check=True).then_inc(s_lm, 1)

                def back(g, par, more):
                    pts = [0]

                    def point():
                        if more and pts[0] < POINTS:
                            front(g + 1, pts[0], 1 - par)
                        pts[0] += 1

                    def split3(o, wh_, wl_, xh_, xl_, s, n=KC, arrive=None):
                        for k in range(n):
                            if arrive is not None:
                                pe.wait_ge(s_stl, arrive + k + 1)
                            pe.matmul(o, wh_(k), xh_(k), start=(k == 0), stop=False)
                            pe.matmul(o, wh_(k), xl_(k), start=False, stop=False)
                            last = pe.matmul(o, wl_(k), xh_(k), start=False, stop=(k == n - 1))
                        if s is not None:
                            last.then_inc(s, 1)
                        return last

                    wait(pe, s_X, g * GB)
                    pe.sem_inc(s_null, 1)
                    pe.transpose(PS[0:32, 2, 0:64], RT[0:64, :], IDF[0:64, 0:64])
                    pe.transpose(PS[0:32, 3, 0:64], RT[64:128, :], IDF[64:128, 64:128]).then_inc(s_rt, 1)
                    wait(pe, s_TT, g * GB + GB)
                    wait(pe, s_UU, g * GB)
                    wait(pe, s_UV, g * GB)

                    def tokens(c):
                        for h2 in range(2):
                            h = 2 * c + h2
                            pe.matmul(PS[64 * h2:64 * h2 + 64, c, :], WfxT[:, h * 64:h * 64 + 64],
                                      TT[:, :, h * G:(h + 1) * G], start=True, stop=False)

                    def bias(c):
                        pe.matmul(PS[:, c, :], BFX[:, c * P:(c + 1) * P], R[:, :], start=False,
                                  stop=True).then_inc(s_st, 1)
                    tokens(0)
                    tokens(1)
                    pe.wait_ge(s_R, g + 1)
                    bias(0)
                    bias(1)
                    point()
                    for c in (2, 3):
                        tokens(c)
                        bias(c)
                    point()
                    for m in range(9):
                        if 4 <= m < 8:
                            wait(pe, s_zs, g * 4 + m - 3)
                        elif m == 8:
                            pe.wait_ge(s_c1, g * 5 + 1)
                        split3(PS[:, m % 4, :], lambda k: winh[:, k, m * P:(m + 1) * P],
                               lambda k: winl[:, k, m * P:(m + 1) * P], lambda k: sth[:, k, :],
                               lambda k: stl[:, k, :], s_z if m < 4 else s_u, arrive=g * 4 if m == 0 else None)
                        point()
                    pe.wait_ge(s_c1, g * 5 + 2)
                    for t in range(NT):
                        q = slice(t * P, (t + 1) * P)
                        last = split3(PS[:, 1, t * 16:(t + 1) * 16], lambda k: sth[:, k, q], lambda k: stl[:, k, q],
                                      lambda k: winh[:, k, 1152:1168], lambda k: winl[:, k, 1152:1168], None)
                    last.then_inc(s_dt, 1)
                    point()
                    pe.wait_ge(s_c1, g * 5 + 3)
                    for k in range(KC):
                        pe.wait_ge(s_cx, g * 5 + k + 1)
                        last = pe.matmul(PS[0:8, 2, :], fcT[:, k * 8:(k + 1) * 8], cx[:, k, :],
                                         start=(k == 0), stop=(k == KC - 1))
                    last.then_inc(s_xq, 1)
                    pe.wait_ge(s_cx, g * 5 + 5)
                    pe.sem_inc(s_null, 1)
                    for j in range(GB):
                        last = pe.matmul(PS[64 * (j % 2):64 * (j % 2) + 64, 3, (j // 2) * G:(j // 2 + 1) * G],
                                         cB[:, 0, j * G:(j + 1) * G], cB[:, 1, j * G:(j + 1) * G], start=True, stop=True)
                    last.then_inc(s_cb, 1)
                    point()
                    pe.wait_ge(s_xs, g + 1)
                    pe.sem_inc(s_null, 1)
                    for t in range(NT):
                        last = pe.transpose(PS[:, 2, t * 8:(t + 1) * 8], xdh[:, t * P:(t + 1) * P], IDF[0:8, 0:8])
                    last.then_inc(s_xd, 1)
                    for t in range(NT):
                        n = g * NT + t
                        pe.wait_ge(s_Rf, n * 2 + 1)
                        wait(pe, s_Dec, n)
                        pe.matmul(PS[:, 0, :], UF[:, :], Rf[:, 0, :], start=True, stop=False)
                        pe.wait_ge(s_Rf, n * 2 + 2)
                        pe.matmul(PS[:, 0, :], UB[:, :], Rf[:, 1, :], start=False, stop=True).then_inc(s_seg, 1)
                        wait(pe, s_XX, n * 3)
                        pe.wait_ge(s_v, g + 1)
                        for c in range(KC):
                            last = pe.transpose(PS[:, 1, c * P:(c + 1) * P], cx[:, c, t * P:(t + 1) * P], IDF[:, :])
                        last.then_inc(s_xt, 1)
                        point()
                        if t == 0:
                            pe.wait_ge(s_CB, g + 1)
                        for r in range(2):
                            wait(pe, s_yg, (n - 1) * 2 + r + 1)
                            q = slice(64 * r, 64 * r + 64)
                            pe.wait_ge(s_XX, n * 3 + 1)
                            for c in range(KC):
                                pe.matmul(PS[:, 2 + r, c * G:(c + 1) * G], XX[q, 2, c * P:(c + 1) * P],
                                          IDF[q, 64 * r:64 * r + 64], start=(c == 0), stop=False,
                                          skip_group_check=True)
                            if r == 0:
                                pe.wait_ge(s_XX, n * 3 + 3)
                                pe.wait_ge(s_W, n + 1)
                                pe.wait_ge(s_Wp, n + 1)
                                pe.sem_inc(s_null, 1)
                            for h in range(HF):
                                h2 = h % 2
                                o = PS[64 * h2:64 * h2 + 64, 2 + r, (h // 2) * G:(h // 2 + 1) * G]
                                for d, Wd in enumerate((Wl, Wu)):
                                    last = pe.matmul(o, XX[q, d, h * 64:(h + 1) * 64], Wd[q, h * G:(h + 1) * G],
                                                     start=False, stop=(d == 1), skip_group_check=True)
                            last.then_inc(s_Y, 1)
                        point()
                        point()
                        point()
                    pe.wait_ge(s_ygl, g * (NT - 1) + NT - 1)
                    pe.wait_ge(s_ygd, g + 1)
                    for i in range(KC):
                        m = (i + 1) % KC
                        if i == 2:
                            pe.wait_ge(s_sqs, g * NT + NT)
                            for w in range(-1, GB):
                                lo, hi = max(w, 0), min(w + 2, GB)
                                q = slice(64 * (lo - w), 64 * (hi - w))
                                last = pe.matmul(PS[q, 0, w + 1:w + 2], sq[:, 0, lo * G:hi * G], ON1[:, :],
                                                 start=True, stop=True)
                            last.then_inc(s_ss, 1)
                        if m == 0:
                            pe.wait_ge(s_ms, g + 1)
                        split3(PS[:, m, :], lambda k: whoh[:, k, m * P:(m + 1) * P],
                               lambda k: whol[:, k, m * P:(m + 1) * P], lambda k: ygh[:, k, :],
                               lambda k: ygl[:, k, :], s_ot)
                        point()
                    pe.wait_ge(s_otT, g * 4 + 4)
                    for j in range(GB + 1):
                        if j < GB:
                            b = g * GB + j
                            wait(pe, s_UU, b)
                            wait(pe, s_UV, b)
                            pe.sem_inc(s_null, 1)
                            for c in range(KC):
                                for h2 in range(2):
                                    q = slice(64 * h2, 64 * h2 + 64)
                                    last = pe.matmul(PS[q, h2, c * P:(c + 1) * P], otT[q, c, j * G:(j + 1) * G],
                                                     WoT2[q, c * P:(c + 1) * P], start=True, stop=True)
                            last.then_inc(s_U, 1)
                            point()
                        if j >= 1:
                            b = g * GB + j - 1
                            pe.wait_ge(s_UU, b + 1)
                            pe.wait_ge(s_UV, b + 1)
                            wait(pe, s_X, b - 1)
                            o = PS[:, 2 + (j - 1) % 2, 0:P]
                            pe.matmul(o, ONB[:, :], OBP[:, :], start=True, stop=False)
                            for c in range(KC):
                                last = pe.matmul(o, swT[:, par, j - 1, c * P:(c + 1) * P],
                                                 UU[:, (j - 1) % 2, c * P:(c + 1) * P], start=False, stop=(c == KC - 1))
                            last.then_inc(s_o, 1)
                    assert pts[0] >= POINTS
                groups(pe, front, back)

            @block.vector
            def _(dve):
                dve.memset(xn[:, :, P:P + 1], 1.0)
                dve.memset(CBl[:, :, :], 0.0)
                dve.memset(CBu[:, :, :], 0.0)
                dve.drain()

                def norm(g, j):
                    b = g * GB + j
                    wait(dve, s_T, b - 1)
                    normalise(C, dve, xn[:, j % 2, 0:P], b).then_inc(s_xn, 1)

                def front(g, k, par):
                    j, p = k // 4, k % 4
                    b = g * GB + j
                    if p == 0:
                        if j == 0:
                            norm(g, 0)
                        if j >= 1:
                            i = (j - 1) % 2
                            wait(dve, s_E, b)
                            e3 = E[:, :].rearrange("p (h g) -> p h g", g=G)
                            dve.tensor_reduce(Z[:, :], e3, AX.X, ALU.add)
                            dve.drain()
                            dve.reciprocal(rZ[:, :], Z[:, :])
                            dve.drain()
                            wait(dve, s_swt, b - 2)
                            dve.tensor_tensor(sw[:, i, :].rearrange("p (h g) -> p h g", g=G), e3,
                                              rZ[:, :].unsqueeze(2).broadcast_to([P, HF, G]), ALU.mult).then_inc(s_sw, 1)
                    if p == 1 and j < GB:
                        dve.wait_ge(s_lg, b + 1)
                        wait(dve, s_mt, b)
                        dve.tensor_reduce(nm[:, :], PS[:, 5, :].rearrange("p (h g) -> p h g", g=G),
                                          AX.X, ALU.max, negate=True).then_inc(s_nm, 1)
                    if p == 2 and j >= 1:
                        wait(dve, s_T, b)
                        t3 = PS[:, 6, 0:387].rearrange("p (c n) -> p c n", n=129)
                        dve.tensor_copy(sn[:, 0:3], t3[:, :, P])
                        dve.tensor_copy(sn[:, 3:4], PS[:, 4, 256 + P:257 + P])
                        dve.drain()
                        dve.tensor_scalar(rs[:, :], sn[:, :], 1e-5, None, ALU.add)
                        dve.drain()
                        dve.reciprocal(rs[:, :], rs[:, :])
                        dve.drain()
                        wait(dve, s_Tt, b - 1)
                        dve.tensor_tensor(Tn[:, 0:384].rearrange("p (c n) -> p c n", n=P), t3[:, :, 0:P],
                                          rs[:, 0:3].unsqueeze(2).broadcast_to([P, 3, P]), ALU.mult)
                        dve.tensor_scalar(Tn[:, 384:512], PS[:, 4, 256:256 + P], rs[:, 3:4], None, ALU.mult)
                        if j == 1:
                            wait(dve, s_rt, g)
                        dve.tensor_tensor(RT[:, (j - 1) * KC:j * KC], sn[:, :], rs[:, :], ALU.mult)
                        dve.drain().then_inc(s_Tn, 1)
                    if p == 3 and j < GB - 1:
                        norm(g, j + 1)

                def back(g, par, more):
                    pts = [0]

                    def point():
                        if more and pts[0] < POINTS:
                            front(g + 1, pts[0], 1 - par)
                        pts[0] += 1

                    dve.wait_ge(s_rt, g + 1)
                    wait(dve, s_st, g * 4)
                    for h2 in range(2):
                        last = dve.tensor_tensor(R[32 * h2:32 * h2 + 32, :].rearrange("p (b g) -> p b g", g=G),
                                                 PS[0:32, 2 + h2, 0:G].unsqueeze(1).broadcast_to([32, GB, G]),
                                                 Rm[:, :].unsqueeze(2).broadcast_to([32, GB, G]), ALU.mult)
                    last.then_inc(s_R, 1)

                    def token_low(c):
                        dve.wait_ge(s_sth, g * 4 + c + 1)
                        dve.tensor_tensor(stl[:, c, :], PS[:, c, :], sth[:, c, :], ALU.subtract).then_inc(s_stl, 1)
                    point()
                    token_low(0)
                    token_low(1)
                    token_low(2)
                    token_low(3)
                    point()

                    def gate(m):
                        dve.wait_ge(s_tz, g * 4 + m + 1)
                        dve.scalar_tensor_tensor(zs[:, m, :], tn[:, m % 2, :], 1.0, PS[:, m, :], ALU.add, ALU.mult)\
                           .then_inc(s_zs, 1)

                    def taps(m):
                        dve.wait_ge(s_c0, g * 5 + m + 1)
                        u = PS[:, m % 4, :].rearrange("p (b l) -> p b l", l=G)
                        dst = (cx[:, m, :] if m < KC else Dec[:, :]).rearrange("p (b l) -> p b l", l=G)
                        dve.scalar_tensor_tensor(dst[:, :, 1:], u[:, :, 0:G - 1], cw[:, 3 * m + 1:3 * m + 2],
                                                 dst[:, :, 1:], ALU.mult, ALU.add)
                        dve.drain()
                        dve.scalar_tensor_tensor(dst[:, :, 2:], u[:, :, 0:G - 2], cw[:, 3 * m:3 * m + 1],
                                                 dst[:, :, 2:], ALU.mult, ALU.add)
                        dve.drain().then_inc(s_c1, 1)

                    def silu(m):
                        dve.wait_ge(s_tc, g * 5 + m + 1)
                        if m < KC:
                            dve.scalar_tensor_tensor(cx[:, m, :], tn[:, m % 2, :], 1.0, cx[:, m, :], ALU.add, ALU.mult)\
                               .then_inc(s_cx, 1)
                        else:
                            for i in range(2):
                                q = slice(64 * i, 64 * i + 64)
                                last = dve.scalar_tensor_tensor(cB[:, i, :], tn[q, m % 2, :], 1.0, Dec[q, :],
                                                                ALU.add, ALU.mult)
                            dve.drain().then_inc(s_cx, 1)
                    for m in range(4):
                        point()
                        gate(m)
                    for m in range(5):
                        point()
                        taps(m)
                        if m >= 1:
                            silu(m - 1)
                    dve.wait_ge(s_dt, g + 1)
                    wait(dve, s_Rf, g * NT * 2)
                    v, e, l = dv[:, 0, :], dv[:, 1, :], dv[:, 2, :]
                    v3 = v.rearrange("p (t h) -> p t h", h=16)
                    dve.tensor_tensor(v3, PS[:, 1, 0:NT * 16].rearrange("p (t h) -> p t h", h=16),
                                      dtb[:, :].unsqueeze(1).broadcast_to([P, NT, 16]), ALU.add)
                    dve.drain().then_inc(s_v, 1)
                    dve.scalar_tensor_tensor(e, v, -1.0, v, ALU.mult, ALU.max)
                    dve.drain().then_inc(s_dv, 1)
                    silu(4)
                    dve.wait_ge(s_sp, g + 1)
                    dve.scalar_tensor_tensor(v, v, 0.0, l, ALU.max, ALU.add)
                    dve.drain()
                    dve.tensor_tensor(dtA[:, :].rearrange("p (t h) -> p t h", h=16), v3,
                                      nA[:, :].unsqueeze(1).broadcast_to([P, NT, 16]), ALU.mult)
                    dve.drain().then_inc(s_dv, 1)
                    point()
                    dve.wait_ge(s_xd, g + 1)
                    dve.tensor_tensor(xd[:, :].rearrange("p (t h) -> p t h", h=8),
                                      PS[:, 2, 0:NT * 8].rearrange("p (t h) -> p t h", h=8),
                                      Dp[:, :].unsqueeze(1).broadcast_to([P, NT, 8]), ALU.add)
                    dve.wait_ge(s_cb, g + 1)
                    wait(dve, s_Wp, g * NT)
                    cbp = PS[:, 3, 0:NT * G].rearrange("p (t l) -> p t l", l=G)
                    dve.tensor_tensor(CBl[:, :, 1:], cbp[:, :, 0:G - 1],
                                      LTM[:, 1:].unsqueeze(1).broadcast_to([P, NT, G - 1]), ALU.mult)
                    dve.tensor_tensor(CBu[:, :, 0:G - 1], cbp[:, :, 1:],
                                      UTM[:, 0:G - 1].unsqueeze(1).broadcast_to([P, NT, G - 1]), ALU.mult)
                    dve.drain().then_inc(s_CB, 1)
                    point()
                    for t in range(NT):
                        n = g * NT + t
                        dve.wait_ge(s_xt, n + 1)
                        wait(dve, s_Y, n * 2)
                        x3 = PS[:, 1, :].rearrange("p (h c) -> p h c", c=64)
                        for i, s in ((2, xd[:, t * 8:t * 8 + 8]), (0, v[:, t * 16:t * 16 + 8]),
                                     (1, v[:, t * 16 + 8:t * 16 + 16])):
                            dve.tensor_tensor(XX[:, i, :].rearrange("p (h c) -> p h c", c=64), x3,
                                              s.unsqueeze(2).broadcast_to([P, 8, 64]), ALU.mult).then_inc(s_XX, 1)
                        dve.wait_ge(s_Dec, n + 1)
                        dve.tensor_tensor(Wl[:, :].rearrange("p (h l) -> p h l", l=G),
                                          Dec[:, :].rearrange("p (h l) -> p h l", l=G),
                                          CBl[:, t, :].unsqueeze(1).broadcast_to([P, 8, G]), ALU.mult).then_inc(s_W, 1)
                        point()
                        point()
                        for r in range(2):
                            dve.wait_ge(s_Y, n * 2 + r + 1)
                            z4 = zs[:, :, (2 * t + r) * G:(2 * t + r + 1) * G]
                            dve.tensor_tensor(z4, PS[:, 2 + r, 0:256].rearrange("p (c l) -> p c l", l=G), z4,
                                              ALU.mult).then_inc(s_yg, 1)
                        point()
                        if t == NT - 1:
                            dve.wait_ge(s_ygh, n + 1)
                            dve.tensor_tensor(pair_cols(ygl, t), pair_cols(zs, t), pair_cols(ygh, t),
                                              ALU.subtract).then_inc(s_ygd, 1)
                        point()
                    point()
                    point()
                    dve.wait_ge(s_ss, g + 1)
                    wait(dve, s_UU, g * GB)
                    for h2 in range(2):
                        q = slice(64 * h2, 64 * h2 + 64)
                        dve.tensor_scalar(R8[q, :], PS[q, 0, 1 - h2:1 - h2 + GB], 1.0 / DI, 1e-5, ALU.mult, ALU.add)
                    dve.drain().then_inc(s_ms, 1)
                    point()
                    dve.wait_ge(s_sd, g + 1)
                    dve.reciprocal(R8[:, :], R8[:, :])
                    dve.drain().then_inc(s_R8, 1)
                    point()
                    for j in range(GB + 1):
                        if j < GB:
                            b = g * GB + j
                            dve.wait_ge(s_U, b + 1)
                            wait(dve, s_o, b - 1)
                            dve.tensor_scalar(UU[64:128, j % 2, :], PS[64:128, 1, :], R8[64:128, j:j + 1],
                                              None, ALU.mult).then_inc(s_UV, 1)
                            point()
                        if j >= 1:
                            b = g * GB + j - 1
                            dve.wait_ge(s_o, b + 1)
                            dve.tensor_tensor(C["xs"](b), PS[:, 2 + (j - 1) % 2, 0:P], C["xs"](b), ALU.add).then_inc(s_X, 1)
                            dve.drain()
                            dve.bn_stats(C["ST"][:, ds(b * 6, 6)], C["xs"](b))
                groups(dve, front, back)

            @block.gpsimd
            def _(pool):
                def ranges(n, t):
                    wait(pool, s_seg, n)
                    for d, M in enumerate((LTM, UTM)):
                        pool.tensor_tensor(
                            Rf[:, d, :].rearrange("p (h l) -> p h l", l=G),
                            dtA[:, t * 16 + 8 * d:t * 16 + 8 * d + 8].unsqueeze(2).broadcast_to([P, 8, G]),
                            M[:, :].unsqueeze(1).broadcast_to([P, 8, G]), ALU.mult).then_inc(s_Rf, 1)

                def back(g):
                    pool.wait_ge(s_dv, g * 2 + 2)
                    ranges(g * NT, 0)
                    for t in range(NT):
                        n = g * NT + t
                        if t == 0:
                            pool.wait_ge(s_CB, g + 1)
                        pool.wait_ge(s_Dec, n + 1)
                        wait(pool, s_Y, n * 2)
                        pool.tensor_tensor(Wu[:, :].rearrange("p (h l) -> p h l", l=G),
                                           Dec[:, :].rearrange("p (h l) -> p h l", l=G),
                                           CBu[:, t, :].unsqueeze(1).broadcast_to([P, 8, G]), ALU.mult).then_inc(s_Wp, 1)
                        if t < NT - 1:
                            ranges(n + 1, t + 1)
                        if t >= 1:
                            low(n - 1, t - 1)
                    low(g * NT + NT - 1, NT - 1)

                def low(n, t):
                    if t < NT - 1:
                        pool.wait_ge(s_ygh, n + 1)
                        pool.tensor_tensor(pair_cols(ygl, t), pair_cols(zs, t), pair_cols(ygh, t),
                                           ALU.subtract).then_inc(s_ygl, 1)
                    pool.wait_ge(s_sq, n + 1)
                    s4 = pair_cols(sq, t)
                    pool.tensor_tensor(s4[:, 0:2, :], s4[:, 0:2, :], s4[:, 2:4, :], ALU.add)
                    pool.drain()
                    pool.tensor_tensor(s4[:, 0, :], s4[:, 0, :], s4[:, 1, :], ALU.add).then_inc(s_sqs, 1)
                back(0)
                if NG > 1:
                    with pool.Fori(1, NG) as g:
                        back(g)

            @block.scalar
            def _(act):
                def front(g, k, par):
                    j, p = k // 4, k % 4
                    b = g * GB + j
                    if p == 0 and j < GB:
                        act.wait_ge(s_tr, b + 1)
                        wait(act, s_lg, b)
                        act.copy(xnT[:, :], PS[:, 4, 0:P]).then_inc(s_xnT, 1)
                    if p == 1 and j >= 1:
                        wait(act, s_swt, b)
                        if j == 1:
                            wait(act, s_o, (g - 1) * GB)
                        act.copy(swT[:, par, j - 1, :], PS[:, 7, :]).then_inc(s_swT, 1)
                    if p == 2 and j < GB:
                        act.wait_ge(s_mt, b + 1)
                        wait(act, s_lm, b)
                        act.copy(mT[:, :], PS[0:8, 4, 0:P // 2].bitcast(BF16)).then_inc(s_mT, 1)
                    if p == 3:
                        if j < GB:
                            act.wait_ge(s_lm, b + 1)
                            wait(act, s_sw, b)
                            act.activation(E[:, :], PS[:, 5, :], ACT.Exp).then_inc(s_E, 1)
                        if j >= 1:
                            wait(act, s_Tt, b)
                            if j == 1:
                                wait(act, s_st, g * 4)
                            act.copy(TT[:, j - 1, :], PS[:, 7, :]).then_inc(s_TT, 1)

                def back(g, par, more):
                    pts = [0]

                    def point():
                        if more and pts[0] < POINTS:
                            front(g + 1, pts[0], 1 - par)
                        pts[0] += 1

                    for c in range(KC):
                        act.wait_ge(s_st, g * 4 + c + 1)
                        wait(act, s_ot, g * 4)
                        act.copy(sth[:, c, :], PS[:, c, :]).then_inc(s_sth, 1)
                        if c % 2:
                            point()
                    for m in range(KC):
                        act.wait_ge(s_z, g * 4 + m + 1)
                        if m < 2:
                            wait(act, s_cx, g * 5)
                        else:
                            wait(act, s_zs, g * 4 + m - 1)
                        act.activation(tn[:, m % 2, :], PS[:, m, :], ACT.Tanh).then_inc(s_tz, 1)
                        point()

                    def tap(m):
                        act.wait_ge(s_u, g * 5 + m + 1)
                        if m < KC:
                            wait(act, s_U, g * GB)
                        else:
                            wait(act, s_W, g * NT)
                            wait(act, s_Wp, g * NT)
                        act.activation(cx[:, m, :] if m < KC else Dec[:, :], PS[:, m % 4, :], ACT.Identity,
                                       bias=cb[:, m:m + 1], scale=cw[:, 3 * m + 2:3 * m + 3]).then_inc(s_c0, 1)

                    def tanh(m):
                        act.wait_ge(s_c1, g * 5 + m + 1)
                        if m < 2:
                            act.wait_ge(s_zs, g * 4 + m + 3)
                        else:
                            wait(act, s_cx, g * 5 + m - 1)
                        act.activation(tn[:, m % 2, :], cx[:, m, :] if m < KC else Dec[:, :], ACT.Tanh).then_inc(s_tc, 1)
                    for m in range(5):
                        tap(m)
                        if m >= 1:
                            tanh(m - 1)
                        point()
                    tanh(4)
                    act.wait_ge(s_dv, g * 2 + 1)
                    act.activation(dv[:, 1, :], dv[:, 1, :], ACT.Exp, scale=-1.0)
                    act.drain()
                    act.activation(dv[:, 2, :], dv[:, 1, :], ACT.Ln, bias=1.0).then_inc(s_sp, 1)
                    act.wait_ge(s_xq, g + 1)
                    wait(act, s_xd, g)
                    act.copy(xdh[:, :], PS[0:8, 2, :]).then_inc(s_xs, 1)
                    point()
                    point()
                    for t in range(NT):
                        n = g * NT + t
                        act.wait_ge(s_seg, n + 1)
                        wait(act, s_W, n)
                        wait(act, s_Wp, n)
                        act.activation(Dec[:, :], PS[:, 0, :], ACT.Exp).then_inc(s_Dec, 1)
                        first = 2 if t == NT - 1 else 4
                        for r in range(first):
                            point()
                        act.wait_ge(s_yg, n * 2 + 2)
                        act.copy(pair_cols(ygh, t), pair_cols(zs, t)).then_inc(s_ygh, 1)
                        act.activation(pair_cols(sq, t), pair_cols(zs, t), ACT.Square).then_inc(s_sq, 1)
                        for r in range(first, 4):
                            point()
                    for i in range(KC):
                        m = (i + 1) % KC
                        if i == 2:
                            act.wait_ge(s_ms, g + 1)
                            act.activation(R8[:, :], R8[:, :], ACT.Sqrt).then_inc(s_sd, 1)
                        act.wait_ge(s_ot, g * 4 + i + 1)
                        if i == 0:
                            act.wait_ge(s_sqs, g * NT + NT)
                        act.copy(otT[:, m, :], PS[:, m, :]).then_inc(s_otT, 1)
                        point()
                    for j in range(GB):
                        b = g * GB + j
                        act.wait_ge(s_U, b + 1)
                        if j == 0:
                            act.wait_ge(s_R8, g + 1)
                        wait(act, s_o, b - 1)
                        act.mul(UU[0:64, j % 2, :], PS[0:64, 0, :], R8[0:64, j:j + 1]).then_inc(s_UU, 1)
                        point()
                groups(act, front, back)


def expert_tiles(C, ctx):
    B, tile = C["B"], C["tile"]
    C["M"] = dict(
        w13=tile(ctx, "d_w13", [P, 2 * NH1]),
        w2=tile(ctx, "d_w2", [P, E8 * 3 * P]),
        wh=tile(ctx, "d_wh", [P, 2, NH1], BF16),
        wl=tile(ctx, "d_wl", [P, 2, NH1], BF16),
        w2h=tile(ctx, "d_w2h", [P, E8 * 3 * P], BF16),
        w2l=tile(ctx, "d_w2l", [P, E8 * 3 * P], BF16),
        rw=tile(ctx, "d_rw", [P, E8]),
        r8=tile(ctx, "d_r8", [P, E8]),
        LG=tile(ctx, "d_LG", [P, B * E8]))



def gnn1(C):
    nc, io, B, NQ, sem, tile, PS = C["nc"], C["io"], C["B"], C["NQ"], C["sem"], C["tile"], C["PS"]
    IDF = C["IDF"]
    WC = P + 2
    with ExitStack() as ctx:
        VS = tile(ctx, "c_VS", [P, B * WC])
        V3 = VS[:, :].rearrange("p (b w) -> p b w", w=WC)
        cf = tile(ctx, "c_cf", [P, B])
        bf = tile(ctx, "c_bf", [P, B])
        KT = tile(ctx, "c_KT", [P, NQ * P], BF16)
        sel = tile(ctx, "c_sel", [P, 4 * P], BF16)
        MT = tile(ctx, "c_MT", [P, P])
        adj = tile(ctx, "c_adj", [P, P], I32)
        mf = tile(ctx, "c_mf", [P, P])
        av = tile(ctx, "c_av", [P, 2 * P])
        tmp = tile(ctx, "c_tmp", [P, P])
        WT = tile(ctx, "c_WT", [P, P])
        s_wd, s_mt, s_sl, s_wst = (sem("c_" + x) for x in ("wd", "mt", "sl", "wst"))
        M = C["M"]
        w13, w2, w2h, w2l = (M[k] for k in ("w13", "w2", "w2h", "w2l"))

        class Load:
            count, zcount = 16, 1

            def __call__(self, block, W, s_w, s_wz):
                self.W, self.s_w, self.s_wz = W, s_w, s_wz

                @block.sync
                def _(sp):
                    sp.dma_start(W[:, 0:P], io["cW"]).then_inc(s_w, 16)
                    sp.dma_start(av[:, :], io["ca"].partition_broadcast(P)).then_inc(s_wd, 16)
                    sp.dma_start(adj[:, :], io["adj"]).then_inc(s_wd, 16)
                    sp.dma_start(sel[:, :], io["c_sel"][:, 0:4 * P]).then_inc(s_sl, 16)
                    sp.dma_start(w2[:, :], io["dw2"]).then_inc(s_wst, 16)
                    sp.dma_start(M["rw"][:, :], io["drw"]).then_inc(s_sl, 16)
                    sp.dma_start(M["r8"][:, :], io["c_r8"].partition_broadcast(P)).then_inc(s_sl, 16)
                    sp.dma_start(w13[:, 0:NH1], io["dw1"]).then_inc(s_sl, 16)
                    sp.dma_start(w13[:, NH1:2 * NH1], io["dw3"]).then_inc(s_sl, 16)
                    sp.wait_ge(s_sl, 80)

                @block.gpsimd
                def _(pool):
                    pool.wait_ge(s_wst, 16)
                    pool.tensor_copy(w2h[:, :], w2[:, :])
                    pool.drain()
                    pool.tensor_tensor(w2l[:, :], w2[:, :], w2h[:, :], ALU.subtract)

            def vector(self, dve):
                dve.wait_ge(self.s_w, 16)
                dve.wait_ge(s_wd, 32)
                for k in range(2):
                    dve.tensor_tensor(tmp[:, :], self.W[:, 0:P], av[:, k * P:(k + 1) * P], ALU.mult)
                    dve.drain()
                    dve.tensor_reduce(self.W[:, P + k:P + k + 1], tmp[:, :], AX.X, ALU.add)
                    dve.drain()
                dve.sem_inc(self.s_wz, 1)
                dve.tensor_copy(mf[:, :], adj[:, :])
                dve.drain()
                dve.tensor_scalar(mf[:, :], mf[:, :], 0.0, None, ALU.is_gt)

        project(C, "c_", ctx, WC, Load(), VS)
        with nc.Block() as block:
            @block.tensor
            def _(pe):
                pe.transpose(PS[:, 0, 0:P], mf[:, :], IDF[:, :]).then_inc(s_mt, 1)

            @block.vector
            def _(dve):
                dve.wait_ge(s_mt, 1)
                dve.tensor_copy(MT[:, :], PS[:, 0, 0:P])
        with ExitStack() as c2:
            factors(C, "c_", c2, V3[:, :, P:P + 1], V3[:, :, P + 1:P + 2], 1, cf[:, :], bf[:, :], KT)

        with ExitStack() as c2:
            W1 = P + 1
            WQ = 2 * NH1 // NQ
            assert WQ * NQ == 2 * NH1
            whf, wlf = (M[k][:, :, :].rearrange("p k n -> p (k n)") for k in ("wh", "wl"))
            VX = tile(c2, "c_VX", [P, 2, 4 * W1])
            PT = tile(c2, "c_PT", [P, 2, 4 * P])
            rec = tile(c2, "c_rec", [P, 2, 4])
            ex = tile(c2, "c_ex", [P, 2, 4 * P])
            pos = tile(c2, "c_pos", [P, 2, 4 * P])
            XB = tile(c2, "c_XB", [P, 2, 4, P])
            XT = tile(c2, "c_XT", [P, 2, 4 * P])
            s_vx, s_K, s_pt, s_av, s_rc, s_ex, s_res, s_xb, s_xt, s_xc, s_lg, s_lc = (
                sem("c2_" + x) for x in ("vx", "K", "pt", "av", "rc", "ex", "res", "xb", "xt", "xc", "lg", "lc"))

            def sums(r):
                return PS[:, 2 + 2 * (r % 2):4 + 2 * (r % 2), 0:2 * W1].rearrange("p k (j w) -> p k j w", w=W1)

            with nc.Block() as block:
                @block.gpsimd
                def _(pool):
                    def values(q, r):
                        wait(pool, s_av, q - 1)
                        vx = VX[:, r % 2, :].rearrange("p (j w) -> p j w", w=W1)
                        v = VS[:, ds(q * 4 * WC, 4 * WC)].rearrange("p (j w) -> p j w", w=WC)
                        bb = bf[:, ds(q * 4, 4)]
                        pool.tensor_tensor(vx[:, :, 0:P], v[:, :, 0:P], bb.unsqueeze(2).broadcast_to([P, 4, P]),
                                           ALU.mult)
                        pool.tensor_copy(vx[:, :, P], bb)
                        pool.drain().then_inc(s_vx, 1)

                    def split(q, r):
                        o = ds(q * WQ, WQ)
                        pool.tensor_copy(whf[:, o], w13[:, o])
                        pool.drain()
                        pool.tensor_tensor(wlf[:, o], w13[:, o], whf[:, o], ALU.subtract)
                    pipelined(pool, NQ, 2, [(0, values), (0, split)])

                @block.tensor
                def _(pe):
                    def spread(q, r):
                        wait(pe, s_pt, q - 1)
                        for j in range(4):
                            last = pe.matmul(PS[:, r % 2, j * P:(j + 1) * P], sel[0:96, j * P:(j + 1) * P],
                                             KT[0:96, ds(q * P, P)], start=True, stop=True)
                        last.then_inc(s_K, 1)

                    def attend(q, r):
                        pe.wait_ge(s_pt, q + 1)
                        pe.wait_ge(s_vx, q + 1)
                        wait(pe, s_ex, q - 1)
                        for j in range(4):
                            last = pe.matmul(PS[:, 2 + 2 * (r % 2) + j // 2, (j % 2) * W1:(j % 2 + 1) * W1],
                                             PT[:, r % 2, j * P:(j + 1) * P], VX[:, r % 2, j * W1:(j + 1) * W1],
                                             start=True, stop=True)
                        last.then_inc(s_av, 1)

                    def turn(q, r):
                        pe.wait_ge(s_xb, q + 1)
                        wait(pe, s_xc, q)
                        for j in range(4):
                            last = pe.transpose(PS[:, 6, j * P:(j + 1) * P], XB[:, r % 2, j, :], IDF[:, :])
                        last.then_inc(s_xt, 1)

                    def route(q, r):
                        pe.wait_ge(s_xc, q + 1)
                        wait(pe, s_lc, q)
                        for j in range(4):
                            last = pe.matmul(PS[:, 7, j * E8:(j + 1) * E8], XT[:, r % 2, j * P:(j + 1) * P],
                                             M["rw"][:, :], start=True, stop=True)
                        last.then_inc(s_lg, 1)
                    pipelined(pe, NQ, 2, [(0, spread), (1, attend), (4, turn), (5, route)])

                @block.vector
                def _(dve):
                    def weights(q, r):
                        dve.wait_ge(s_K, q + 1)
                        wait(dve, s_av, q - 1)
                        for j in range(4):
                            last = dve.scalar_tensor_tensor(PT[:, r % 2, j * P:(j + 1) * P],
                                                            PS[:, r % 2, j * P:(j + 1) * P], cf[:, ds(q * 4 + j, 1)],
                                                            MT[:, :], ALU.max, ALU.mult)
                        last.then_inc(s_pt, 1)

                    def recip(q, r):
                        dve.wait_ge(s_av, q + 1)
                        wait(dve, s_ex, q - 1)
                        dve.reciprocal(rec[:, r % 2, :].rearrange("p (k j) -> p k j", j=2),
                                       sums(r)[:, :, :, P]).then_inc(s_rc, 1)

                    def elu(q, r):
                        dve.wait_ge(s_ex, q + 1)
                        dve.scalar_tensor_tensor(pos[:, r % 2, :], ex[:, r % 2, :], 1.0, pos[:, r % 2, :],
                                                 ALU.min, ALU.add)
                        dve.drain()
                        xq = C["X"][:, ds(q * 4 * P, 4 * P)]
                        dve.scalar_tensor_tensor(xq, pos[:, r % 2, :], -1.0, xq, ALU.add, ALU.add)
                        dve.drain().then_inc(s_res, 1)
                        for j in range(4):
                            dve.bn_stats(C["ST"][:, ds((q * 4 + j) * 6, 6)], C["xs"](q * 4 + j))
                    pipelined(dve, NQ, 2, [(0, weights), (1, recip), (2, elu)])

                @block.scalar
                def _(act):
                    def parts(q, r):
                        act.wait_ge(s_rc, q + 1)
                        wait(act, s_res, q - 1)
                        for j in range(4):
                            h, o = sums(r)[:, j // 2, j % 2, 0:P], slice(j * P, (j + 1) * P)
                            act.activation(ex[:, r % 2, o], h, ACT.Exp, scale=rec[:, r % 2, j:j + 1])
                            act.activation(pos[:, r % 2, o], h, ACT.Relu, scale=rec[:, r % 2, j:j + 1])
                        act.drain().then_inc(s_ex, 1)

                    def hold(q, r):
                        act.wait_ge(s_res, q + 1)
                        wait(act, s_xt, q - 1)
                        act.copy(XB[:, r % 2, :, :].rearrange("p j d -> p (j d)"),
                                 C["X"][:, ds(q * 4 * P, 4 * P)]).then_inc(s_xb, 1)

                    def copy_x(q, r):
                        act.wait_ge(s_xt, q + 1)
                        wait(act, s_lg, q - 1)
                        act.copy(XT[:, r % 2, :], PS[:, 6, :]).then_inc(s_xc, 1)

                    def copy_l(q, r):
                        act.wait_ge(s_lg, q + 1)
                        act.copy(M["LG"][:, ds(q * 4 * E8, 4 * E8)], PS[:, 7, 0:4 * E8]).then_inc(s_lc, 1)
                    pipelined(act, NQ, 2, [(0, parts), (2, hold), (3, copy_x), (4, copy_l)])


def moe(C, out):
    nc, io, B, sem, tile, PS = C["nc"], C["io"], C["B"], C["sem"], C["tile"], C["PS"]
    IDF = C["IDF"]
    NTG = B // 4
    with ExitStack() as ctx:
        gates = tile(ctx, "d_gates", [P, B * E8])
        M = C["M"]
        wh, wl, w2h, w2l, r8, LG = (M[k] for k in ("wh", "wl", "w2h", "w2l", "r8", "LG"))

        with ExitStack() as c2:
            mm = tile(c2, "d_mm", [P, B])
            m1 = tile(c2, "d_m1", [P, B])
            m2 = tile(c2, "d_m2", [P, B])
            oh = tile(c2, "d_oh", [P, 2, B * E8])
            sc = tile(c2, "d_sc", [P, B * E8])
            ones = tile(c2, "d_ones", [P, P])
            cs = tile(c2, "d_cs", [P, E8])
            s_on, s_cs, s_var, s_std, s_e0, s_e1 = (sem("d_" + x) for x in ("on", "cs", "var", "std", "e0", "e1"))

            with nc.Block() as block:
                @block.vector
                def _(dve):
                    def by(a):
                        return a[:, :].unsqueeze(2).broadcast_to([P, B, E8])

                    def v(a):
                        return a.rearrange("p (b e) -> p b e", e=E8)
                    L, S = v(LG[:, :]), v(sc[:, :])
                    r8b = r8[:, :].unsqueeze(1).broadcast_to([P, B, E8])
                    dve.memset(ones[:, :], 1.0).then_inc(s_on, 1)
                    ln_vector(C, dve, s_var, s_std)
                    dve.wait_ge(s_cs, 1)
                    dve.tensor_copy(cs[:, :], PS[:, 0, 0:E8])
                    dve.drain()
                    dve.tensor_tensor(S, by(C["MU"]), cs[:, :].unsqueeze(1).broadcast_to([P, B, E8]), ALU.mult)
                    dve.drain()
                    dve.tensor_tensor(L, L, S, ALU.subtract)
                    dve.drain()
                    dve.tensor_tensor(L, L, by(C["RS"]), ALU.mult)
                    dve.drain()
                    dve.tensor_reduce(mm[:, :], L, AX.X, ALU.max)
                    dve.drain()
                    dve.tensor_tensor(L, L, by(mm), ALU.subtract)
                    dve.drain().then_inc(s_e0, 1)
                    dve.wait_ge(s_e1, 1)
                    dve.tensor_reduce(mm[:, :], L, AX.X, ALU.add)
                    dve.drain()
                    dve.reciprocal(mm[:, :], mm[:, :])
                    dve.drain()
                    dve.tensor_tensor(L, L, by(mm), ALU.mult)
                    dve.drain()
                    for k, m in enumerate((m1, m2)):
                        o = v(oh[:, k, :])
                        dve.tensor_reduce(m[:, :], L, AX.X, ALU.max)
                        dve.drain()
                        dve.tensor_tensor(S, L, by(m), ALU.is_equal)
                        dve.drain()
                        dve.tensor_tensor(S, S, r8b, ALU.mult)
                        dve.drain()
                        dve.tensor_reduce(mm[:, :], S, AX.X, ALU.max)
                        dve.drain()
                        dve.tensor_tensor(o, S, by(mm), ALU.is_equal)
                        dve.drain()
                        if k == 0:
                            dve.scalar_tensor_tensor(LG[:, :], oh[:, 0, :], -2.0, LG[:, :], ALU.mult, ALU.add)
                            dve.drain()
                    dve.scalar_tensor_tensor(mm[:, :], m1[:, :], 1e-9, m2[:, :], ALU.add, ALU.add)
                    dve.drain()
                    dve.reciprocal(mm[:, :], mm[:, :])
                    dve.drain()
                    for k, m in enumerate((m1, m2)):
                        dve.tensor_tensor(m[:, :], m[:, :], mm[:, :], ALU.mult)
                        dve.drain()
                        dve.tensor_tensor(v(oh[:, k, :]), v(oh[:, k, :]), by(m), ALU.mult)
                    dve.drain()
                    dve.tensor_tensor(gates[:, :], oh[:, 0, :], oh[:, 1, :], ALU.add)

                @block.tensor
                def _(pe):
                    pe.wait_ge(s_on, 1)
                    pe.matmul(PS[:, 0, 0:E8], ones[:, :], M["rw"][:, :], start=True, stop=True).then_inc(s_cs, 1)

                @block.scalar
                def _(act):
                    ln_scalar(C, act, s_var, s_std)
                    act.wait_ge(s_e0, 1)
                    act.activation(LG[:, :], LG[:, :], ACT.Exp).then_inc(s_e1, 1)

        xn = tile(ctx, "d_xn2", [P, 4, P])
        xh = tile(ctx, "d_xh", [P, 2, 512], BF16)
        xl = tile(ctx, "d_xl", [P, 2, 512], BF16)
        sg = tile(ctx, "d_sg", [P, 2, 512])
        hf = tile(ctx, "d_hf", [P, 3, 512])
        hh = tile(ctx, "d_hh", [P, 2, 3, 512], BF16)
        hl = tile(ctx, "d_hl", [P, 2, 3, 512], BF16)
        s_xn, s_tr, s_xh, s_xl, s_up, s_sg, s_hf, s_hh, s_hl, s_y, s_acc, s_out = (
            sem("d2_" + x) for x in "xn tr xh xl up sg hf hh hl y acc out".split())
        NU = E8 * 3

        def groups(eng, body):
            body(0, NTG == 1)
            if NTG > 2:
                with eng.Fori(1, NTG - 1) as g:
                    body(g, False)
            if NTG > 1:
                body(NTG - 1, True)

        with nc.Block() as block:
            @block.tensor
            def _(pe):
                def prep(g):
                    pe.wait_ge(s_xn, g * 4 + 4)
                    wait(pe, s_xl, g)
                    for j in range(4):
                        last = pe.transpose(PS[:, 7, j * P:(j + 1) * P], xn[:, j, :], IDF[:, :])
                    last.then_inc(s_tr, 1)

                def up(g, e, gp):
                    for k in range(3):
                        i = e * 3 + k
                        w = HCH[k]
                        cols = slice(e * HID + 128 * k, e * HID + 128 * k + w)
                        wait(pe, s_hf, g * NU + i - 2)
                        if i == 0:
                            pe.wait_ge(s_xl, g + 1)
                        for m in range(2):
                            o = PS[0:w, 2 * k + m, :]
                            pe.matmul(o, wh[:, m, cols], gp(xh), start=True, stop=False)
                            pe.matmul(o, wh[:, m, cols], gp(xl), start=False, stop=False)
                            last = pe.matmul(o, wl[:, m, cols], gp(xh), start=False, stop=True)
                        last.then_inc(s_up, 1)

                def down(n, e):
                    pe.wait_ge(s_hl, n * 3 + 3)
                    pe.wait_ge(s_hh, n * 3 + 3)
                    wait(pe, s_acc, n)
                    for t in range(4):
                        o = PS[:, 6, t * P:(t + 1) * P]
                        q = slice(t * P, (t + 1) * P)
                        for k in range(3):
                            w = HCH[k]
                            wc = slice((e * 3 + k) * P, (e * 3 + k + 1) * P)
                            pe.matmul(o, hh[0:w, e % 2, k, q], w2h[0:w, wc], start=(k == 0), stop=False)
                            pe.matmul(o, hh[0:w, e % 2, k, q], w2l[0:w, wc], start=False, stop=False)
                            last = pe.matmul(o, hl[0:w, e % 2, k, q], w2h[0:w, wc], start=False, stop=(k == 2))
                    last.then_inc(s_y, 1)

                def body(g, end):
                    def gp(a):
                        return a[:, :, :].rearrange("p a n -> p (a n)")[:, ds((g % 2) * 512, 512)]
                    for e in range(E8):
                        up(g, e, gp)
                        if e > 0 or not (isinstance(g, int) and g == 0):
                            down(g * E8 + (e - 1), (e - 1) % E8)
                        if e == 4 and not end:
                            prep(g + 1)
                    if end:
                        down(g * E8 + E8 - 1, E8 - 1)
                prep(0)
                groups(pe, body)

            @block.vector
            def _(dve):
                def prep(g):
                    wait(dve, s_tr, g)
                    for j in range(4):
                        normalise(C, dve, xn[:, j, :], g * 4 + j).then_inc(s_xn, 1)

                def split(g):
                    dve.wait_ge(s_tr, g + 1)
                    wait(dve, s_up, (g - 1) * NU)
                    def gp(a):
                        return a[:, :, :].rearrange("p a n -> p (a n)")[:, ds((g % 2) * 512, 512)]
                    dve.tensor_copy(gp(xh), PS[:, 7, :])
                    dve.drain()
                    dve.tensor_tensor(gp(xl), PS[:, 7, :], gp(xh), ALU.subtract).then_inc(s_xl, 1)

                def hidden(g, i):
                    w = HCH[i % 3]
                    n = g * NU + i
                    dve.wait_ge(s_sg, n + 1)
                    wait(dve, s_hh, n - 2)
                    wait(dve, s_hl, n - 2)
                    dve.tensor_tensor(hf[0:w, i % 3, :], sg[0:w, i % 2, :], PS[0:w, 2 * (i % 3) + 1, :],
                                      ALU.mult).then_inc(s_hf, 1)

                def add(g, n, e):
                    dve.wait_ge(s_y, n + 1)
                    for t in range(4):
                        b = g * 4 + t
                        last = dve.scalar_tensor_tensor(C["xs"](b), PS[:, 6, t * P:(t + 1) * P],
                                                        gates[:, ds(b * E8 + e, 1)], C["xs"](b), ALU.mult, ALU.add)
                    dve.drain().then_inc(s_acc, 1)

                def body(g, end):
                    first = isinstance(g, int) and g == 0
                    for e in range(E8):
                        for k in range(3):
                            i = e * 3 + k
                            hidden(g, i)
                        if e > 0:
                            add(g, g * E8 + (e - 1), e - 1)
                        elif not first:
                            add(g - 1, g * E8 - 1, E8 - 1)
                        if e == 2 and not end:
                            prep(g + 1)
                        if e == 6 and not end:
                            split(g + 1)
                    if end:
                        add(g, g * E8 + 7, 7)
                prep(0)
                split(0)
                groups(dve, body)

            @block.gpsimd
            def _(pool):
                def low(g, i):
                    w = HCH[i % 3]
                    e = i // 3
                    n = g * NU + i
                    pool.wait_ge(s_hh, n + 1)
                    if i % 3 == 0:
                        wait(pool, s_y, g * E8 + (e - 1))
                    pool.tensor_tensor(hl[0:w, e % 2, i % 3, :], hf[0:w, i % 3, :], hh[0:w, e % 2, i % 3, :],
                                      ALU.subtract).then_inc(s_hl, 1)

                def body(g, end):
                    for i in range(NU):
                        low(g, i)
                groups(pool, body)

            @block.scalar
            def _(act):
                def silu(g, i):
                    w = HCH[i % 3]
                    n = g * NU + i
                    act.wait_ge(s_up, n + 1)
                    wait(act, s_hf, n - 1)
                    act.activation(sg[0:w, i % 2, :], PS[0:w, 2 * (i % 3), :], ACT.Silu).then_inc(s_sg, 1)

                def high(g, i):
                    w = HCH[i % 3]
                    e = i // 3
                    n = g * NU + i
                    act.wait_ge(s_hf, n + 1)
                    if i % 3 == 0:
                        wait(act, s_y, g * E8 + (e - 1))
                    act.copy(hh[0:w, e % 2, i % 3, :], hf[0:w, i % 3, :]).then_inc(s_hh, 1)

                def body(g, end):
                    first = isinstance(g, int) and g == 0
                    for i in range(NU):
                        silu(g, i)
                        if i > 0:
                            high(g, i - 1)
                        elif not first:
                            high(g - 1, NU - 1)
                    if end:
                        high(g, NU - 1)
                groups(act, body)

            @block.sync
            def _(sp):
                o = out.rearrange("b p d -> p b d")

                def body(g, end):
                    wait(sp, s_acc, g * E8 + E8)
                    sp.dma_start(o[:, ds(g * 4, 4), :], C["X3"][:, ds(g * 4, 4), :]).then_inc(s_out, 16)
                groups(sp, body)
                sp.wait_ge(s_out, 16 * NTG)


def host_inputs(a):
    import numpy as np
    c = np.ascontiguousarray

    def bits(ones):
        return c((ones != 0).astype(np.uint16) * np.uint16(0x3F80))
    sel = np.zeros((128, 32, 128), np.float32)
    for r in range(32):
        for t in range(3):
            sel[32 * t + r, r, :] = 1.0
    io = {
        "x": c(a["x"]), "adj": c(a["adj"]),
        "gW": c(np.transpose(a["L0_gnn_W"], (1, 0, 2)).reshape(128, 128)),
        "g_as": c(a["L0_gnn_a_src"].reshape(128)), "g_ad": c(a["L0_gnn_a_dst"].reshape(128)),
        "beta": c(a["L0_gnn_beta_tilde"].reshape(1)), "gWoT": c(a["L0_gnn_W_out"].T),
        "c_id": np.eye(128, dtype=np.float32), "c_idb": bits(np.eye(128)),
        "c_sel": bits(sel.reshape(128, 32 * 128)),
    }
    hw, ho, ow = a["L0_ffn_hy_in_w"], a["L0_ffn_hy_out_w"], a["L0_ffn_out_w"]

    def chunked(wT):
        return c(wT.reshape(-1, 128, wT.shape[1]).transpose(1, 0, 2).reshape(128, -1))

    def conv(w):
        return c(w.reshape(5, 128, -1).transpose(1, 0, 2).reshape(128, -1))
    m = np.arange(64)
    bfm = np.zeros((2, 8, 4, 4, 2, 64), np.float32)
    rm = np.zeros((8, 4, 8), np.float32)
    for h2 in range(2):
        for ch in range(4):
            bfm[h2, :, ch, ch, h2, :] = 1.0
    for b in range(8):
        rm[b, :, b] = 1.0
    lt = np.tile((m[:, None] < m[None, :]).astype(np.float32), (2, 1))
    ut = np.tile((m[:, None] > m[None, :]).astype(np.float32), (2, 1))
    io.update({
        "bWxR": c(a["L0_ffn_W_x"].reshape(8, 64, 128).transpose(1, 0, 2).reshape(64, 1024)),
        "bWsT": c(a["L0_ffn_W_slice"].T), "bbx": c(a["L0_ffn_b_x"].reshape(8, 64).T),
        "btemp": c(a["L0_ffn_temperature"].reshape(8)), "bbs": c(a["L0_ffn_b_slice"].reshape(1, 64)),
        "bob": c(a["L0_ffn_out_b"].reshape(1, 128)), "bWin": chunked(hw.T), "bWho": chunked(ho.T),
        "bWfx": c(a["L0_ffn_W_fx"].T), "bWo2": chunked(ow.T), "bfc": chunked(a["L0_ffn_hy_fcD_w"].T),
        "c_bfm": bits(bfm.reshape(64, 512)), "c_rm": rm.reshape(32, 8),
        "c_selh": bits(np.repeat(np.eye(8), 64, axis=1)),
        "c_lt": lt, "c_ut": ut, "c_uf": np.kron(np.eye(2, dtype=np.float32), ut[:64]),
        "c_ub": np.kron(np.eye(2, dtype=np.float32), lt[:64]),
        "bnw": c(a["L0_ffn_hy_norm_w"].reshape(4, 128).T), "bbfx": c(a["L0_ffn_b_fx"]),
        "bdtb": c(a["L0_ffn_hy_dt_bias"]), "bAl": c(a["L0_ffn_hy_A_log"]), "bD": c(a["L0_ffn_hy_D"]),
        "bcw": conv(a["L0_ffn_hy_conv_w"]), "bcb": conv(a["L0_ffn_hy_conv_b"].reshape(640, 1)),
    })
    io.update({"cW": c(a["L1_gnn_W"]), "ca": c(a["L1_gnn_a"].reshape(256))})
    w2 = np.zeros((8, 384, 128), np.float32)
    w2[:, 0:341] = a["L1_ffn_w2"].transpose(0, 2, 1)
    io.update({
        "drw": c(a["L1_ffn_router_w"].T), "c_r8": np.arange(8, 0, -1).astype(np.float32),
        "dw1": c(a["L1_ffn_w1"].reshape(2728, 128).T), "dw3": c(a["L1_ffn_w3"].reshape(2728, 128).T),
        "dw2": c(w2.reshape(8, 3, 128, 128).transpose(2, 0, 1, 3).reshape(128, 3072)),
    })
    return io


def kernel(**inputs):
    import numpy as _np
    import concourse.bacc as _bacc
    from concourse import mybir as _mybir
    from concourse.bass_utils import run_bass_kernel_spmd as _run

    nc = _bacc.Bacc("TRN2", target_bir_lowering=False, num_devices=1)
    arrays = {f"in_{k}": v for k, v in host_inputs({k: _np.asarray(v) for k, v in inputs.items()}).items()}
    io = {k[3:]: nc.dram_tensor(k, v.shape, _mybir.dt.from_np(v.dtype), kind="ExternalInput").ap()
          for k, v in arrays.items()}
    out = nc.dram_tensor("out_x", inputs["x"].shape, _mybir.dt.float32, kind="ExternalOutput").ap()
    build(nc, io, out)
    r = _run(nc, [arrays], core_ids=[0])
    return r.results[0]["out_x"]
```
